# Optimizing a Trainium2 kernel written in Bass

```python
import numpy as np
import jax
import jax.numpy as jnp

def _softmax(x, axis=-1):
    return jax.nn.softmax(x, axis=axis)

def _gelu(x):
    return jax.nn.gelu(x, approximate=True)

def _silu(x):
    return jax.nn.silu(x)

def _sigmoid(x):
    return jax.nn.sigmoid(x)

def _layernorm(x, axis=-1, eps=1e-05):
    m = jnp.mean(x, axis=axis, keepdims=True)
    v = jnp.var(x, axis=axis, keepdims=True)
    return (x - m) / jnp.sqrt(v + eps)

def _scatter_add(tgt, idx, src, axis=0):
    return tgt.at[idx].add(src)

def _segment_sum(src, seg, n):
    return jax.ops.segment_sum(src, seg, n)
kernel_name = 'mk_decoder_postln_d1_seqx_r4_4b5d56'

def setup_inputs(seed: int=0):
    np.random.seed(seed)
    _w = jnp.asarray

    def _rec_inputs():
        import jax
        import jax.numpy as jnp
        _rk = jax.random.key(seed)
        x = 7.22e-05 + 1 * jax.random.normal(jax.random.fold_in(_rk, 1), (4, 1024, 256), jnp.float32)
        _lenS = 1024 - jax.random.randint(jax.random.fold_in(_rk, 7), (4,), 0, max(1, 1024 // 4) + 1, jnp.int32)
        _lenS2 = 154 - jax.random.randint(jax.random.fold_in(_rk, 8), (4,), 0, max(1, 154 // 4) + 1, jnp.int32)
        _ctx_1024P = jax.random.normal(jax.random.fold_in(_rk, 11), (4, 16, 256), jnp.float32)
        _ctx_1024c = jax.random.dirichlet(jax.random.fold_in(_rk, 511), 0.3 * jnp.ones((16,), jnp.float32), (4, 154))
        _ctx_1024t = jnp.einsum('bsk,bkd->bsd', _ctx_1024c, _ctx_1024P)
        _ctx_1024t = _ctx_1024t * jax.lax.rsqrt(jnp.mean(jnp.square(_ctx_1024t)) + 1e-12) * 0.953939
        ctx_1024 = 0.000227908 + 0.99994 * (_ctx_1024t + 0.3 * jax.random.normal(jax.random.fold_in(_rk, 611), (4, 154, 256), jnp.float32))
        return (x, ctx_1024)
    x, ctx_1024 = _rec_inputs()

    def _L0_attn_setup():
        import jax, jax.numpy as jnp
        import numpy as np
        import math
        N_HEAD = 16
        EPS = 1e-06

        def _phi(x, omega):
            m = omega.shape[1]
            proj = jnp.einsum('bhtd,dm->bhtm', x, omega)
            norm_sq_half = 0.5 * jnp.sum(x * x, axis=-1, keepdims=True)
            return jnp.exp(proj - norm_sq_half) / math.sqrt(m)
        key = jax.random.key(seed)
        ks = jax.random.split(key, 4)
        B, T, C = (2, 256, 256)
        d_h, m = (C // N_HEAD, 128)
        x = jax.random.normal(ks[0], (B, T, C), dtype=jnp.float32)
        W_attn = jax.random.normal(ks[1], (C, 3 * C), dtype=jnp.float32) * (1.0 / math.sqrt(C))
        b_attn = jnp.zeros((3 * C,), dtype=jnp.float32)
        W_proj = jax.random.normal(ks[2], (C, C), dtype=jnp.float32) * (1.0 / math.sqrt(C))
        b_proj = jnp.zeros((C,), dtype=jnp.float32)
        omega = jax.random.normal(ks[3], (d_h, m), dtype=jnp.float32)
        return {'x': x, 'W_attn': W_attn, 'b_attn': b_attn, 'W_proj': W_proj, 'b_proj': b_proj, 'omega': omega}
    _L0_attn_all = _L0_attn_setup()
    _L0_attn_in = {k: v for k, v in _L0_attn_all.items() if k in ('W_attn', 'b_attn', 'W_proj', 'b_proj', 'omega')}
    del _L0_attn_all

    def _L0_xattn_setup():
        import jax, jax.numpy as jnp
        import numpy as np
        EMBED_DIM = 256
        N_HEAD = 16
        HEAD_DIM = EMBED_DIM // N_HEAD
        key = jax.random.key(seed)
        k1, k2, k3, k4, k5, k6 = jax.random.split(key, 6)
        B, T, MEM = (4, 512, 64)
        x = jax.random.normal(k1, (B, T, EMBED_DIM), dtype=jnp.float32)
        ext_mem = jax.random.normal(k2, (B, MEM, EMBED_DIM), dtype=jnp.float32)
        W_attn = jax.random.normal(k3, (EMBED_DIM, 3 * EMBED_DIM), dtype=jnp.float32) / np.sqrt(EMBED_DIM)
        b_attn = jax.random.normal(k4, (3 * EMBED_DIM,), dtype=jnp.float32) * 0.02
        W_proj = jax.random.normal(k5, (EMBED_DIM, EMBED_DIM), dtype=jnp.float32) / np.sqrt(EMBED_DIM)
        b_proj = jax.random.normal(k6, (EMBED_DIM,), dtype=jnp.float32) * 0.02
        return {'x': x, 'ext_mem': ext_mem, 'W_attn': W_attn, 'b_attn': b_attn, 'W_proj': W_proj, 'b_proj': b_proj}
    _L0_xattn_all = _L0_xattn_setup()
    _L0_xattn_in = {k: v for k, v in _L0_xattn_all.items() if k in ('W_attn', 'b_attn', 'W_proj', 'b_proj')}
    del _L0_xattn_all

    def _L0_ffn_setup():
        import jax, jax.numpy as jnp
        import numpy as np
        B, S, H = (1, 512, 256)
        E, K = (16, 4)
        G, TG = (4, 2)
        I_MOE = 128
        N_SH = 2
        SCALE = 2.5

        def _mlp(x, gw, uw, dw):
            return jax.nn.silu(x @ gw.T) * (x @ uw.T) @ dw.T

        def _route(x2d, router_weight, e_bias):
            T = x2d.shape[0]
            scores = jax.nn.sigmoid(x2d @ router_weight.T)
            sc = scores + e_bias[None, :]
            group_scores = jnp.sum(jax.lax.top_k(sc.reshape(T, G, E // G), 2)[0], axis=-1)
            _, gidx = jax.lax.top_k(group_scores, TG)
            gmask = jnp.zeros((T, G), sc.dtype).at[jnp.arange(T)[:, None], gidx].set(1.0)
            smask = jnp.repeat(gmask, E // G, axis=1)
            masked = jnp.where(smask > 0, sc, 0.0)
            _, tidx = jax.lax.top_k(masked, K)
            tw = jnp.take_along_axis(scores, tidx, axis=1)
            tw = tw / (jnp.sum(tw, axis=-1, keepdims=True) + 1e-20)
            tw = tw * SCALE
            return (tidx, tw)

        def _moe_forward(hidden_states, router_weight, e_bias, gate_w, up_w, down_w, sh_gate_w, sh_up_w, sh_down_w):
            orig_shape = hidden_states.shape
            x = hidden_states.reshape(-1, H)
            T = x.shape[0]
            tidx, tw = _route(x, router_weight, e_bias)
            g = jnp.einsum('th,eih->tei', x, gate_w)
            u = jnp.einsum('th,eih->tei', x, up_w)
            h = jax.nn.silu(g) * u
            yo = jnp.einsum('tei,ehi->teh', h, down_w)
            combine = jnp.zeros((T, E), tw.dtype).at[jnp.arange(T)[:, None], tidx].add(tw)
            routed = jnp.einsum('te,teh->th', combine, yo)
            shared = _mlp(hidden_states.reshape(-1, H), sh_gate_w, sh_up_w, sh_down_w)
            return (routed + shared).reshape(orig_shape)
        key = jax.random.key(seed)
        ks = jax.random.split(key, 9)
        s = 0.02
        return {'hidden_states': jax.random.normal(ks[0], (B, S, H), jnp.float32), 'router_weight': jax.random.normal(ks[1], (E, H), jnp.float32) * s, 'e_bias': jnp.zeros((E,), jnp.float32), 'gate_w': jax.random.normal(ks[2], (E, I_MOE, H), jnp.float32) * s, 'up_w': jax.random.normal(ks[3], (E, I_MOE, H), jnp.float32) * s, 'down_w': jax.random.normal(ks[4], (E, H, I_MOE), jnp.float32) * s, 'sh_gate_w': jax.random.normal(ks[5], (N_SH * I_MOE, H), jnp.float32) * s, 'sh_up_w': jax.random.normal(ks[6], (N_SH * I_MOE, H), jnp.float32) * s, 'sh_down_w': jax.random.normal(ks[7], (H, N_SH * I_MOE), jnp.float32) * s}
    _L0_ffn_all = _L0_ffn_setup()
    _L0_ffn_in = {k: v for k, v in _L0_ffn_all.items() if k in ('router_weight', 'e_bias', 'gate_w', 'up_w', 'down_w', 'sh_gate_w', 'sh_up_w', 'sh_down_w')}
    del _L0_ffn_all
    return {'x': x, 'ctx_1024': ctx_1024, 'L0_attn_W_attn': _L0_attn_in['W_attn'], 'L0_attn_b_attn': _L0_attn_in['b_attn'], 'L0_attn_W_proj': _L0_attn_in['W_proj'], 'L0_attn_b_proj': _L0_attn_in['b_proj'], 'L0_attn_omega': _L0_attn_in['omega'], 'L0_xattn_W_attn': _L0_xattn_in['W_attn'], 'L0_xattn_b_attn': _L0_xattn_in['b_attn'], 'L0_xattn_W_proj': _L0_xattn_in['W_proj'], 'L0_xattn_b_proj': _L0_xattn_in['b_proj'], 'L0_ffn_router_weight': _L0_ffn_in['router_weight'], 'L0_ffn_e_bias': _L0_ffn_in['e_bias'], 'L0_ffn_gate_w': _L0_ffn_in['gate_w'], 'L0_ffn_up_w': _L0_ffn_in['up_w'], 'L0_ffn_down_w': _L0_ffn_in['down_w'], 'L0_ffn_sh_gate_w': _L0_ffn_in['sh_gate_w'], 'L0_ffn_sh_up_w': _L0_ffn_in['sh_up_w'], 'L0_ffn_sh_down_w': _L0_ffn_in['sh_down_w']}

def reference(x, ctx_1024, L0_attn_W_attn, L0_attn_b_attn, L0_attn_W_proj, L0_attn_b_proj, L0_attn_omega, L0_xattn_W_attn, L0_xattn_b_attn, L0_xattn_W_proj, L0_xattn_b_proj, L0_ffn_router_weight, L0_ffn_e_bias, L0_ffn_gate_w, L0_ffn_up_w, L0_ffn_down_w, L0_ffn_sh_gate_w, L0_ffn_sh_up_w, L0_ffn_sh_down_w):
    import jax
    import jax.numpy as jnp

    def _L0_attn_ref(x, W_attn, b_attn, W_proj, b_proj, omega):
        import jax, jax.numpy as jnp
        import numpy as np
        import math
        N_HEAD = 16
        EPS = 1e-06

        def _phi(x, omega):
            m = omega.shape[1]
            proj = jnp.einsum('bhtd,dm->bhtm', x, omega)
            norm_sq_half = 0.5 * jnp.sum(x * x, axis=-1, keepdims=True)
            return jnp.exp(proj - norm_sq_half) / math.sqrt(m)
        B, T, C = x.shape
        nh = N_HEAD
        d_h = C // nh
        qkv = x @ W_attn + b_attn
        q, k, v = jnp.split(qkv, 3, axis=-1)
        q = q.reshape(B, T, nh, d_h).transpose(0, 2, 1, 3)
        k = k.reshape(B, T, nh, d_h).transpose(0, 2, 1, 3)
        v = v.reshape(B, T, nh, d_h).transpose(0, 2, 1, 3)
        scale = 1.0 / math.sqrt(d_h)
        q = q * scale
        k = k * scale
        phi_q = _phi(q, omega)
        phi_k = _phi(k, omega)
        kv = phi_k[..., :, None] * v[..., None, :]
        S = jnp.cumsum(kv, axis=2)
        Z = jnp.cumsum(phi_k, axis=2)
        num = jnp.einsum('bhtm,bhtmd->bhtd', phi_q, S)
        den = jnp.einsum('bhtm,bhtm->bht', phi_q, Z)[..., None] + EPS
        y = num / den
        y = y.transpose(0, 2, 1, 3).reshape(B, T, C)
        return y @ W_proj + b_proj

    def _L0_xattn_ref(x, ext_mem, W_attn, b_attn, W_proj, b_proj):
        import jax, jax.numpy as jnp
        import numpy as np
        EMBED_DIM = 256
        N_HEAD = 16
        HEAD_DIM = EMBED_DIM // N_HEAD
        B, T, C = x.shape
        qkv = x @ W_attn + b_attn
        q, k, v = jnp.split(qkv, 3, axis=2)
        to_heads = lambda t: t.reshape(B, -1, N_HEAD, HEAD_DIM).transpose(0, 2, 1, 3)
        q, k, v = (to_heads(q), to_heads(k), to_heads(v))
        mem_k = to_heads(ext_mem)
        k = jnp.concatenate([mem_k, k], axis=2)
        v = jnp.concatenate([mem_k, v], axis=2)
        mem_len = k.shape[2] - T
        att = jnp.einsum('bhtd,bhsd->bhts', q, k) * (1.0 / np.sqrt(HEAD_DIM))
        causal = jnp.tril(jnp.ones((T, T), dtype=bool))
        full_mask = jnp.concatenate([jnp.ones((T, mem_len), dtype=bool), causal], axis=1)
        att = jnp.where(full_mask[None, None], att, -jnp.inf)
        att = jax.nn.softmax(att, axis=-1)
        y = jnp.einsum('bhts,bhsd->bhtd', att, v)
        y = y.transpose(0, 2, 1, 3).reshape(B, T, C)
        return y @ W_proj + b_proj

    def _L0_ffn_ref(hidden_states, router_weight, e_bias, gate_w, up_w, down_w, sh_gate_w, sh_up_w, sh_down_w):
        import jax, jax.numpy as jnp
        import numpy as np
        B, S, H = (1, 512, 256)
        E, K = (16, 4)
        G, TG = (4, 2)
        I_MOE = 128
        N_SH = 2
        SCALE = 2.5

        def _mlp(x, gw, uw, dw):
            return jax.nn.silu(x @ gw.T) * (x @ uw.T) @ dw.T

        def _route(x2d, router_weight, e_bias):
            T = x2d.shape[0]
            scores = jax.nn.sigmoid(x2d @ router_weight.T)
            sc = scores + e_bias[None, :]
            group_scores = jnp.sum(jax.lax.top_k(sc.reshape(T, G, E // G), 2)[0], axis=-1)
            _, gidx = jax.lax.top_k(group_scores, TG)
            gmask = jnp.zeros((T, G), sc.dtype).at[jnp.arange(T)[:, None], gidx].set(1.0)
            smask = jnp.repeat(gmask, E // G, axis=1)
            masked = jnp.where(smask > 0, sc, 0.0)
            _, tidx = jax.lax.top_k(masked, K)
            tw = jnp.take_along_axis(scores, tidx, axis=1)
            tw = tw / (jnp.sum(tw, axis=-1, keepdims=True) + 1e-20)
            tw = tw * SCALE
            return (tidx, tw)

        def _moe_forward(hidden_states, router_weight, e_bias, gate_w, up_w, down_w, sh_gate_w, sh_up_w, sh_down_w):
            orig_shape = hidden_states.shape
            x = hidden_states.reshape(-1, H)
            T = x.shape[0]
            tidx, tw = _route(x, router_weight, e_bias)
            g = jnp.einsum('th,eih->tei', x, gate_w)
            u = jnp.einsum('th,eih->tei', x, up_w)
            h = jax.nn.silu(g) * u
            yo = jnp.einsum('tei,ehi->teh', h, down_w)
            combine = jnp.zeros((T, E), tw.dtype).at[jnp.arange(T)[:, None], tidx].add(tw)
            routed = jnp.einsum('te,teh->th', combine, yo)
            shared = _mlp(hidden_states.reshape(-1, H), sh_gate_w, sh_up_w, sh_down_w)
            return (routed + shared).reshape(orig_shape)
        return _moe_forward(hidden_states, router_weight, e_bias, gate_w, up_w, down_w, sh_gate_w, sh_up_w, sh_down_w)
    x = _layernorm(x + _L0_attn_ref(x, L0_attn_W_attn, L0_attn_b_attn, L0_attn_W_proj, L0_attn_b_proj, L0_attn_omega), axis=-1)
    x = _layernorm(x + _L0_xattn_ref(x, ctx_1024, L0_xattn_W_attn, L0_xattn_b_attn, L0_xattn_W_proj, L0_xattn_b_proj), axis=-1)
    x = _layernorm(x + _L0_ffn_ref(x, L0_ffn_router_weight, L0_ffn_e_bias, L0_ffn_gate_w, L0_ffn_up_w, L0_ffn_down_w, L0_ffn_sh_gate_w, L0_ffn_sh_up_w, L0_ffn_sh_down_w), axis=-1)
    return x

_drawn_inputs = setup_inputs


def setup_inputs(seed=0):
    import zlib

    import numpy as np

    out = dict(_drawn_inputs(seed))
    spreads = {'L0_attn_b_attn': (0.0, 0.1), 'L0_attn_b_proj': (0.0, 0.1), 'L0_ffn_e_bias': (0.0, 0.489)}
    factors = {'L0_attn_omega': 2.992,
     'L0_xattn_b_attn': 3.822,
     'L0_xattn_b_proj': 2.794,
     'L0_ffn_router_weight': 8.0,
     'L0_ffn_gate_w': 3.823,
     'L0_ffn_up_w': 3.754,
     'L0_ffn_down_w': 3.775,
     'L0_ffn_sh_gate_w': 3.394,
     'L0_ffn_sh_up_w': 3.361,
     'L0_ffn_sh_down_w': 3.374}
    for name, (base, spread) in spreads.items():
        noise = np.random.default_rng([zlib.crc32(name.encode()), seed]).standard_normal(out[name].shape)
        drawn = base * np.exp(spread * noise) if base else spread * noise
        out[name] = jnp.asarray(drawn.astype(out[name].dtype))
    for name, factor in factors.items():
        out[name] = (out[name] * factor).astype(out[name].dtype)
    return out
```

```python
from contextlib import ExitStack

import concourse.bass as bass
from concourse import mybir

F32 = mybir.dt.float32
BF16 = mybir.dt.bfloat16
ALU = mybir.AluOpType
ACT = mybir.ActivationFunctionType
AX = mybir.AxisListType

B, T, C = 4, 1024, 256
HEADS, HD = 16, 16
FEAT = 128
MEM = 154
EXPERTS, SHARED, INNER = 16, 2, 128
ALL_EXPERTS = EXPERTS + SHARED
TOPK, GROUPS, TOP_GROUPS, ROUTE_SCALE = 4, 4, 2, 2.5
LN_EPS = 1e-5
DEN_EPS = 1e-6
P = 128
TILE = 512
HALVES = T // TILE
CT = C // P
TB = TILE // P
QUADS = HEADS // 4
NQ = B * QUADS
BLOCKS = T // P
V1 = HD + 1
VW = 4 * V1
PARTS = 3
LEFT = (0, 0, 0, 1, 1, 2)
RIGHT = (0, 1, 2, 0, 1, 0)
STACK = len(LEFT) * HD
STACK1 = STACK + PARTS
START = 1
BIG = 3.0e38
MEMR = MEM - P
MEMW = P + 32


class Phase:

    def __init__(self, nc, name):
        self.nc, self.name, self.ctx, self.held = nc, name, ExitStack(), []
        self.chain = None

    def __enter__(self):
        return self

    def __exit__(self, *a):
        self.ctx.__exit__(*a)
        if a[0] is None:
            self.nc.clear_and_free_semaphores(self.held)
            self.nc.all_engine_barrier()

    def sb(self, name, shape, dt=F32):
        return self.ctx.enter_context(self.nc.sbuf_tensor(f"{self.name}_{name}", shape, dt))

    def ps(self, name, shape, dt=F32):
        return self.ctx.enter_context(self.nc.psum_tensor(f"{self.name}_{name}", shape, dt))

    def sem(self, name):
        self.held.append(self.nc.alloc_semaphore(f"{self.name}_{name}"))
        return self.held[-1]

    def chain_sem(self):
        self.held.append(self.nc.alloc_semaphore(f"{self.name}_chain"))
        self.chain = self.held[-1]
        return self.chain

    def start(self, eng):
        for sem in self.held:
            if sem is not self.chain:
                eng.sem_inc(sem, START)

    def sems(self, name, n):
        return [self.sem(f"{name}{i}") for i in range(n)]

    def block(self):
        return self.ctx.enter_context(self.nc.Block())


class Chain:

    def __init__(self, eng, sem):
        self.eng, self.sem, self.n = eng, sem, 0

    def restart(self):
        self.eng.sem_clear(self.sem)
        self.n = 0

    def link(self, ins):
        self.n += 1
        ins.then_inc(self.sem, 1)
        self.eng.wait_ge(self.sem, self.n)


def split_constants(nc, io):
    with Phase(nc, "sc") as ph:
        om = ph.sb("om", [HD, FEAT])
        om_rest = ph.sb("om_rest", [HD, FEAT])
        om_parts = ph.sb("om_parts", [HD, PARTS, FEAT], BF16)
        n_tiles = B * C // P
        mk = ph.sb("mk", [P, n_tiles, MEM])
        mk_rest = ph.sb("mk_rest", [P, n_tiles, MEM])
        mk_parts = ph.sb("mk_parts", [P, PARTS, n_tiles, MEM], BF16)
        loaded, split, stored, chain_sem = ph.sem("loaded"), ph.sem("split"), ph.sem("stored"), ph.chain_sem()
        blk = ph.block()

        @blk.sync
        def _(sp):
            ph.start(sp)
            sp.dma_start(om[:, :], io["omega"]).then_inc(loaded, 16)
            sp.dma_start(mk[:, :, :], io["memT"].rearrange("(a p) s -> p a s", p=P)).then_inc(loaded, 16)
            sp.wait_ge(split, 2 + START)
            sp.dma_start(io["omega_parts"], om_parts[:, :, :]).then_inc(stored, 16)
            for part in range(PARTS):
                sp.dma_start(io["mem_parts"][part].rearrange("(a p) s -> p a s", p=P),
                             mk_parts[:, part]).then_inc(stored, 16)
            sp.wait_ge(stored, 16 * (1 + PARTS) + START)

        @blk.vector
        def _(dve):
            chain = Chain(dve, chain_sem)
            dve.wait_ge(loaded, 32 + START)
            chain.link(nc.vector.tensor_scalar(om[:, :], om[:, :], HD ** -0.5, None, ALU.mult))
            for full, rest, parts in ((om[:, :], om_rest[:, :], [om_parts[:, i] for i in range(PARTS)]),
                                      (mk[:, :, :], mk_rest[:, :, :], [mk_parts[:, i] for i in range(PARTS)])):
                chain.link(nc.vector.tensor_copy(parts[0], full))
                chain.link(nc.vector.tensor_tensor(rest, full, parts[0], ALU.subtract))
                chain.link(nc.vector.tensor_copy(parts[1], rest))
                nc.vector.tensor_tensor(parts[2], rest, parts[1], ALU.subtract).then_inc(split, 1)


def project(nc, io, stage):
    xT, w_d, bT_d, bv_d = io[f"xT{stage}"], io[f"w{stage}"], io[f"bT{stage}"], io[f"bv{stage}"]
    q_parts, k_parts, v_out = io["q_parts"], io["k_parts"], io["v"]
    norms = stage == 1
    NS = 2 * CT
    with Phase(nc, f"pj{stage}") as ph:
        w = ph.sb("w", [P, CT, 3 * C])
        bias = ph.sb("bias", [P, 6])
        bias_v = ph.sb("bias_v", [P, C])
        x = ph.sb("x", [P, HALVES, CT, TILE])
        full = ph.sb("full", [P, 2, TILE])
        rest = ph.sb("rest", [P, 2, TILE])
        parts = ph.sb("parts", [P, NS, PARTS, TILE], BF16)
        v = ph.sb("v", [P, 2, TB, HEADS, V1])
        ps_qk = ph.ps("ps_qk", [P, 2, TILE])
        ps_v = ph.ps("ps_v", [P, TB, C])
        consts_in, chain_sem = ph.sem("consts_in"), ph.chain_sem()
        x_in = ph.sems("x_in", HALVES)
        qk_ps = ph.sem("qk_ps")
        v_ps = ph.sems("v_ps", HALVES)
        qk_full = ph.sems("qk_full", 2)
        qk_split = ph.sems("qk_split", 2)
        v_full = ph.sem("v_full")
        qk_out = ph.sems("qk_out", NS)
        v_out_sem = ph.sems("v_out", 2)
        if norms:
            squares = ph.sb("squares", [P, NS, TILE])
            select = ph.sb("select", [P, NS, 32])
            n_rest = ph.sb("n_rest", [32, TILE])
            n_parts = ph.sb("n_parts", [32, 2, PARTS, TILE], BF16)
            ps_n = ph.ps("ps_n", [32, TILE])
            squared, n_ps, n_split = ph.sem("squared"), ph.sem("n_ps"), ph.sem("n_split")
            n_out = ph.sems("n_out", 2)
        n_consts = 3 + norms
        blk = ph.block()

        @blk.sync
        def _(sp):
            ph.start(sp)
            sp.dma_start(w[:, :, :], w_d.rearrange("(a p) n -> p a n", p=P)).then_inc(consts_in, 16)
            sp.dma_start(bias[:, :], bT_d).then_inc(consts_in, 16)
            sp.dma_start(bias_v[:, :], bv_d).then_inc(consts_in, 16)
            if norms:
                sp.dma_start(select[:, :, :], io["select"]).then_inc(consts_in, 16)

            def load_x(b, half):
                sp.dma_start(x[:, half], xT[bass.ds(b * C, C), half * TILE:(half + 1) * TILE]
                             .rearrange("(a p) t -> p a t", p=P)).then_inc(x_in[half], 16)

            def batch_row(b, more):
                for half in range(HALVES):
                    cols = slice(half * TILE, (half + 1) * TILE)
                    for s in range(NS):
                        dst = q_parts if s < CT else k_parts
                        sp.wait_ge(qk_split[s % 2], b * (HALVES * NS // 2) + half * (NS // 2) + s // 2 + 1 + START)
                        sp.dma_start(dst[:, bass.ds(b * C + (s % CT) * P, P), cols].rearrange("n p t -> p n t"),
                                     parts[:, s]).then_inc(qk_out[s], 16)
                    if more:
                        sp.wait_ge(v_ps[half], b + 1 + START)
                        load_x(b + 1, half)
                    sp.wait_ge(v_full, b * HALVES + half + 1 + START)
                    for t in range(TB):
                        rows = v_out.rearrange("(i t) w -> i t w", t=T)[bass.ds(b * QUADS, QUADS),
                                                                        half * TILE + t * P:half * TILE + (t + 1) * P]
                        sp.dma_start(rows.rearrange("g t w -> t g w"),
                                     v[:, half, t].rearrange("p (g h) d -> p g (h d)", g=QUADS)).then_inc(v_out_sem[half], 16)
                    if norms:
                        sp.wait_ge(n_split, b * HALVES + half + 1 + START)
                        for side, dst in enumerate((io["q_norm"], io["k_norm"])):
                            for part in range(PARTS):
                                sp.dma_start(dst[part, bass.ds(b * HEADS, HEADS), cols],
                                             n_parts[side * HEADS:(side + 1) * HEADS, half, part]).then_inc(n_out[half], 16)

            for half in range(HALVES):
                load_x(0, half)
            with sp.Fori(0, B - 1) as b:
                batch_row(b, True)
            batch_row(B - 1, False)
            for s in range(NS):
                sp.wait_ge(qk_out[s], 16 * B * HALVES + START)
            for half in range(HALVES):
                sp.wait_ge(v_out_sem[half], 16 * TB * B + START)
                if norms:
                    sp.wait_ge(n_out[half], 16 * 2 * PARTS * B + START)

        @blk.tensor
        def _(pe):
            pe.wait_ge(consts_in, 16 * n_consts + START)
            with pe.Fori(0, B) as b:
                for half in range(HALVES):
                    pe.wait_ge(x_in[half], b * 16 + 16 + START)
                    for s in range(NS):
                        pe.wait_ge(qk_full[s % 2], b * (HALVES * NS // 2) + half * (NS // 2) + s // 2 + START)
                        for a in range(CT):
                            last = nc.tensor.matmul(ps_qk[:, s % 2], w[:, a, s * P:(s + 1) * P], x[:, half, a],
                                                    start=a == 0, stop=a == CT - 1)
                        last.then_inc(qk_ps, 1)
                    pe.wait_ge(v_full, b * HALVES + half + START)
                    for t in range(TB):
                        for a in range(CT):
                            last = nc.tensor.matmul(ps_v[:, t], x[:, half, a, t * P:(t + 1) * P], w[:, a, 2 * C:3 * C],
                                                    start=a == 0, stop=a == CT - 1)
                    last.then_inc(v_ps[half], 1)
                    if norms:
                        pe.wait_ge(squared, b * (HALVES * NS) + (half + 1) * NS + START)
                        pe.wait_ge(n_split, b * HALVES + half + START)
                        for s in range(NS):
                            last = nc.tensor.matmul(ps_n[:, :], select[:, s], squares[:, s],
                                                    start=s == 0, stop=s == NS - 1)
                        last.then_inc(n_ps, 1)

        @blk.scalar
        def _(act):
            act.wait_ge(consts_in, 16 * n_consts + START)
            with act.Fori(0, B) as b:
                for half in range(HALVES):
                    if norms:
                        act.wait_ge(n_ps, b * HALVES + half + START)
                    for s in range(NS):
                        act.wait_ge(qk_ps, b * (HALVES * NS) + half * NS + s + 1 + START)
                        if norms:
                            nc.scalar.activation(squares[:, s], ps_qk[:, s % 2], ACT.Square,
                                                 bias=bias[:, s:s + 1]).then_inc(squared, 1)
                        use = b * (HALVES * NS // 2) + half * (NS // 2) + s // 2
                        act.wait_ge(qk_split[s % 2], use + START)
                        nc.scalar.activation(full[:, s % 2], ps_qk[:, s % 2], ACT.Identity,
                                             bias=bias[:, s:s + 1]).then_inc(qk_full[s % 2], 1)

        @blk.vector
        def _(dve):
            chain = Chain(dve, chain_sem)
            chain.link(nc.vector.memset(v[:, :, :, :, HD:V1], 1.0))
            dve.wait_ge(consts_in, 16 * n_consts + START)
            with dve.Fori(0, B) as b:
                chain.restart()
                for half in range(HALVES):
                    for s in range(NS):
                        use = b * (HALVES * NS // 2) + half * (NS // 2) + s // 2
                        dve.wait_ge(qk_full[s % 2], use + 1 + START)
                        dve.wait_ge(qk_out[s], (b * HALVES + half) * 16 + START)
                        chain.link(nc.vector.tensor_copy(parts[:, s, 0], full[:, s % 2]))
                        chain.link(nc.vector.tensor_tensor(rest[:, s % 2], full[:, s % 2], parts[:, s, 0], ALU.subtract))
                        chain.link(nc.vector.tensor_copy(parts[:, s, 1], rest[:, s % 2]))
                        nc.vector.tensor_tensor(parts[:, s, 2], rest[:, s % 2], parts[:, s, 1],
                                                ALU.subtract).then_inc(qk_split[s % 2], 1)
                    dve.wait_ge(v_ps[half], b + 1 + START)
                    dve.wait_ge(v_out_sem[half], b * (16 * TB) + START)
                    for t in range(TB):
                        last = nc.vector.tensor_tensor(v[:, half, t, :, 0:HD],
                                                       ps_v[:, t].rearrange("p (h d) -> p h d", d=HD),
                                                       bias_v[:, :].rearrange("p (h d) -> p h d", d=HD), ALU.add)
                    last.then_inc(v_full, 1)
                    if norms:
                        dve.wait_ge(n_ps, b * HALVES + half + 1 + START)
                        dve.wait_ge(n_out[half], b * (16 * 2 * PARTS) + START)
                        chain.link(nc.vector.tensor_copy(n_parts[:, half, 0], ps_n[:, :]))
                        chain.link(nc.vector.tensor_tensor(n_rest[:, :], ps_n[:, :], n_parts[:, half, 0], ALU.subtract))
                        chain.link(nc.vector.tensor_copy(n_parts[:, half, 1], n_rest[:, :]))
                        nc.vector.tensor_tensor(n_parts[:, half, 2], n_rest[:, :], n_parts[:, half, 1],
                                                ALU.subtract).then_inc(n_split, 1)


def load_stack(eng, dst, parts, order, rows, landed):
    for blk, part in enumerate(order):
        eng.dma_start(dst[blk * HD:(blk + 1) * HD], parts[part, rows].rearrange("(h d) t -> d h t", d=HD)).then_inc(landed, 16)


def linear_attention(nc, io):
    PAIRS = NQ // 2
    with Phase(nc, "la") as ph:
        omega = ph.sb("omega", [STACK1, FEAT], BF16)
        cap = ph.sb("cap", [P, 4, P])
        ident = ph.sb("ident", [P, P])
        q = [ph.sb(f"q{i}", [STACK1, 4, T], BF16) for i in range(2)]
        k = [ph.sb(f"k{i}", [STACK1, 4, T], BF16) for i in range(2)]
        v = [ph.sb(f"v{i}", [P, BLOCKS, VW]) for i in range(2)]
        phi_kT = ph.sb("phi_kT", [P, 2, 4, P])
        phi_qT = ph.sb("phi_qT", [P, 2, 4, P])
        phi_k = ph.sb("phi_k", [P, 2, 4, FEAT])
        att = ph.sb("att", [P, 2, 4, P])
        stateT = ph.sb("stateT", [P, FEAT])
        state = ph.sb("state", [P, P])
        y = ph.sb("y", [P, 2, T])
        ps_kT, ps_qT, ps_k, ps_att = (ph.ps(n, [P, 4, P]) for n in ("ps_kT", "ps_qT", "ps_k", "ps_att"))
        ps_y = ph.ps("ps_y", [P, TILE])
        ps_stateT = ph.ps("ps_stateT", [P, TILE])
        ps_state = ph.ps("ps_state", [P, TILE])
        consts_in, cleared = ph.sem("consts_in"), ph.sem("cleared")
        landed = ph.sems("landed", 2)
        kT_ps, qT_ps, k_ps, att_ps, y_ps, stateT_ps, state_ps = (
            ph.sem(n) for n in ("kT_ps", "qT_ps", "k_ps", "att_ps", "y_ps", "stateT_ps", "state_ps"))
        kT_done, qT_done, k_done, att_done, stateT_done, state_done = (
            ph.sem(n) for n in ("kT_done", "qT_done", "k_done", "att_done", "stateT_done", "state_done"))
        y_done = ph.sems("y_done", 2)
        stored = ph.sems("stored", 2)
        LOADS = 2 * (len(LEFT) + 1) + 1
        N_CONST = len(RIGHT) + 2
        STORES = 8
        blk = ph.block()

        @blk.sync
        def _(sp):
            ph.start(sp)
            for n, part in enumerate(RIGHT):
                sp.dma_start(omega[n * HD:(n + 1) * HD, :], io["omega_parts"][:, part]).then_inc(consts_in, 16)
            sp.dma_start(cap[:, :, :], io["cap"]).then_inc(consts_in, 16)
            sp.dma_start(ident[:, :], io["ident"]).then_inc(consts_in, 16)

            def load(kk, pr):
                rows = bass.ds(kk * (8 * HD) + pr * (4 * HD), 4 * HD)
                heads = bass.ds(kk * 8 + pr * 4, 4)
                load_stack(sp, q[pr], io["q_parts"], LEFT, rows, landed[pr])
                load_stack(sp, k[pr], io["k_parts"], LEFT, rows, landed[pr])
                sp.dma_start(q[pr][STACK:STACK1], io["q_norm"][:, heads]).then_inc(landed[pr], 16)
                sp.dma_start(k[pr][STACK:STACK1], io["k_norm"][:, heads]).then_inc(landed[pr], 16)
                sp.dma_start(v[pr][:, :, :], io["v"][bass.ds(kk * (2 * T) + pr * T, T)]
                             .rearrange("(n p) w -> p n w", p=P)).then_inc(landed[pr], 16)

            def pair(kk, more):
                for pr in range(2):
                    sp.wait_ge(y_done[pr], kk * BLOCKS + BLOCKS + START)
                    store_y(sp, io, y[:, pr], kk * 8 + pr * 4, stored[pr])
                    if more:
                        load(kk + 1, pr)

            for pr in range(2):
                load(0, pr)
            with sp.Fori(0, PAIRS - 1) as kk:
                pair(kk, True)
            pair(PAIRS - 1, False)
            for pr in range(2):
                sp.wait_ge(stored[pr], PAIRS * 16 * STORES + START)

        @blk.tensor
        def _(pe):
            pe.wait_ge(consts_in, 16 * N_CONST + START)
            pe.wait_ge(cleared, 3 + START)
            with pe.Fori(0, PAIRS) as kk:
                for pr in range(2):
                    def step(c):
                        return kk * (2 * BLOCKS) + pr * BLOCKS + c

                    def state_step(c):
                        return kk * (2 * (BLOCKS - 1)) + pr * (BLOCKS - 1) + c

                    def features(c):
                        cols = slice(c * P, (c + 1) * P)
                        pe.wait_ge(kT_done, step(c) + START)
                        nc.tensor.matmul(ps_kT[:, :, :], omega[:, :], k[pr][:, :, cols],
                                         start=True, stop=True).then_inc(kT_ps, 1)
                        pe.wait_ge(qT_done, step(c) + START)
                        nc.tensor.matmul(ps_qT[:, :, :], omega[:, :], q[pr][:, :, cols],
                                         start=True, stop=True).then_inc(qT_ps, 1)
                        if c < BLOCKS - 1:
                            pe.wait_ge(k_done, state_step(c) + START)
                            for j in range(4):
                                last = nc.tensor.matmul(ps_k[:, j], k[pr][:, j, cols], omega[:, :], start=True, stop=True)
                            last.then_inc(k_ps, 1)

                    pe.wait_ge(landed[pr], kk * (16 * LOADS) + 16 * LOADS + START)
                    features(0)
                    for c in range(BLOCKS):
                        d = c % 2
                        pe.wait_ge(kT_done, step(c) + 1 + START)
                        pe.wait_ge(qT_done, step(c) + 1 + START)
                        pe.wait_ge(att_done, step(c) + START)
                        for j in range(4):
                            last = nc.tensor.matmul(ps_att[:, j], phi_kT[:, d, j], phi_qT[:, d, j], start=True, stop=True)
                        last.then_inc(att_ps, 1)
                        if c < BLOCKS - 1:
                            features(c + 1)
                            pe.wait_ge(k_done, state_step(c) + 1 + START)
                            pe.wait_ge(stateT_done, state_step(c) + START)
                            for j in range(4):
                                last = nc.tensor.matmul(ps_stateT[32 * j:32 * j + V1, 0:FEAT],
                                                        v[pr][:, c, j * V1:(j + 1) * V1], phi_k[:, d, j],
                                                        start=c == 0, stop=True, skip_group_check=True)
                            last.then_inc(stateT_ps, 1)
                        pe.wait_ge(att_done, step(c) + 1 + START)
                        if c == 0:
                            pe.wait_ge(y_done[1 - pr], kk * BLOCKS + pr * BLOCKS + START)
                        else:
                            pe.wait_ge(y_done[pr], kk * BLOCKS + c + START)
                        if c > 0:
                            pe.wait_ge(state_done, state_step(c - 1) + 1 + START)
                        for j in range(4):
                            last = nc.tensor.matmul(ps_y[32 * j:32 * j + V1, 0:P], v[pr][:, c, j * V1:(j + 1) * V1],
                                                    att[:, d, j], start=True, stop=c == 0)
                        if c > 0:
                            for j in range(4):
                                last = nc.tensor.matmul(ps_y[32 * j:32 * j + V1, 0:P], state[:, 32 * j:32 * j + V1],
                                                        phi_qT[:, d, j], start=False, stop=True)
                        last.then_inc(y_ps, 1)
                        if c < BLOCKS - 1:
                            pe.wait_ge(stateT_done, state_step(c) + 1 + START)
                            pe.wait_ge(state_done, state_step(c) + START)
                            nc.tensor.transpose(ps_state[:, 0:P], stateT[:, :], ident[:, :]).then_inc(state_ps, 1)

        @blk.scalar
        def _(act):
            with act.Fori(0, PAIRS) as kk:
                for pr in range(2):
                    def step(c):
                        return kk * (2 * BLOCKS) + pr * BLOCKS + c

                    def state_step(c):
                        return kk * (2 * (BLOCKS - 1)) + pr * (BLOCKS - 1) + c

                    def exps(c):
                        d = c % 2
                        act.wait_ge(kT_ps, step(c) + 1 + START)
                        nc.scalar.activation(phi_kT[:, d], ps_kT[:, :, :], ACT.Exp).then_inc(kT_done, 1)
                        act.wait_ge(qT_ps, step(c) + 1 + START)
                        nc.scalar.activation(phi_qT[:, d], ps_qT[:, :, :], ACT.Exp).then_inc(qT_done, 1)

                    def exp_k(c):
                        act.wait_ge(k_ps, state_step(c) + 1 + START)
                        nc.scalar.activation(phi_k[:, c % 2], ps_k[:, :, :], ACT.Exp).then_inc(k_done, 1)

                    exps(0)
                    exp_k(0)
                    for c in range(BLOCKS - 1):
                        exps(c + 1)
                        act.wait_ge(stateT_ps, state_step(c) + 1 + START)
                        nc.scalar.activation(stateT[:, :], ps_stateT[:, 0:FEAT], ACT.Copy).then_inc(stateT_done, 1)
                        if c < BLOCKS - 2:
                            exp_k(c + 1)

        @blk.vector
        def _(dve):
            nc.vector.memset(omega[STACK:STACK1, :], 1.0).then_inc(cleared, 1)
            nc.vector.memset(ps_y[:, :], 0.0).then_inc(cleared, 1)
            nc.vector.memset(ps_stateT[:, :], 0.0).then_inc(cleared, 1)
            dve.wait_ge(consts_in, 16 * N_CONST + START)
            with dve.Fori(0, PAIRS) as kk:
                for pr in range(2):
                    def step(c):
                        return kk * (2 * BLOCKS) + pr * BLOCKS + c

                    def state_step(c):
                        return kk * (2 * (BLOCKS - 1)) + pr * (BLOCKS - 1) + c

                    dve.wait_ge(stored[pr], kk * (16 * STORES) + START)
                    for c in range(BLOCKS):
                        dve.wait_ge(att_ps, step(c) + 1 + START)
                        nc.vector.tensor_tensor(att[:, c % 2], ps_att[:, :, :], cap[:, :, :], ALU.min).then_inc(att_done, 1)
                        dve.wait_ge(y_ps, step(c) + 1 + START)
                        nc.vector.tensor_copy(y[:, pr, c * P:(c + 1) * P], ps_y[:, 0:P]).then_inc(y_done[pr], 1)
                        if c < BLOCKS - 1:
                            dve.wait_ge(state_ps, state_step(c) + 1 + START)
                            nc.vector.tensor_copy(state[:, :], ps_state[:, 0:P]).then_inc(state_done, 1)


def store_y(eng, io, y, head, stored):
    for j in range(4):
        eng.dma_start(io["y"][bass.ds((head + j) * HD, HD)], y[32 * j:32 * j + HD]).then_inc(stored, 16)
        eng.dma_start(io["den"][bass.ds(head + j, 1)], y[32 * j + HD:32 * j + V1]).then_inc(stored, 16)


def layernorm_stats(nc, dve, chain, z, stats, moments, std):
    for t in range(TB):
        chain.link(nc.vector.bn_stats(stats[:, t], z[:, t])) if t == TB - 1 else nc.vector.bn_stats(stats[:, t], z[:, t])
    for t in range(TB):
        ins = nc.vector.bn_aggr(moments[:, t], stats[:, t])
    chain.link(ins)
    return nc.vector.tensor_scalar(std[:, :], moments[:, :, 1], LN_EPS, None, ALU.add)


def close_attention(nc, io, stage):
    x_d, xo_d, xT_d = io[f"x{stage}"], io[f"x{stage + 1}"], io[f"xT{stage + 1}"]
    eps = DEN_EPS * FEAT if stage == 1 else 0.0
    with Phase(nc, f"cl{stage}") as ph:
        w = ph.sb("w", [P, CT, C])
        bias = ph.sb("bias", [P, TB, C])
        ident = ph.sb("ident", [P, P])
        den = ph.sb("den", [P, T * B * HEADS // P])
        y = ph.sb("y", [P, HALVES, CT, TILE])
        inv = ph.sb("inv", [P, HALVES, CT, TILE])
        yn = ph.sb("yn", [P, HALVES, CT, TILE])
        x = ph.sb("x", [P, HALVES, TB, C])
        xb = ph.sb("xb", [P, HALVES, TB, C])
        z = ph.sb("z", [P, HALVES, TB, C])
        xn = ph.sb("xn", [P, HALVES, TB, C])
        xT = ph.sb("xT", [P, HALVES, CT, TILE])
        stats = ph.sb("stats", [P, TB, 6])
        moments = ph.sb("moments", [P, TB, 2])
        std = ph.sb("std", [P, TB])
        root = ph.sb("root", [P, TB])
        rstd = ph.sb("rstd", [P, TB])
        ps_o = ph.ps("ps_o", [P, HALVES, TB, C])
        ps_t = ph.ps("ps_t", [P, HALVES, CT, TILE])
        consts_in, chain_sem = ph.sem("consts_in"), ph.chain_sem()
        den_in, den_inv, inv_out = ph.sem("den_in"), ph.sem("den_inv"), ph.sem("inv_out")
        landed = ph.sems("landed", HALVES)
        scaled, biased, o_ps, var_ready, rooted = (
            ph.sem(n) for n in ("scaled", "biased", "o_ps", "var_ready", "rooted"))
        normed, t_ps, t_done = (ph.sems(n, HALVES) for n in ("normed", "t_ps", "t_done"))
        stored = ph.sems("stored", HALVES)
        LOADS = 4
        blk = ph.block()

        @blk.sync
        def _(sp):
            ph.start(sp)
            sp.dma_start(den[:, :], io["den"].rearrange("h (s t) -> (h s) t", s=2)).then_inc(den_in, 16)
            sp.dma_start(w[:, :, :], io[f"wo{stage}"].rearrange("(a p) n -> p a n", p=P)).then_inc(consts_in, 16)
            sp.dma_start(bias[:, :, :], io[f"bo{stage}"]).then_inc(consts_in, 16)
            sp.dma_start(ident[:, :], io["ident"]).then_inc(consts_in, 16)
            sp.wait_ge(den_inv, 1 + START)
            sp.dma_start(io["inv"].rearrange("h (s t) -> (h s) t", s=2), den[:, :]).then_inc(inv_out, 16)
            sp.wait_ge(inv_out, 16 + START)
            with sp.Fori(0, B) as b:
                for half in range(HALVES):
                    cols = slice(half * TILE, (half + 1) * TILE)
                    sp.wait_ge(t_ps[half], b + START)
                    sp.dma_start(y[:, half], io["y"][bass.ds(b * C, C), cols]
                                 .rearrange("(a p) t -> p a t", p=P)).then_inc(landed[half], 16)
                    for a in range(CT):
                        heads = io["inv"][bass.ds(b * HEADS + a * (HEADS // CT), HEADS // CT), cols]
                        sp.dma_start(inv[:, half, a], heads.unsqueeze(1).broadcast_to([HEADS // CT, HD, TILE])).then_inc(landed[half], 16)
                    sp.dma_start(x[:, half], x_d[bass.ds(b * T + half * TILE, TILE)]
                                 .rearrange("(n p) c -> p n c", p=P)).then_inc(landed[half], 16)

        @blk.gpsimd
        def _(pool):
            pool.wait_ge(consts_in, 48 + START)
            with pool.Fori(0, B) as b:
                for half in range(HALVES):
                    pool.wait_ge(landed[half], b * (16 * LOADS) + 16 * LOADS + START)
                    pool.wait_ge(t_ps[half], b + START)
                    nc.gpsimd.tensor_tensor(yn[:, half], y[:, half], inv[:, half], ALU.mult).then_inc(scaled, 1)
                    nc.gpsimd.tensor_tensor(xb[:, half], x[:, half], bias[:, :, :], ALU.add).then_inc(biased, 1)

        @blk.tensor
        def _(pe):
            pe.wait_ge(consts_in, 48 + START)
            with pe.Fori(0, B) as b:
                for half in range(HALVES):
                    n = b * HALVES + half
                    pe.wait_ge(scaled, n + 1 + START)
                    pe.wait_ge(normed[half], b + START)
                    for t in range(TB):
                        for a in range(CT):
                            last = nc.tensor.matmul(ps_o[:, half, t], yn[:, half, a, t * P:(t + 1) * P], w[:, a],
                                                    start=a == 0, stop=a == CT - 1)
                    last.then_inc(o_ps, 1)
                    pe.wait_ge(normed[half], b + 1 + START)
                    pe.wait_ge(t_done[half], b + START)
                    for a in range(CT):
                        for t in range(TB):
                            last = nc.tensor.transpose(ps_t[:, half, a, t * P:(t + 1) * P], xn[:, half, t, a * P:(a + 1) * P], ident[:, :])
                    last.then_inc(t_ps[half], 1)

        @blk.scalar
        def _(act):
            with act.Fori(0, B) as b:
                for half in range(HALVES):
                    n = b * HALVES + half
                    act.wait_ge(var_ready, n + 1 + START)
                    nc.scalar.activation(root[:, :], std[:, :], ACT.Sqrt).then_inc(rooted, 1)
                    act.wait_ge(normed[half], b + 1 + START)
                    act.dma_start(xo_d[bass.ds(b * T + half * TILE, TILE)].rearrange("(n p) c -> p n c", p=P),
                                  xn[:, half]).then_inc(stored[half], 16)
                    act.wait_ge(t_ps[half], b + 1 + START)
                    act.wait_ge(stored[half], b * 32 + START)
                    nc.scalar.activation(xT[:, half], ps_t[:, half], ACT.Copy).then_inc(t_done[half], 1)
                    act.wait_ge(t_done[half], b + 1 + START)
                    act.dma_start(xT_d[bass.ds(b * C, C), half * TILE:(half + 1) * TILE].rearrange("(a p) t -> p a t", p=P),
                                  xT[:, half]).then_inc(stored[half], 16)
            for half in range(HALVES):
                act.wait_ge(stored[half], 32 * B + START)

        @blk.vector
        def _(dve):
            chain = Chain(dve, chain_sem)
            dve.wait_ge(den_in, 16 + START)
            if eps:
                chain.link(nc.vector.tensor_scalar(den[:, :], den[:, :], eps, None, ALU.add))
            nc.vector.reciprocal(den[:, :], den[:, :]).then_inc(den_inv, 1)
            dve.wait_ge(den_inv, 1 + START)
            with dve.Fori(0, B) as b:
                chain.restart()
                for half in range(HALVES):
                    n = b * HALVES + half
                    dve.wait_ge(o_ps, n + 1 + START)
                    dve.wait_ge(biased, n + 1 + START)
                    for t in range(0, TB, 2):
                        ins = nc.vector.tensor_tensor(z[:, half, t:t + 2], ps_o[:, half, t:t + 2], xb[:, half, t:t + 2], ALU.add)
                    chain.link(ins)
                    layernorm_stats(nc, dve, chain, z[:, half], stats, moments, std).then_inc(var_ready, 1)
                    dve.wait_ge(rooted, n + 1 + START)
                    chain.link(nc.vector.reciprocal(rstd[:, :], root[:, :]))
                    dve.wait_ge(stored[half], b * 32 + START)
                    for t in range(TB):
                        ins = nc.vector.tensor_scalar(xn[:, half, t], z[:, half, t], moments[:, t, 0:1], rstd[:, t:t + 1],
                                                      ALU.subtract, ALU.mult)
                    ins.then_inc(normed[half], 1)
                    dve.wait_ge(normed[half], b + 1 + START)


KEY_BLOCKS = TILE // P


def score_groups():
    groups, unit = [], 0
    for half in range(HALVES):
        groups.append((half, "rest", None, 0, [unit]))
        unit += 1
        groups.append((half, "memory", None, 0, [unit, unit + 1]))
        unit += 2
        for blk in range((half + 1) * KEY_BLOCKS):
            groups.append((half, "causal", blk, max(0, blk - half * KEY_BLOCKS) * P, [unit, unit + 1]))
            unit += 2
    return groups, unit


GROUPS_OF_QUAD, UNITS = score_groups()
DIAGONALS = 2 * BLOCKS
BANK = 512
MAX_PIECES = [(j, t, n, n * BANK, min(MEM + (t + 1) * P, (n + 1) * BANK))
              for t in range(BLOCKS) for j in range(4) for n in range(-(-(MEM + (t + 1) * P) // BANK))]
PIECES = len(MAX_PIECES)
PIECE_SLOTS = 3


def softmax_attention(nc, io):
    PAIRS = NQ // 2
    with Phase(nc, "sa") as ph:
        ident = ph.sb("ident", [P, P])
        eye = ph.sb("eye", [P, P], BF16)
        later_f = ph.sb("later_f", [P, P])
        later = ph.sb("later", [P, P], BF16)
        q = [ph.sb(f"q{i}", [STACK1, 4, T], BF16) for i in range(2)]
        k = [ph.sb(f"k{i}", [STACK1, 4, T], BF16) for i in range(2)]
        km = [ph.sb(f"km{i}", [STACK1, 4, MEMW], BF16) for i in range(2)]
        v = [ph.sb(f"v{i}", [P, BLOCKS, VW]) for i in range(2)]
        vm = [ph.sb(f"vm{i}", [P, 4, V1]) for i in range(2)]
        vr = [ph.sb(f"vr{i}", [P, P]) for i in range(2)]
        prob = ph.sb("prob", [P, 4, 2, TILE])
        y = ph.sb("y", [P, 2, T])
        piece_max = ph.sb("piece_max", [P, 4, BLOCKS, PIECE_SLOTS])
        neg_max = ph.sb("neg_max", [P, 4 * BLOCKS])
        max_rest = ph.sb("max_rest", [4 * BLOCKS, P])
        max_parts = ph.sb("max_parts", [4 * BLOCKS, 2, PARTS, P], BF16)
        ps_s = ph.ps("ps_s", [P, 2, 2, TILE])
        ps_m = ph.ps("ps_m", [P, 2, BANK])
        ps_y = ph.ps("ps_y", [P, TILE])
        ps_c = ph.ps("ps_c", [4 * BLOCKS, TILE])
        consts_in, cleared, chain_sem = ph.sem("consts_in"), ph.sem("cleared"), ph.chain_sem()
        landed, max_in, stored = ph.sems("landed", 2), ph.sems("max_in", 2), ph.sems("stored", 2)
        scored = ph.sem("scored")
        expd = ph.sems("expd", 2)
        masked, summed = ph.sem("masked"), ph.sem("summed")
        turn = ph.sem("turn")
        y_done = ph.sems("y_done", 2)
        piece_ps, piece_done = ph.sem("piece_ps"), ph.sems("piece_done", 2)
        max_done, max_ps, max_split = ph.sem("max_done"), ph.sem("max_ps"), ph.sem("max_split")
        LOADS = 3 * len(LEFT) + 2 + 4
        STORES = 8
        blk = ph.block()

        @blk.sync
        def _(sp):
            ph.start(sp)
            for dst, name in ((ident, "ident"), (later_f, "later")):
                sp.dma_start(dst[:, :], io[name]).then_inc(consts_in, 16)

            def load(kk, pr):
                rows = bass.ds(kk * (8 * HD) + pr * (4 * HD), 4 * HD)
                load_stack(sp, q[pr], io["q_parts"], LEFT, rows, landed[pr])
                load_stack(sp, k[pr], io["k_parts"], RIGHT, rows, landed[pr])
                for n, part in enumerate(RIGHT):
                    sp.dma_start(km[pr][n * HD:(n + 1) * HD, :, 0:MEM], io["mem_parts"][part, rows]
                                 .rearrange("(h d) s -> d h s", d=HD)).then_inc(landed[pr], 16)
                sp.dma_start(v[pr][:, :, :], io["v"][bass.ds(kk * (2 * T) + pr * T, T)]
                             .rearrange("(n p) w -> p n w", p=P)).then_inc(landed[pr], 16)
                sp.dma_start(vm[pr][:, :, 0:HD], io["mem"][bass.ds(kk * (2 * MEM) + pr * MEM, P)]
                             .rearrange("s (h d) -> s h d", d=HD)).then_inc(landed[pr], 16)
                for j in range(4):
                    sp.dma_start(vr[pr][32 * j:32 * j + MEMR, 32 * j:32 * j + HD],
                                 io["mem"][bass.ds(kk * (2 * MEM) + pr * MEM + P, MEMR), j * HD:(j + 1) * HD]).then_inc(landed[pr], 16)

            def maxima(kk, pr):
                sp.wait_ge(max_split, kk * 2 + pr + 1 + START)
                for part in range(PARTS):
                    sp.dma_start(q[pr][STACK + part:STACK + part + 1].rearrange("a h t -> a (h t)"),
                                 max_parts[:, pr, part]).then_inc(max_in[pr], 16)

            def pair(kk, more):
                for pr in range(2):
                    if pr == 0:
                        maxima(kk, 1)
                    elif more:
                        maxima(kk + 1, 0)
                    sp.wait_ge(y_done[pr], kk * HALVES + HALVES + START)
                    store_y(sp, io, y[:, pr], kk * 8 + pr * 4, stored[pr])
                    if more:
                        load(kk + 1, pr)

            sp.wait_ge(cleared, 1 + START)
            load(0, 0)
            load(0, 1)
            maxima(0, 0)
            with sp.Fori(0, PAIRS - 1) as kk:
                pair(kk, True)
            pair(PAIRS - 1, False)
            for pr in range(2):
                sp.wait_ge(stored[pr], PAIRS * 16 * STORES + START)

        @blk.tensor
        def _(pe):
            pe.wait_ge(consts_in, 32 + START)
            pe.wait_ge(cleared, 1 + START)

            def piece(kk, pr, m):
                j, t, _, lo, hi = MAX_PIECES[m]
                s = m % 2
                qs = q[pr][0:STACK, j, t * P:(t + 1) * P]
                pe.wait_ge(piece_done[s], kk * PIECES + pr * (PIECES // 2) + m // 2 + START)
                if lo == 0:
                    nc.tensor.matmul(ps_m[:, s, 0:MEM], qs, km[pr][0:STACK, j, 0:MEM], start=True, stop=True, skip_group_check=True)
                a = max(lo, MEM)
                last = nc.tensor.matmul(ps_m[:, s, a - lo:hi - lo], qs, k[pr][0:STACK, j, a - MEM:hi - MEM],
                                        start=lo > 0, stop=True, skip_group_check=True)
                a, e = max(lo, MEM + t * P), hi
                if a < e:
                    first = MEM + t * P
                    last = nc.tensor.matmul(ps_m[:, s, a - lo:e - lo], eye[:, :], later[:, a - first:e - first],
                                            start=False, stop=True, skip_group_check=True)
                last.then_inc(piece_ps, 1)

            def turn_maxima(kk, pr):
                pe.wait_ge(max_done, kk * 2 + pr + 1 + START)
                pe.wait_ge(max_split, kk * 2 + pr + START)
                nc.tensor.transpose(ps_c[:, 0:P], neg_max[:, :], ident[:, :]).then_inc(max_ps, 1)

            def scores(kk, pr, group, u):
                half, kind, kb, first, units = group
                s = u % 2
                pe.wait_ge(expd[s], kk * UNITS + (pr * UNITS + u) // 2 + START)
                queries = slice(half * TILE + first, (half + 1) * TILE)
                if kind == "rest":
                    for j in range(4):
                        last = nc.tensor.matmul(ps_s[32 * j:32 * j + 32, s, 0], km[pr][:, j, P:MEMW], q[pr][:, j, queries],
                                                start=True, stop=True)
                else:
                    for jj in range(2):
                        j = 2 * (u - units[0]) + jj
                        keys = km[pr][:, j, 0:P] if kind == "memory" else k[pr][:, j, kb * P:(kb + 1) * P]
                        last = nc.tensor.matmul(ps_s[:, s, jj, 0:TILE - first], keys, q[pr][:, j, queries], start=True, stop=True)
                last.then_inc(scored, 1)

            def sums(kk, pr, group, n_masked, finish):
                half, kind, kb, first, units = group
                for u in units:
                    pe.wait_ge(expd[u % 2], kk * UNITS + (pr * UNITS + u) // 2 + 1 + START)
                if n_masked:
                    pe.wait_ge(masked, kk * (2 * DIAGONALS) + pr * DIAGONALS + n_masked + START)
                if kind == "rest":
                    if half == 1:
                        pe.wait_ge(y_done[pr], kk * HALVES + 1 + START)
                    elif pr == 1:
                        pe.wait_ge(y_done[0], kk * HALVES + HALVES + START)
                    else:
                        pe.wait_ge(y_done[1], kk * HALVES + START)
                    slot = (pr * UNITS + units[0]) % 4
                    last = nc.tensor.matmul(ps_y[:, :], vr[pr][:, :], prob[:, slot, 0], start=True, stop=True, skip_group_check=True)
                else:
                    for j in range(4):
                        slot = (pr * UNITS + units[j // 2]) % 4
                        values = vm[pr][:, j] if kind == "memory" else v[pr][:, kb, j * V1:(j + 1) * V1]
                        last = nc.tensor.matmul(ps_y[32 * j:32 * j + V1, first:TILE], values, prob[:, slot, j % 2, 0:TILE - first],
                                                start=False, stop=True, skip_group_check=True)
                if finish:
                    last.then_inc(summed, 1)

            def quad(kk, pr, following):
                pe.wait_ge(max_in[pr], kk * (16 * PARTS) + 16 * PARTS + START)
                if following is not None:
                    pe.wait_ge(landed[following[1]], following[0] * (16 * LOADS) + 16 * LOADS + START)
                done, n_masked, before, steps = 0, 0, None, 0
                total_steps = UNITS - 1
                for g, group in enumerate(GROUPS_OF_QUAD):
                    for u in group[4]:
                        scores(kk, pr, group, u)
                        if following is not None:
                            steps += 1
                            until = min(PIECES, -(-PIECES * steps // total_steps))
                            while done < until:
                                piece(*following, done)
                                done += 1
                    if before is not None:
                        sums(kk, pr, *before)
                    if group[1] == "causal" and group[2] >= group[0] * KEY_BLOCKS:
                        n_masked += 2
                    diagonal = group[1] == "causal" and group[2] >= group[0] * KEY_BLOCKS
                    end = g + 1 == len(GROUPS_OF_QUAD) or GROUPS_OF_QUAD[g + 1][1] == "rest"
                    before = (group, n_masked if diagonal else 0, end)
                sums(kk, pr, *before)
                if following is not None:
                    turn_maxima(*following)

            pe.wait_ge(landed[0], 16 * LOADS + START)
            for m in range(PIECES):
                piece(0, 0, m)
            turn_maxima(0, 0)
            with pe.Fori(0, PAIRS - 1) as kk:
                quad(kk, 0, (kk, 1))
                quad(kk, 1, (kk + 1, 0))
            quad(PAIRS - 1, 0, (PAIRS - 1, 1))
            quad(PAIRS - 1, 1, None)

        @blk.scalar
        def _(act):
            with act.Fori(0, PAIRS) as kk:
                for pr in range(2):
                    for g, (half, kind, kb, first, units) in enumerate(GROUPS_OF_QUAD):
                        for u in units:
                            s, slot = u % 2, (pr * UNITS + u) % 4
                            act.wait_ge(scored, kk * (2 * UNITS) + pr * UNITS + u + 1 + START)
                            if kind == "rest":
                                src, dst = ps_s[:, s, 0], prob[:, slot, 0]
                            else:
                                src, dst = ps_s[:, s, :, 0:TILE - first], prob[:, slot, :, 0:TILE - first]
                            nc.scalar.activation(dst, src, ACT.Exp, scale=HD ** -0.5).then_inc(expd[s], 1)
                        if kind == "rest" and half == 1:
                            copy_half(nc, act, kk, pr, 0, y, ps_y, summed, stored, y_done, STORES)
                    copy_half(nc, act, kk, pr, 1, y, ps_y, summed, stored, y_done, STORES)

        @blk.gpsimd
        def _(pool):
            with pool.Fori(0, PAIRS) as kk:
                for pr in range(2):
                    for half, kind, kb, first, units in GROUPS_OF_QUAD:
                        if kind == "causal" and kb >= half * KEY_BLOCKS:
                            for u in units:
                                pool.wait_ge(expd[u % 2], kk * UNITS + (pr * UNITS + u) // 2 + 1 + START)
                                pool.sem_inc(turn, 1)
                                square = prob[:, (pr * UNITS + u) % 4, :, 0:P]
                                nc.gpsimd.affine_select(out=square, in_=square, compare_op=ALU.is_ge, fill=0.0, base=0,
                                                        pattern=[[0, 2], [1, P]], channel_multiplier=-1).then_inc(masked, 1)

        @blk.vector
        def _(dve):
            chain = Chain(dve, chain_sem)
            for i in range(2):
                chain.link(nc.vector.memset(km[i][:, :, :], 0.0))
                nc.vector.memset(km[i][STACK:STACK1, :, 0:MEM], 1.0)
                nc.vector.memset(k[i][STACK:STACK1, :, :], 1.0)
                nc.vector.memset(vm[i][:, :, HD:V1], 1.0)
                chain.link(nc.vector.memset(vr[i][:, :], 0.0))
                for j in range(4):
                    nc.vector.memset(vr[i][32 * j:32 * j + MEMR, 32 * j + HD:32 * j + V1], 1.0)
            dve.wait_ge(consts_in, 32 + START)
            nc.vector.tensor_copy(eye[:, :], ident[:, :])
            nc.vector.tensor_copy(later[:, :], later_f[:, :])
            chain.link(nc.vector.memset(piece_max[:, :, :, :], -BIG))
            nc.vector.memset(ps_y[:, :], 0.0).then_inc(cleared, 1)

            def maxima(kk, pr):
                for m, (j, t, n, lo, hi) in enumerate(MAX_PIECES):
                    dve.wait_ge(piece_ps, kk * (2 * PIECES) + pr * PIECES + m + 1 + START)
                    nc.vector.tensor_reduce(piece_max[:, j, t, n:n + 1], ps_m[:, m % 2, 0:hi - lo], AX.X, ALU.max).then_inc(piece_done[m % 2], 1)
                for s in range(2):
                    dve.wait_ge(piece_done[s], kk * PIECES + (pr + 1) * (PIECES // 2) + START)
                nc.vector.tensor_reduce(neg_max[:, :], piece_max[:, :, :, :].rearrange("p h t n -> p (h t) n"),
                                        AX.X, ALU.max, negate=True).then_inc(max_done, 1)
                dve.wait_ge(max_ps, kk * 2 + pr + 1 + START)
                dve.wait_ge(max_in[pr], kk * (16 * PARTS) + START)
                chain.link(nc.vector.tensor_copy(max_parts[:, pr, 0], ps_c[:, 0:P]))
                chain.link(nc.vector.tensor_tensor(max_rest[:, :], ps_c[:, 0:P], max_parts[:, pr, 0], ALU.subtract))
                chain.link(nc.vector.tensor_copy(max_parts[:, pr, 1], max_rest[:, :]))
                nc.vector.tensor_tensor(max_parts[:, pr, 2], max_rest[:, :], max_parts[:, pr, 1], ALU.subtract).then_inc(max_split, 1)

            with dve.Fori(0, PAIRS) as kk:
                chain.restart()
                for pr in range(2):
                    maxima(kk, pr)


def copy_half(nc, act, kk, pr, half, y, ps_y, summed, stored, y_done, stores):
    act.wait_ge(summed, kk * (2 * HALVES) + pr * HALVES + half + 1 + START)
    act.wait_ge(stored[pr], kk * (16 * stores) + START)
    nc.scalar.activation(y[:, pr, half * TILE:(half + 1) * TILE], ps_y[:, :], ACT.Copy).then_inc(y_done[pr], 1)


def experts(nc, io):
    NT = B * HALVES
    ALLB = NT * TB
    CHUNK = 3
    N_CHUNKS = ALL_EXPERTS // CHUNK
    E2 = ALL_EXPERTS // 2
    O_USES = (1 + EXPERTS // 2, EXPERTS // 2)
    with Phase(nc, "mo") as ph:
        gate = ph.sb("gate", [P, CT, ALL_EXPERTS, INNER])
        up = ph.sb("up", [P, CT, ALL_EXPERTS, INNER])
        down = ph.sb("down", [P, ALL_EXPERTS, C])
        router = ph.sb("router", [P, CT, EXPERTS])
        e_bias = ph.sb("e_bias", [P, ALLB, EXPERTS])
        rank0 = ph.sb("rank0", [P, ALLB, EXPERTS])
        grank0 = ph.sb("grank0", [P, ALLB, GROUPS])
        xT = ph.sb("xT", [P, HALVES, CT, TILE])
        x = ph.sb("x", [P, HALVES, TB, C])
        comb = ph.sb("comb", [P, HALVES, TB, EXPERTS])
        silu = ph.sb("silu", [P, 2, TILE])
        h = ph.sb("h", [P, 2, TILE])
        acc = ph.sb("acc", [P, HALVES, TB, C])
        o = ph.sb("o", [P, HALVES, TB, C])
        stats, moments = ph.sb("stats", [P, TB, 6]), ph.sb("moments", [P, TB, 2])
        std, root, rstd = (ph.sb(n, [P, TB]) for n in ("std", "root", "rstd"))
        score, biased, keep, rank, ge = (ph.sb(n, [P, ALLB, EXPERTS]) for n in ("score", "biased", "keep", "rank", "ge"))
        pair_hi, pair_lo = ph.sb("pair_hi", [P, ALLB, GROUPS, 2]), ph.sb("pair_lo", [P, ALLB, GROUPS, 2])
        g1, g2, g3, gsum, grank, gge = (ph.sb(n, [P, ALLB, GROUPS]) for n in ("g1", "g2", "g3", "gsum", "grank", "gge"))
        wsum = ph.sb("wsum", [P, ALLB])
        ps_g, ps_u = ph.ps("ps_g", [P, 2, TILE]), ph.ps("ps_u", [P, 2, TILE])
        ps_o = ph.ps("ps_o", [P, 2, TB, C])
        consts_in, chain_sem = ph.sem("consts_in"), ph.chain_sem()
        w_in = ph.sems("w_in", N_CHUNKS)
        rx_in = ph.sems("rx_in", HALVES)
        rx_used, logits, sigmoid, routed, comb_out = (ph.sem(n) for n in ("rx_used", "logits", "sigmoid", "routed", "comb_out"))
        landed = ph.sems("landed", HALVES)
        g_ps, u_ps, silu_done = ph.sem("g_ps"), ph.sem("u_ps"), ph.sem("silu_done")
        h_done, o_done = ph.sems("h_done", 2), ph.sems("o_done", 2)
        o_ps, var_ready, rooted = ph.sem("o_ps"), ph.sem("var_ready"), ph.sem("rooted")
        normed, stored = ph.sems("normed", HALVES), ph.sems("stored", HALVES)
        blk = ph.block()

        @blk.sync
        def _(sp):
            ph.start(sp)
            sp.dma_start(router[:, :, :], io["router"].rearrange("(a p) e -> p a e", p=P)).then_inc(consts_in, 16)

            def load_xT(b, half, sem):
                sp.dma_start(xT[:, half], io["xT3"][bass.ds(b * C, C), half * TILE:(half + 1) * TILE]
                             .rearrange("(a p) t -> p a t", p=P)).then_inc(sem, 16)

            for n in range(NT):
                if n >= 2:
                    sp.wait_ge(rx_used, n - 1 + START)
                load_xT(n // HALVES, n % HALVES, rx_in[n % HALVES])
                if n == 0:
                    for dst, name in ((e_bias, "e_bias"), (rank0, "rank0"), (grank0, "grank0")):
                        sp.dma_start(dst[:, :, :], io[name]).then_inc(consts_in, 16)
            for ch in range(N_CHUNKS):
                es = slice(ch * CHUNK, (ch + 1) * CHUNK)
                sp.dma_start(gate[:, :, es], io["gate"][:, :, es]).then_inc(w_in[ch], 16)
                sp.dma_start(up[:, :, es], io["up"][:, :, es]).then_inc(w_in[ch], 16)
                sp.dma_start(down[:, es], io["down"][:, es]).then_inc(w_in[ch], 16)
            sp.wait_ge(routed, 1 + START)
            sp.dma_start(io["combine"].rearrange("(n p) e -> p n e", p=P), keep[:, :, :]).then_inc(comb_out, 16)
            sp.wait_ge(comb_out, 16 + START)
            sp.wait_ge(rx_used, NT + START)

            def load(b, half):
                load_xT(b, half, landed[half])
                rows = bass.ds(b * T + half * TILE, TILE)
                sp.dma_start(x[:, half], io["x3"][rows].rearrange("(n p) c -> p n c", p=P)).then_inc(landed[half], 16)
                sp.dma_start(comb[:, half], io["combine"][rows].rearrange("(n p) e -> p n e", p=P)).then_inc(landed[half], 16)

            def batch_row(b, more):
                for half in range(HALVES):
                    sp.wait_ge(normed[half], b + 1 + START)
                    sp.dma_start(io["out"][bass.ds(b * T + half * TILE, TILE)].rearrange("(n p) c -> p n c", p=P),
                                 o[:, half]).then_inc(stored[half], 16)
                    if more:
                        load(b + 1, half)

            for half in range(HALVES):
                load(0, half)
            with sp.Fori(0, B - 1) as b:
                batch_row(b, True)
            batch_row(B - 1, False)
            for half in range(HALVES):
                sp.wait_ge(stored[half], 16 * B + START)

        @blk.tensor
        def _(pe):
            pe.wait_ge(consts_in, 16 + START)
            logit = ps_g[:, 0].rearrange("p (n e) -> p n e", e=EXPERTS)
            for n in range(NT):
                half = n % HALVES
                pe.wait_ge(rx_in[half], 16 * (n // HALVES + 1) + START)
                for t in range(TB):
                    for a in range(CT):
                        last = nc.tensor.matmul(logit[:, n * TB + t], xT[:, half, a, t * P:(t + 1) * P], router[:, a],
                                                start=a == 0, stop=a == CT - 1)
                last.then_inc(rx_used, 1)
            pe.wait_ge(sigmoid, 1 + START)

            with pe.Fori(0, B) as b:
                for half in range(HALVES):
                    def use(per_tile, i):
                        return b * (HALVES * per_tile) + half * per_tile + i

                    def gate_up(e):
                        s = e % 2
                        pe.wait_ge(w_in[e // CHUNK], 48 + START)
                        pe.wait_ge(h_done[s], use(E2, e // 2) + START)
                        for w, ps, ready in ((gate, ps_g, g_ps), (up, ps_u, u_ps)):
                            for a in range(CT):
                                last = nc.tensor.matmul(ps[:, s], w[:, a, e], xT[:, half, a], start=a == 0, stop=a == CT - 1)
                            last.then_inc(ready, 1)

                    def project_down(es, slot_use):
                        s = slot_use % 2
                        for e in es:
                            pe.wait_ge(h_done[e % 2], use(E2, e // 2) + 1 + START)
                        pe.wait_ge(o_done[s], use(O_USES[s], slot_use // 2) + START)
                        for t in range(TB):
                            for i, e in enumerate(es):
                                last = nc.tensor.matmul(ps_o[:, s, t], h[:, e % 2, t * P:(t + 1) * P], down[:, e],
                                                        start=i == 0, stop=i == len(es) - 1)
                        last.then_inc(o_ps, 1)

                    pe.wait_ge(landed[half], b * 48 + 48 + START)
                    gate_up(0)
                    gate_up(1)
                    project_down((0, 1), 0)
                    gate_up(2)
                    for e in range(2, ALL_EXPERTS):
                        if e + 1 < ALL_EXPERTS:
                            gate_up(e + 1)
                        project_down((e,), e - 1)

        @blk.scalar
        def _(act):
            act.wait_ge(rx_used, NT + START)
            nc.scalar.activation(score[:, :, :], ps_g[:, 0].rearrange("p (n e) -> p n e", e=EXPERTS), ACT.Sigmoid).then_inc(sigmoid, 1)
            with act.Fori(0, B) as b:
                for half in range(HALVES):
                    n = b * HALVES + half
                    for e in range(ALL_EXPERTS):
                        act.wait_ge(g_ps, b * (HALVES * ALL_EXPERTS) + half * ALL_EXPERTS + e + 1 + START)
                        nc.scalar.activation(silu[:, e % 2], ps_g[:, e % 2], ACT.Silu).then_inc(silu_done, 1)
                    act.wait_ge(var_ready, n + 1 + START)
                    nc.scalar.activation(root[:, :], std[:, :], ACT.Sqrt).then_inc(rooted, 1)

        @blk.vector
        def _(dve):
            chain = Chain(dve, chain_sem)
            tt, ts = nc.vector.tensor_tensor, nc.vector.tensor_scalar
            link = chain.link
            dve.wait_ge(consts_in, 64 + START)
            dve.wait_ge(sigmoid, 1 + START)
            link(tt(biased[:, :, :], score[:, :, :], e_bias[:, :, :], ALU.add))
            four = biased[:, :, :].rearrange("p n (g a b) -> p n g a b", g=GROUPS, a=2)
            tt(pair_hi[:, :, :, :], four[:, :, :, :, 0], four[:, :, :, :, 1], ALU.max)
            link(tt(pair_lo[:, :, :, :], four[:, :, :, :, 0], four[:, :, :, :, 1], ALU.min))
            tt(g1[:, :, :], pair_hi[:, :, :, 0], pair_hi[:, :, :, 1], ALU.max)
            tt(g2[:, :, :], pair_hi[:, :, :, 0], pair_hi[:, :, :, 1], ALU.min)
            link(tt(g3[:, :, :], pair_lo[:, :, :, 0], pair_lo[:, :, :, 1], ALU.max))
            link(tt(g2[:, :, :], g2[:, :, :], g3[:, :, :], ALU.max))
            link(tt(gsum[:, :, :], g1[:, :, :], g2[:, :, :], ALU.add))

            def ranks(values, out, first, ahead, width):
                link(nc.vector.tensor_copy(out[:, :, :], first[:, :, :]))
                for d in range(1, width):
                    w = width - d
                    link(tt(ahead[:, :, 0:w], values[:, :, 0:w], values[:, :, d:width], ALU.is_ge))
                    link(tt(out[:, :, d:width], out[:, :, d:width], ahead[:, :, 0:w], ALU.add))
                    link(tt(out[:, :, 0:w], out[:, :, 0:w], ahead[:, :, 0:w], ALU.subtract))

            ranks(gsum, grank, grank0, gge, GROUPS)
            link(ts(gge[:, :, :], grank[:, :, :], float(TOP_GROUPS), None, ALU.is_lt))
            per = EXPERTS // GROUPS
            for i in range(per):
                last = tt(biased[:, :, i::per], biased[:, :, i::per], gge[:, :, :], ALU.mult)
            link(last)
            ranks(biased, rank, rank0, ge, EXPERTS)
            link(ts(keep[:, :, :], rank[:, :, :], float(TOPK), None, ALU.is_lt))
            link(tt(keep[:, :, :], keep[:, :, :], score[:, :, :], ALU.mult))
            link(nc.vector.tensor_reduce(wsum[:, :], keep[:, :, :], AX.X, ALU.add))
            link(ts(wsum[:, :], wsum[:, :], 1e-20, None, ALU.add))
            link(nc.vector.reciprocal(wsum[:, :], wsum[:, :]))
            link(ts(wsum[:, :], wsum[:, :], ROUTE_SCALE, None, ALU.mult))
            tt(keep[:, :, :], keep[:, :, :], wsum[:, :].unsqueeze(2).broadcast_to([P, ALLB, EXPERTS]), ALU.mult).then_inc(routed, 1)

            with dve.Fori(0, B) as b:
                chain.restart()
                for half in range(HALVES):
                    n = b * HALVES + half
                    base_e = b * (HALVES * ALL_EXPERTS) + half * ALL_EXPERTS
                    base_o = b * (HALVES * (EXPERTS + 1)) + half * (EXPERTS + 1)

                    def multiply(e):
                        dve.wait_ge(silu_done, base_e + e + 1 + START)
                        dve.wait_ge(u_ps, base_e + e + 1 + START)
                        tt(h[:, e % 2], silu[:, e % 2], ps_u[:, e % 2], ALU.mult).then_inc(h_done[e % 2], 1)

                    def add_up(i):
                        s = i % 2
                        dve.wait_ge(o_ps, base_o + i + 1 + START)
                        if i == 0:
                            for t in range(0, TB, 2):
                                last = tt(acc[:, half, t:t + 2], ps_o[:, s, t:t + 2], x[:, half, t:t + 2], ALU.add)
                        else:
                            uses = O_USES[(i - 1) % 2]
                            dve.wait_ge(o_done[(i - 1) % 2], b * (HALVES * uses) + half * uses + (i - 1) // 2 + 1 + START)
                            for t in range(TB):
                                last = nc.vector.scalar_tensor_tensor(acc[:, half, t], ps_o[:, s, t], comb[:, half, t, i - 1:i],
                                                                      acc[:, half, t], ALU.mult, ALU.add)
                        last.then_inc(o_done[s], 1)

                    dve.wait_ge(landed[half], b * 48 + 48 + START)
                    for e in range(3):
                        multiply(e)
                    for e in range(3, ALL_EXPERTS):
                        add_up(e - 3)
                        multiply(e)
                    for i in range(ALL_EXPERTS - 3, ALL_EXPERTS - 1):
                        add_up(i)
                    dve.wait_ge(o_done[0], b * (HALVES * O_USES[0]) + (half + 1) * O_USES[0] + START)
                    layernorm_stats(nc, dve, chain, acc[:, half], stats, moments, std).then_inc(var_ready, 1)
                    dve.wait_ge(rooted, n + 1 + START)
                    chain.link(nc.vector.reciprocal(rstd[:, :], root[:, :]))
                    dve.wait_ge(stored[half], b * 16 + START)
                    for t in range(TB):
                        last = ts(o[:, half, t], acc[:, half, t], moments[:, t, 0:1], rstd[:, t:t + 1], ALU.subtract, ALU.mult)
                    last.then_inc(normed[half], 1)


SCRATCH = {
    "omega_parts": ((HD, PARTS, FEAT), BF16), "mem_parts": ((PARTS, B * C, MEM), BF16),
    "q_parts": ((PARTS, B * C, T), BF16), "k_parts": ((PARTS, B * C, T), BF16),
    "q_norm": ((PARTS, B * HEADS, T), BF16), "k_norm": ((PARTS, B * HEADS, T), BF16),
    "v": ((NQ * T, VW), F32), "y": ((B * C, T), F32), "den": ((B * HEADS, T), F32), "inv": ((B * HEADS, T), F32),
    "combine": ((B * T, EXPERTS), F32), "x2": ((B * T, C), F32), "x3": ((B * T, C), F32), "xT2": ((B * C, T), F32), "xT3": ((B * C, T), F32),
}


def decoder_layer(nc, io, phases=("const", "p1", "a1", "c1", "p2", "a2", "c2", "moe")):
    for name, (shape, dt) in SCRATCH.items():
        if name not in io:
            io[name] = nc.dram_tensor(f"s_{name}", shape, dt).ap()
    if "const" in phases:
        split_constants(nc, io)
    if "p1" in phases:
        project(nc, io, 1)
    if "a1" in phases:
        linear_attention(nc, io)
    if "c1" in phases:
        close_attention(nc, io, 1)
    if "p2" in phases:
        project(nc, io, 2)
    if "a2" in phases:
        softmax_attention(nc, io)
    if "c2" in phases:
        close_attention(nc, io, 2)
    if "moe" in phases:
        experts(nc, io)


def lay_out(x, ctx_1024, L0_attn_W_attn, L0_attn_b_attn, L0_attn_W_proj, L0_attn_b_proj, L0_attn_omega,
            L0_xattn_W_attn, L0_xattn_b_attn, L0_xattn_W_proj, L0_xattn_b_proj, L0_ffn_router_weight,
            L0_ffn_e_bias, L0_ffn_gate_w, L0_ffn_up_w, L0_ffn_down_w, L0_ffn_sh_gate_w, L0_ffn_sh_up_w,
            L0_ffn_sh_down_w):
    import numpy as np

    def rows(v, n):
        return np.ascontiguousarray(np.broadcast_to(np.asarray(v)[None], (n, *np.asarray(v).shape)))

    a = {}
    x = np.asarray(x)
    a["x1"] = x.reshape(B * T, C)
    a["xT1"] = x.transpose(0, 2, 1).reshape(B * C, T)
    ctx = np.asarray(ctx_1024)
    a["memT"] = ctx.transpose(0, 2, 1).reshape(B * C, MEM)
    a["mem"] = ctx.reshape(B, MEM, QUADS, 4 * HD).transpose(0, 2, 1, 3).reshape(NQ * MEM, 4 * HD)
    a["omega"] = np.asarray(L0_attn_omega)
    for n, (w, b, wo, bo) in enumerate(((L0_attn_W_attn, L0_attn_b_attn, L0_attn_W_proj, L0_attn_b_proj),
                                        (L0_xattn_W_attn, L0_xattn_b_attn, L0_xattn_W_proj, L0_xattn_b_proj)), 1):
        a[f"w{n}"] = np.asarray(w)
        a[f"bT{n}"] = np.asarray(b).reshape(6, P).T
        a[f"bv{n}"] = rows(np.asarray(b)[2 * C:], P)
        a[f"wo{n}"] = np.asarray(wo)
        a[f"bo{n}"] = rows(rows(bo, TB), P)
    a["router"] = np.asarray(L0_ffn_router_weight).T
    a["e_bias"] = rows(rows(L0_ffn_e_bias, B * BLOCKS), P)
    a["rank0"] = rows(rows(np.arange(EXPERTS - 1, -1, -1, dtype=np.float32), B * BLOCKS), P)
    a["grank0"] = rows(rows(np.arange(GROUPS - 1, -1, -1, dtype=np.float32), B * BLOCKS), P)
    for name, routed, shared in (("gate", L0_ffn_gate_w, L0_ffn_sh_gate_w), ("up", L0_ffn_up_w, L0_ffn_sh_up_w)):
        both = np.concatenate([np.asarray(shared).reshape(SHARED, INNER, C), np.asarray(routed)])
        a[name] = both.transpose(2, 0, 1).reshape(CT, P, ALL_EXPERTS, INNER).transpose(1, 0, 2, 3)
    down = np.concatenate([np.asarray(L0_ffn_sh_down_w).reshape(C, SHARED, INNER).transpose(1, 0, 2), np.asarray(L0_ffn_down_w)])
    a["down"] = down.transpose(2, 0, 1)
    eye = np.eye(P, dtype=np.float32)
    a["ident"] = eye
    a["cap"] = rows(np.where(np.arange(P)[:, None] <= np.arange(P)[None], np.finfo(np.float32).max, np.float32(0)), 4).transpose(1, 0, 2)
    sel = np.zeros((P, 2 * CT, 32), np.float32)
    for s in range(2 * CT):
        for p in range(P):
            sel[p, s, (s // CT) * HEADS + (s % CT) * (P // HD) + p // HD] = -0.5 / HD
    a["select"] = sel
    a["later"] = np.where(np.arange(P)[None] <= np.arange(P)[:, None], np.float32(0), np.float32(-1.0e30))
    return {k: np.ascontiguousarray(v) for k, v in a.items()}


def kernel(**inputs):
    import numpy as np
    import concourse.bacc as bacc
    from concourse.bass_utils import run_bass_kernel_spmd

    arrays = lay_out(**inputs)
    nc = bacc.Bacc("TRN2", target_bir_lowering=False, num_devices=1)
    io = {n: nc.dram_tensor(n, a.shape, mybir.dt.from_np(a.dtype), kind="ExternalInput").ap() for n, a in arrays.items()}
    io["out"] = nc.dram_tensor("out", (B * T, C), F32, kind="ExternalOutput").ap()
    decoder_layer(nc, io)
    r = run_bass_kernel_spmd(nc, [arrays], core_ids=[0])
    return r.results[0]["out"].reshape(B, T, C)
```

```python
from contextlib import ExitStack

import concourse.bass as bass
from concourse import mybir

F32 = mybir.dt.float32
BF16 = mybir.dt.bfloat16
F32R = mybir.dt.float32r
ALU = mybir.AluOpType
ACT = mybir.ActivationFunctionType
AX = mybir.AxisListType

B, T, C = 4, 1024, 256
HEADS, HD = 16, 16
FEAT = 128
MEM = 154
EXPERTS, SHARED, INNER = 16, 2, 128
ALL_EXPERTS = EXPERTS + SHARED
TOPK, GROUPS, TOP_GROUPS, ROUTE_SCALE = 4, 4, 2, 2.5
LN_EPS = 1e-5
DEN_EPS = 1e-6
P = 128
TILE = 512
HALVES = T // TILE
CT = C // P
TB = TILE // P
QUADS = HEADS // 4
NQ = B * QUADS
BLOCKS = T // P
V1 = HD + 1
VW = 4 * V1
PARTS = 3
LEFT = ((0, 3, 0, 1), (3, 2, 1, 1), (5, 1, 2, 1))
RIGHT = ((0, 3, 0, 3), (3, 2, 0, 2), (5, 1, 0, 1))
SIX = 6
STACK = SIX * HD
STACK1 = STACK + PARTS
START = 1
BIG = 3.0e38
MEMR = MEM - P
MEMW = P + 32


class Phase:

    def __init__(self, nc, name):
        self.nc, self.name, self.ctx, self.held = nc, name, ExitStack(), []
        self.chain = None

    def __enter__(self):
        return self

    def __exit__(self, *a):
        self.ctx.__exit__(*a)
        if a[0] is None:
            self.nc.clear_and_free_semaphores(self.held)
            self.nc.all_engine_barrier()

    def sb(self, name, shape, dt=F32):
        return self.ctx.enter_context(self.nc.sbuf_tensor(f"{self.name}_{name}", shape, dt))

    def ps(self, name, shape, dt=F32):
        return self.ctx.enter_context(self.nc.psum_tensor(f"{self.name}_{name}", shape, dt))

    def sem(self, name):
        self.held.append(self.nc.alloc_semaphore(f"{self.name}_{name}"))
        return self.held[-1]

    def chain_sem(self):
        self.held.append(self.nc.alloc_semaphore(f"{self.name}_chain"))
        self.chain = self.held[-1]
        return self.chain

    def start(self, eng):
        for sem in self.held:
            if sem is not self.chain:
                eng.sem_inc(sem, START)

    def sems(self, name, n):
        return [self.sem(f"{name}{i}") for i in range(n)]

    def block(self):
        return self.ctx.enter_context(self.nc.Block())


class Chain:

    def __init__(self, eng, sem):
        self.eng, self.sem, self.n = eng, sem, 0

    def restart(self):
        self.eng.sem_clear(self.sem)
        self.n = 0

    def link(self, ins):
        self.n += 1
        ins.then_inc(self.sem, 1)
        self.eng.wait_ge(self.sem, self.n)


def store_stack(eng, dst, parts, order, stored):
    for first, count, part, n in order:
        src = parts[:, part:part + n]
        if n < count:
            src = src.broadcast_to([src.shape[0], count, src.shape[2]])
        eng.dma_start(dst[:, first:first + count], src).then_inc(stored, 16)


def split_constants(nc, io):
    with Phase(nc, "sc") as ph:
        om = ph.sb("om", [HD, FEAT])
        om_rest = ph.sb("om_rest", [HD, FEAT])
        om_parts = ph.sb("om_parts", [HD, PARTS, FEAT], BF16)
        n_tiles = B * C // P
        mk = ph.sb("mk", [P, n_tiles, MEM])
        mk_rest = ph.sb("mk_rest", [P, n_tiles, MEM])
        mk_parts = ph.sb("mk_parts", [P, PARTS, n_tiles, MEM], BF16)
        loaded, split, stored, chain_sem = ph.sem("loaded"), ph.sem("split"), ph.sem("stored"), ph.chain_sem()
        blk = ph.block()

        @blk.sync
        def _(sp):
            ph.start(sp)
            sp.dma_start(om[:, :], io["omega"]).then_inc(loaded, 16)
            sp.dma_start(mk[:, :, :], io["memT"].rearrange("(a p) s -> p a s", p=P)).then_inc(loaded, 16)
            sp.wait_ge(split, 2 + START)
            store_stack(sp, io["omega_stack"], om_parts[:, :, :], RIGHT, stored)
            for a in range(n_tiles):
                store_stack(sp, io["mem_stack"][a * P:(a + 1) * P], mk_parts[:, :, a], RIGHT, stored)
            sp.wait_ge(stored, 16 * 3 * (1 + n_tiles) + START)

        @blk.vector
        def _(dve):
            chain = Chain(dve, chain_sem)
            dve.wait_ge(loaded, 32 + START)
            chain.link(nc.vector.tensor_scalar(om[:, :], om[:, :], HD ** -0.5, None, ALU.mult))
            for full, rest, parts in ((om[:, :], om_rest[:, :], [om_parts[:, i] for i in range(PARTS)]),
                                      (mk[:, :, :], mk_rest[:, :, :], [mk_parts[:, i] for i in range(PARTS)])):
                chain.link(nc.vector.tensor_copy(parts[0], full))
                chain.link(nc.vector.tensor_tensor(rest, full, parts[0], ALU.subtract))
                chain.link(nc.vector.tensor_copy(parts[1], rest))
                nc.vector.tensor_tensor(parts[2], rest, parts[1], ALU.subtract).then_inc(split, 1)


def project(nc, io, stage):
    xT, w_d, bT_d, bv_d = io[f"xT{stage}"], io[f"w{stage}"], io[f"bT{stage}"], io[f"bv{stage}"]
    stacks = ((io["q_stack"], LEFT), (io["k_stack"], LEFT if stage == 1 else RIGHT))
    v_out = io["v"]
    norms = stage == 1
    NS = 2 * CT
    with Phase(nc, f"pj{stage}") as ph:
        w = ph.sb("w", [P, CT, 3 * C])
        bias = ph.sb("bias", [P, 6])
        bias_v = ph.sb("bias_v", [P, C])
        x = ph.sb("x", [P, HALVES, CT, TILE])
        full = ph.sb("full", [P, 2, TILE])
        rest = ph.sb("rest", [P, 2, TILE])
        parts = ph.sb("parts", [P, NS, PARTS, TILE], BF16)
        v = ph.sb("v", [P, 2, TB, HEADS, V1])
        ps_qk = ph.ps("ps_qk", [P, 2, TILE])
        ps_v = ph.ps("ps_v", [P, TB, C])
        consts_in, chain_sem = ph.sem("consts_in"), ph.chain_sem()
        x_in = ph.sems("x_in", HALVES)
        qk_ps = ph.sem("qk_ps")
        v_ps = ph.sems("v_ps", HALVES)
        qk_full = ph.sems("qk_full", 2)
        qk_split = ph.sems("qk_split", 2)
        v_full = ph.sem("v_full")
        qk_out = ph.sems("qk_out", NS)
        v_out_sem = ph.sems("v_out", 2)
        if norms:
            squares = ph.sb("squares", [P, NS, TILE])
            select = ph.sb("select", [P, NS, 32])
            n_rest = ph.sb("n_rest", [32, TILE])
            n_parts = ph.sb("n_parts", [32, 2, PARTS, TILE], BF16)
            ps_n = ph.ps("ps_n", [32, TILE])
            squared, n_ps, n_split = ph.sem("squared"), ph.sem("n_ps"), ph.sem("n_split")
            n_out = ph.sems("n_out", 2)
        n_consts = 3 + norms
        blk = ph.block()

        @blk.sync
        def _(sp):
            ph.start(sp)
            sp.dma_start(w[:, :, :], w_d.rearrange("(a p) n -> p a n", p=P)).then_inc(consts_in, 16)
            sp.dma_start(bias[:, :], bT_d).then_inc(consts_in, 16)
            sp.dma_start(bias_v[:, :], bv_d).then_inc(consts_in, 16)
            if norms:
                sp.dma_start(select[:, :, :], io["select"]).then_inc(consts_in, 16)

            def load_x(b, half):
                sp.dma_start(x[:, half], xT[bass.ds(b * C, C), half * TILE:(half + 1) * TILE]
                             .rearrange("(a p) t -> p a t", p=P)).then_inc(x_in[half], 16)

            def batch_row(b, more):
                for half in range(HALVES):
                    cols = slice(half * TILE, (half + 1) * TILE)
                    for s in range(NS):
                        dst, order = stacks[s // CT]
                        sp.wait_ge(qk_split[s % 2], b * (HALVES * NS // 2) + half * (NS // 2) + s // 2 + 1 + START)
                        store_stack(sp, dst[bass.ds(b * C + (s % CT) * P, P), :, cols], parts[:, s], order, qk_out[s])
                    if more:
                        sp.wait_ge(v_ps[half], b + 1 + START)
                        load_x(b + 1, half)
                    sp.wait_ge(v_full, b * HALVES + half + 1 + START)
                    for t in range(TB):
                        rows = v_out.rearrange("(i t) w -> i t w", t=T)[bass.ds(b * QUADS, QUADS),
                                                                        half * TILE + t * P:half * TILE + (t + 1) * P]
                        sp.dma_start(rows.rearrange("g t w -> t g w"),
                                     v[:, half, t].rearrange("p (g h) d -> p g (h d)", g=QUADS)).then_inc(v_out_sem[half], 16)
                    if norms:
                        sp.wait_ge(n_split, b * HALVES + half + 1 + START)
                        sp.dma_start(io["norms"][:, bass.ds(b * 2 * HEADS, 2 * HEADS), cols].rearrange("n h t -> h n t"),
                                     n_parts[:, half]).then_inc(n_out[half], 16)

            for half in range(HALVES):
                load_x(0, half)
            with sp.Fori(0, B - 1) as b:
                batch_row(b, True)
            batch_row(B - 1, False)
            for s in range(NS):
                sp.wait_ge(qk_out[s], 48 * B * HALVES + START)
            for half in range(HALVES):
                sp.wait_ge(v_out_sem[half], 16 * TB * B + START)
                if norms:
                    sp.wait_ge(n_out[half], 16 * B + START)

        @blk.tensor
        def _(pe):
            pe.wait_ge(consts_in, 16 * n_consts + START)
            with pe.Fori(0, B) as b:
                for half in range(HALVES):
                    pe.wait_ge(x_in[half], b * 16 + 16 + START)
                    for s in range(NS):
                        pe.wait_ge(qk_full[s % 2], b * (HALVES * NS // 2) + half * (NS // 2) + s // 2 + START)
                        for a in range(CT):
                            last = nc.tensor.matmul(ps_qk[:, s % 2], w[:, a, s * P:(s + 1) * P], x[:, half, a],
                                                    start=a == 0, stop=a == CT - 1)
                        last.then_inc(qk_ps, 1)
                    pe.wait_ge(v_full, b * HALVES + half + START)
                    for t in range(TB):
                        for a in range(CT):
                            last = nc.tensor.matmul(ps_v[:, t], x[:, half, a, t * P:(t + 1) * P], w[:, a, 2 * C:3 * C],
                                                    start=a == 0, stop=a == CT - 1)
                    last.then_inc(v_ps[half], 1)
                    if norms:
                        pe.wait_ge(squared, b * (HALVES * NS) + (half + 1) * NS + START)
                        pe.wait_ge(n_split, b * HALVES + half + START)
                        for s in range(NS):
                            last = nc.tensor.matmul(ps_n[:, :], select[:, s], squares[:, s],
                                                    start=s == 0, stop=s == NS - 1)
                        last.then_inc(n_ps, 1)

        @blk.scalar
        def _(act):
            act.wait_ge(consts_in, 16 * n_consts + START)
            with act.Fori(0, B) as b:
                for half in range(HALVES):
                    if norms:
                        act.wait_ge(n_ps, b * HALVES + half + START)
                    for s in range(NS):
                        act.wait_ge(qk_ps, b * (HALVES * NS) + half * NS + s + 1 + START)
                        if norms:
                            nc.scalar.activation(squares[:, s], ps_qk[:, s % 2], ACT.Square,
                                                 bias=bias[:, s:s + 1]).then_inc(squared, 1)
                        use = b * (HALVES * NS // 2) + half * (NS // 2) + s // 2
                        act.wait_ge(qk_split[s % 2], use + START)
                        nc.scalar.activation(full[:, s % 2], ps_qk[:, s % 2], ACT.Identity,
                                             bias=bias[:, s:s + 1]).then_inc(qk_full[s % 2], 1)

        @blk.vector
        def _(dve):
            chain = Chain(dve, chain_sem)
            chain.link(nc.vector.memset(v[:, :, :, :, HD:V1], 1.0))
            dve.wait_ge(consts_in, 16 * n_consts + START)
            with dve.Fori(0, B) as b:
                chain.restart()
                for half in range(HALVES):
                    for s in range(NS):
                        use = b * (HALVES * NS // 2) + half * (NS // 2) + s // 2
                        dve.wait_ge(qk_full[s % 2], use + 1 + START)
                        dve.wait_ge(qk_out[s], (b * HALVES + half) * 48 + START)
                        chain.link(nc.vector.tensor_copy(parts[:, s, 0], full[:, s % 2]))
                        chain.link(nc.vector.tensor_tensor(rest[:, s % 2], full[:, s % 2], parts[:, s, 0], ALU.subtract))
                        chain.link(nc.vector.tensor_copy(parts[:, s, 1], rest[:, s % 2]))
                        nc.vector.tensor_tensor(parts[:, s, 2], rest[:, s % 2], parts[:, s, 1],
                                                ALU.subtract).then_inc(qk_split[s % 2], 1)
                    dve.wait_ge(v_ps[half], b + 1 + START)
                    dve.wait_ge(v_out_sem[half], b * (16 * TB) + START)
                    for t in range(TB):
                        last = nc.vector.tensor_tensor(v[:, half, t, :, 0:HD],
                                                       ps_v[:, t].rearrange("p (h d) -> p h d", d=HD),
                                                       bias_v[:, :].rearrange("p (h d) -> p h d", d=HD), ALU.add)
                    last.then_inc(v_full, 1)
                    if norms:
                        dve.wait_ge(n_ps, b * HALVES + half + 1 + START)
                        dve.wait_ge(n_out[half], b * 16 + START)
                        chain.link(nc.vector.tensor_copy(n_parts[:, half, 0], ps_n[:, :]))
                        chain.link(nc.vector.tensor_tensor(n_rest[:, :], ps_n[:, :], n_parts[:, half, 0], ALU.subtract))
                        chain.link(nc.vector.tensor_copy(n_parts[:, half, 1], n_rest[:, :]))
                        nc.vector.tensor_tensor(n_parts[:, half, 2], n_rest[:, :], n_parts[:, half, 1],
                                                ALU.subtract).then_inc(n_split, 1)


def stack_rows(stack, heads):
    return stack.rearrange("(h d) r t -> h (d r) t", d=HD)[heads].rearrange("h r t -> r h t")


def linear_attention(nc, io):
    PAIRS = NQ // 2
    with Phase(nc, "la") as ph:
        omega = ph.sb("omega", [STACK1, FEAT], BF16)
        cap = ph.sb("cap", [P, 4, P])
        ident = ph.sb("ident", [P, P])
        q = [ph.sb(f"q{i}", [STACK1, 4, T], BF16) for i in range(2)]
        k = [ph.sb(f"k{i}", [STACK1, 4, T], BF16) for i in range(2)]
        v = [ph.sb(f"v{i}", [P, BLOCKS, VW]) for i in range(2)]
        phi_kT = ph.sb("phi_kT", [P, 2, 4, P])
        phi_qT = ph.sb("phi_qT", [P, 2, 4, P])
        phi_k = ph.sb("phi_k", [P, 2, 4, FEAT])
        att = ph.sb("att", [P, 2, 4, P])
        stateT = ph.sb("stateT", [P, FEAT])
        state = ph.sb("state", [P, P])
        y = ph.sb("y", [P, 2, T])
        ps_kT, ps_qT, ps_k, ps_att = (ph.ps(n, [P, 4, P]) for n in ("ps_kT", "ps_qT", "ps_k", "ps_att"))
        ps_y = ph.ps("ps_y", [P, TILE])
        ps_stateT = ph.ps("ps_stateT", [P, TILE])
        ps_state = ph.ps("ps_state", [P, TILE])
        consts_in, cleared = ph.sem("consts_in"), ph.sem("cleared")
        landed = ph.sems("landed", 2)
        kT_ps, qT_ps, k_ps, att_ps, y_ps, stateT_ps, state_ps = (
            ph.sem(n) for n in ("kT_ps", "qT_ps", "k_ps", "att_ps", "y_ps", "stateT_ps", "state_ps"))
        kT_done, qT_done, k_done, att_done, stateT_done, state_done = (
            ph.sem(n) for n in ("kT_done", "qT_done", "k_done", "att_done", "stateT_done", "state_done"))
        y_done = ph.sems("y_done", 2)
        stored = ph.sems("stored", 2)
        LOADS = 5
        N_CONST = 3

        def step(kk, pr, c):
            return kk * (2 * BLOCKS) + pr * BLOCKS + c

        def state_step(kk, pr, c):
            return kk * (2 * (BLOCKS - 1)) + pr * (BLOCKS - 1) + c

        blk = ph.block()

        @blk.sync
        def _(sp):
            ph.start(sp)
            sp.dma_start(omega[0:STACK, :], io["omega_stack"].rearrange("d r m -> (d r) m")).then_inc(consts_in, 16)
            sp.dma_start(cap[:, :, :], io["cap"]).then_inc(consts_in, 16)
            sp.dma_start(ident[:, :], io["ident"]).then_inc(consts_in, 16)

            def load(kk, pr):
                heads = bass.ds(kk * 8 + pr * 4, 4)
                for side, (dst, stack) in enumerate(((q[pr], io["q_stack"]), (k[pr], io["k_stack"]))):
                    sp.dma_start(dst[0:STACK], stack_rows(stack, heads)).then_inc(landed[pr], 16)
                    sp.dma_start(dst[STACK:STACK1], io["norms"].rearrange("n (h s) t -> n h s t", s=2)[:, heads, side]).then_inc(landed[pr], 16)
                sp.dma_start(v[pr][:, :, :], io["v"][bass.ds(kk * (2 * T) + pr * T, T)]
                             .rearrange("(n p) w -> p n w", p=P)).then_inc(landed[pr], 16)

            def pair(kk, more):
                for pr in range(2):
                    sp.wait_ge(y_done[pr], kk * BLOCKS + BLOCKS + START)
                    sp.dma_start(io["y"][bass.ds(kk * (2 * P) + pr * P, P)], y[:, pr]).then_inc(stored[pr], 16)
                    if more:
                        load(kk + 1, pr)

            for pr in range(2):
                load(0, pr)
            with sp.Fori(0, PAIRS - 1) as kk:
                pair(kk, True)
            pair(PAIRS - 1, False)
            for pr in range(2):
                sp.wait_ge(stored[pr], PAIRS * 16 + START)

        @blk.tensor
        def _(pe):
            pe.wait_ge(consts_in, 16 * N_CONST + START)
            pe.wait_ge(cleared, 3 + START)

            def features(kk, pr, c):
                if c == 0:
                    pe.wait_ge(landed[pr], kk * (16 * LOADS) + 16 * LOADS + START)
                cols = slice(c * P, (c + 1) * P)
                pe.wait_ge(kT_done, step(kk, pr, c) + START)
                nc.tensor.matmul(ps_kT[:, :, :], omega[:, :], k[pr][:, :, cols],
                                 start=True, stop=True).then_inc(kT_ps, 1)
                pe.wait_ge(qT_done, step(kk, pr, c) + START)
                nc.tensor.matmul(ps_qT[:, :, :], omega[:, :], q[pr][:, :, cols],
                                 start=True, stop=True).then_inc(qT_ps, 1)
                if c < BLOCKS - 1:
                    pe.wait_ge(k_done, state_step(kk, pr, c) + START)
                    for j in range(4):
                        last = nc.tensor.matmul(ps_k[:, j], k[pr][:, j, cols], omega[:, :], start=True, stop=True)
                    last.then_inc(k_ps, 1)

            def quad(kk, pr, following):
                for c in range(BLOCKS):
                    d = c % 2
                    pe.wait_ge(kT_done, step(kk, pr, c) + 1 + START)
                    pe.wait_ge(qT_done, step(kk, pr, c) + 1 + START)
                    pe.wait_ge(att_done, step(kk, pr, c) + START)
                    for j in range(4):
                        last = nc.tensor.matmul(ps_att[:, j], phi_kT[:, d, j], phi_qT[:, d, j], start=True, stop=True)
                    last.then_inc(att_ps, 1)
                    if c < BLOCKS - 1:
                        features(kk, pr, c + 1)
                        pe.wait_ge(k_done, state_step(kk, pr, c) + 1 + START)
                        pe.wait_ge(stateT_done, state_step(kk, pr, c) + START)
                        for j in range(4):
                            last = nc.tensor.matmul(ps_stateT[32 * j:32 * j + V1, 0:FEAT],
                                                    v[pr][:, c, j * V1:(j + 1) * V1], phi_k[:, d, j],
                                                    start=c == 0, stop=True, skip_group_check=True)
                        last.then_inc(stateT_ps, 1)
                    elif following is not None:
                        features(*following, 0)
                    pe.wait_ge(att_done, step(kk, pr, c) + 1 + START)
                    if c > 0:
                        pe.wait_ge(y_done[pr], kk * BLOCKS + c + START)
                    else:
                        pe.wait_ge(y_done[1 - pr], kk * BLOCKS + pr * BLOCKS + START)
                    if c > 0:
                        pe.wait_ge(state_done, state_step(kk, pr, c - 1) + 1 + START)
                    for j in range(4):
                        last = nc.tensor.matmul(ps_y[32 * j:32 * j + V1, 0:P], v[pr][:, c, j * V1:(j + 1) * V1],
                                                att[:, d, j], start=True, stop=c == 0)
                    if c > 0:
                        for j in range(4):
                            last = nc.tensor.matmul(ps_y[32 * j:32 * j + V1, 0:P], state[:, 32 * j:32 * j + V1],
                                                    phi_qT[:, d, j], start=False, stop=True)
                    last.then_inc(y_ps, 1)
                    if c < BLOCKS - 1:
                        pe.wait_ge(stateT_done, state_step(kk, pr, c) + 1 + START)
                        pe.wait_ge(state_done, state_step(kk, pr, c) + START)
                        nc.tensor.transpose(ps_state[:, 0:P], stateT[:, :], ident[:, :]).then_inc(state_ps, 1)

            features(0, 0, 0)
            with pe.Fori(0, PAIRS - 1) as kk:
                quad(kk, 0, (kk, 1))
                quad(kk, 1, (kk + 1, 0))
            quad(PAIRS - 1, 0, (PAIRS - 1, 1))
            quad(PAIRS - 1, 1, None)

        @blk.scalar
        def _(act):
            def exps(kk, pr, c):
                d = c % 2
                act.wait_ge(kT_ps, step(kk, pr, c) + 1 + START)
                nc.scalar.activation(phi_kT[:, d], ps_kT[:, :, :], ACT.Exp).then_inc(kT_done, 1)
                act.wait_ge(qT_ps, step(kk, pr, c) + 1 + START)
                nc.scalar.activation(phi_qT[:, d], ps_qT[:, :, :], ACT.Exp).then_inc(qT_done, 1)

            def exp_k(kk, pr, c):
                act.wait_ge(k_ps, state_step(kk, pr, c) + 1 + START)
                nc.scalar.activation(phi_k[:, c % 2], ps_k[:, :, :], ACT.Exp).then_inc(k_done, 1)

            def quad(kk, pr, following):
                for c in range(BLOCKS - 1):
                    exps(kk, pr, c + 1)
                    act.wait_ge(stateT_ps, state_step(kk, pr, c) + 1 + START)
                    nc.scalar.activation(stateT[:, :], ps_stateT[:, 0:FEAT], ACT.Copy).then_inc(stateT_done, 1)
                    if c < BLOCKS - 2:
                        exp_k(kk, pr, c + 1)
                if following is not None:
                    exps(*following, 0)
                    exp_k(*following, 0)

            exps(0, 0, 0)
            exp_k(0, 0, 0)
            with act.Fori(0, PAIRS - 1) as kk:
                quad(kk, 0, (kk, 1))
                quad(kk, 1, (kk + 1, 0))
            quad(PAIRS - 1, 0, (PAIRS - 1, 1))
            quad(PAIRS - 1, 1, None)

        @blk.vector
        def _(dve):
            nc.vector.memset(omega[STACK:STACK1, :], 1.0).then_inc(cleared, 1)
            nc.vector.memset(ps_y[:, :], 0.0).then_inc(cleared, 1)
            nc.vector.memset(ps_stateT[:, :], 0.0).then_inc(cleared, 1)
            dve.wait_ge(consts_in, 16 * N_CONST + START)
            with dve.Fori(0, PAIRS) as kk:
                for pr in range(2):
                    dve.wait_ge(stored[pr], kk * 16 + START)
                    for c in range(BLOCKS):
                        dve.wait_ge(att_ps, step(kk, pr, c) + 1 + START)
                        nc.vector.tensor_tensor(att[:, c % 2], ps_att[:, :, :], cap[:, :, :], ALU.min).then_inc(att_done, 1)
                        dve.wait_ge(y_ps, step(kk, pr, c) + 1 + START)
                        nc.vector.tensor_copy(y[:, pr, c * P:(c + 1) * P], ps_y[:, 0:P]).then_inc(y_done[pr], 1)
                        if c < BLOCKS - 1:
                            dve.wait_ge(state_ps, state_step(kk, pr, c) + 1 + START)
                            nc.vector.tensor_copy(state[:, :], ps_state[:, 0:P]).then_inc(state_done, 1)


def layernorm_stats(nc, dve, chain, z, stats, moments, std):
    for t in range(TB):
        chain.link(nc.vector.bn_stats(stats[:, t], z[:, t])) if t == TB - 1 else nc.vector.bn_stats(stats[:, t], z[:, t])
    for t in range(TB):
        ins = nc.vector.bn_aggr(moments[:, t], stats[:, t])
    chain.link(ins)
    return nc.vector.tensor_scalar(std[:, :], moments[:, :, 1], LN_EPS, None, ALU.add)


def close_attention(nc, io, stage):
    x_d, xo_d, xT_d = io[f"x{stage}"], io[f"x{stage + 1}"], io[f"xT{stage + 1}"]
    eps = DEN_EPS * FEAT if stage == 1 else 0.0
    with Phase(nc, f"cl{stage}") as ph:
        w = ph.sb("w", [P, CT, C])
        bias = ph.sb("bias", [P, TB, C])
        ident = ph.sb("ident", [P, P])
        den = ph.sb("den", [P, T * B * HEADS // P])
        y = ph.sb("y", [P, HALVES, CT, TILE])
        inv = ph.sb("inv", [P, HALVES, CT, TILE])
        yn = ph.sb("yn", [P, HALVES, CT, TILE])
        x = ph.sb("x", [P, HALVES, TB, C])
        xb = ph.sb("xb", [P, HALVES, TB, C])
        z = ph.sb("z", [P, HALVES, TB, C])
        xn = ph.sb("xn", [P, HALVES, TB, C])
        xT = ph.sb("xT", [P, HALVES, CT, TILE])
        stats = ph.sb("stats", [P, TB, 6])
        moments = ph.sb("moments", [P, TB, 2])
        std = ph.sb("std", [P, TB])
        root = ph.sb("root", [P, TB])
        rstd = ph.sb("rstd", [P, TB])
        ps_o = ph.ps("ps_o", [P, HALVES, TB, C])
        ps_t = ph.ps("ps_t", [P, HALVES, CT, TILE])
        consts_in, chain_sem = ph.sem("consts_in"), ph.chain_sem()
        den_in, den_inv, inv_out = ph.sem("den_in"), ph.sem("den_inv"), ph.sem("inv_out")
        landed = ph.sems("landed", HALVES)
        scaled, biased, o_ps, var_ready, rooted = (
            ph.sem(n) for n in ("scaled", "biased", "o_ps", "var_ready", "rooted"))
        normed, t_ps, t_done = (ph.sems(n, HALVES) for n in ("normed", "t_ps", "t_done"))
        stored = ph.sems("stored", HALVES)
        LOADS = 5
        blk = ph.block()

        @blk.sync
        def _(sp):
            ph.start(sp)
            sp.dma_start(den[:, :], io["y"].rearrange("(h r) (s t) -> h r s t", r=32, s=2)[:, HD]).then_inc(den_in, 16)
            sp.dma_start(w[:, :, :], io[f"wo{stage}"].rearrange("(a p) n -> p a n", p=P)).then_inc(consts_in, 16)
            sp.dma_start(bias[:, :, :], io[f"bo{stage}"]).then_inc(consts_in, 16)
            sp.dma_start(ident[:, :], io["ident"]).then_inc(consts_in, 16)
            sp.wait_ge(den_inv, 1 + START)
            sp.dma_start(io["inv"].rearrange("h (s t) -> (h s) t", s=2), den[:, :]).then_inc(inv_out, 16)
            sp.wait_ge(inv_out, 16 + START)
            with sp.Fori(0, B) as b:
                for half in range(HALVES):
                    cols = slice(half * TILE, (half + 1) * TILE)
                    sp.wait_ge(t_ps[half], b + START)
                    for a in range(CT):
                        rows = io["y"].rearrange("(h r) t -> h r t", r=32)[bass.ds(b * HEADS + a * (HEADS // CT), HEADS // CT), 0:HD, cols]
                        sp.dma_start(y[:, half, a], rows).then_inc(landed[half], 16)
                        heads = io["inv"][bass.ds(b * HEADS + a * (HEADS // CT), HEADS // CT), cols]
                        sp.dma_start(inv[:, half, a], heads.unsqueeze(1).broadcast_to([HEADS // CT, HD, TILE])).then_inc(landed[half], 16)
                    sp.dma_start(x[:, half], x_d[bass.ds(b * T + half * TILE, TILE)]
                                 .rearrange("(n p) c -> p n c", p=P)).then_inc(landed[half], 16)

        @blk.gpsimd
        def _(pool):
            pool.wait_ge(consts_in, 48 + START)
            with pool.Fori(0, B) as b:
                for half in range(HALVES):
                    pool.wait_ge(landed[half], b * (16 * LOADS) + 16 * LOADS + START)
                    pool.wait_ge(t_ps[half], b + START)
                    nc.gpsimd.tensor_tensor(yn[:, half], y[:, half], inv[:, half], ALU.mult).then_inc(scaled, 1)
                    nc.gpsimd.tensor_tensor(xb[:, half], x[:, half], bias[:, :, :], ALU.add).then_inc(biased, 1)

        @blk.tensor
        def _(pe):
            pe.wait_ge(consts_in, 48 + START)
            with pe.Fori(0, B) as b:
                for half in range(HALVES):
                    n = b * HALVES + half
                    pe.wait_ge(scaled, n + 1 + START)
                    pe.wait_ge(normed[half], b + START)
                    for t in range(TB):
                        for a in range(CT):
                            last = nc.tensor.matmul(ps_o[:, half, t], yn[:, half, a, t * P:(t + 1) * P], w[:, a],
                                                    start=a == 0, stop=a == CT - 1)
                    last.then_inc(o_ps, 1)
                    pe.wait_ge(normed[half], b + 1 + START)
                    pe.wait_ge(t_done[half], b + START)
                    for a in range(CT):
                        for t in range(TB):
                            last = nc.tensor.transpose(ps_t[:, half, a, t * P:(t + 1) * P], xn[:, half, t, a * P:(a + 1) * P], ident[:, :])
                    last.then_inc(t_ps[half], 1)

        @blk.scalar
        def _(act):
            with act.Fori(0, B) as b:
                for half in range(HALVES):
                    n = b * HALVES + half
                    act.wait_ge(var_ready, n + 1 + START)
                    nc.scalar.activation(root[:, :], std[:, :], ACT.Sqrt).then_inc(rooted, 1)
                    act.wait_ge(normed[half], b + 1 + START)
                    act.dma_start(xo_d[bass.ds(b * T + half * TILE, TILE)].rearrange("(n p) c -> p n c", p=P),
                                  xn[:, half]).then_inc(stored[half], 16)
                    act.wait_ge(t_ps[half], b + 1 + START)
                    act.wait_ge(stored[half], b * 32 + START)
                    nc.scalar.activation(xT[:, half], ps_t[:, half], ACT.Copy).then_inc(t_done[half], 1)
                    act.wait_ge(t_done[half], b + 1 + START)
                    act.dma_start(xT_d[bass.ds(b * C, C), half * TILE:(half + 1) * TILE].rearrange("(a p) t -> p a t", p=P),
                                  xT[:, half]).then_inc(stored[half], 16)
            for half in range(HALVES):
                act.wait_ge(stored[half], 32 * B + START)

        @blk.vector
        def _(dve):
            chain = Chain(dve, chain_sem)
            dve.wait_ge(den_in, 16 + START)
            if eps:
                chain.link(nc.vector.tensor_scalar(den[:, :], den[:, :], eps, None, ALU.add))
            nc.vector.reciprocal(den[:, :], den[:, :]).then_inc(den_inv, 1)
            dve.wait_ge(den_inv, 1 + START)
            with dve.Fori(0, B) as b:
                chain.restart()
                for half in range(HALVES):
                    n = b * HALVES + half
                    dve.wait_ge(o_ps, n + 1 + START)
                    dve.wait_ge(biased, n + 1 + START)
                    for t in range(0, TB, 2):
                        ins = nc.vector.tensor_tensor(z[:, half, t:t + 2], ps_o[:, half, t:t + 2], xb[:, half, t:t + 2], ALU.add)
                    chain.link(ins)
                    layernorm_stats(nc, dve, chain, z[:, half], stats, moments, std).then_inc(var_ready, 1)
                    dve.wait_ge(rooted, n + 1 + START)
                    chain.link(nc.vector.reciprocal(rstd[:, :], root[:, :]))
                    dve.wait_ge(stored[half], b * 32 + START)
                    for t in range(TB):
                        ins = nc.vector.tensor_scalar(xn[:, half, t], z[:, half, t], moments[:, t, 0:1], rstd[:, t:t + 1],
                                                      ALU.subtract, ALU.mult)
                    ins.then_inc(normed[half], 1)
                    dve.wait_ge(normed[half], b + 1 + START)


KEY_BLOCKS = TILE // P


def score_groups():
    groups, unit = [], 0
    for half in range(HALVES):
        groups.append((half, "rest", None, 0, [unit]))
        unit += 1
        groups.append((half, "memory", None, 0, [unit, unit + 1]))
        unit += 2
        for blk in range((half + 1) * KEY_BLOCKS):
            groups.append((half, "causal", blk, max(0, blk - half * KEY_BLOCKS) * P, [unit, unit + 1]))
            unit += 2
    return groups, unit


GROUPS_OF_QUAD, UNITS = score_groups()
DIAGONALS = 2 * BLOCKS
BANK = 512
MAX_PIECES = [(j, t, n, n * BANK, min(MEM + (t + 1) * P, (n + 1) * BANK))
              for t in range(BLOCKS) for j in range(4) for n in range(-(-(MEM + (t + 1) * P) // BANK))]
PIECES = len(MAX_PIECES)
PIECE_SLOTS = 3

MAX_BANKS = 3
START_PIECES = 5
TURN_BANK = START_PIECES % MAX_BANKS


def piece_banks():
    places, used = [], [0] * MAX_BANKS
    for m in range(PIECES):
        bank = (m + (m >= START_PIECES)) % MAX_BANKS
        places.append((bank, used[bank]))
        used[bank] += 1
    return places, used


PIECE_BANK, BANK_USES = piece_banks()
AFTER_TURN = [m for m in range(START_PIECES, PIECES) if PIECE_BANK[m][0] == TURN_BANK][0]


def pieces_between(lead):
    steps = []
    for half, kind, kb, first, units in GROUPS_OF_QUAD:
        steps += [2 * (TILE - first)] * len(units) + [4 * (TILE - first) if kind != "rest" else 2 * TILE]
    reduction = [64 + hi - lo for _, _, _, lo, hi in MAX_PIECES]
    order = [reduction[(lead + i) % PIECES] for i in range(PIECES)]
    through, at, done, total = [], 0, 0, sum(order)
    for n, cost in enumerate(steps):
        at += cost
        while done < PIECES and sum(order[:done + 1]) <= total * at / sum(steps):
            done += 1
        through.append(done)
    through[-1] = PIECES
    return through


LAG = 2
PROB_SLOTS = 2 * (LAG + 1)


def prob_slot(g, u):
    return (g * UNITS + u) % PROB_SLOTS


def softmax_attention(nc, io):
    SLOTS = QUADS
    with Phase(nc, "sa") as ph:
        ident = ph.sb("ident", [P, P])
        eye = ph.sb("eye", [P, P], BF16)
        later_f = ph.sb("later_f", [P, P])
        later = ph.sb("later", [P, P], BF16)
        q = [ph.sb(f"q{i}", [STACK1, 4, T], BF16) for i in range(SLOTS)]
        k = [ph.sb(f"k{i}", [STACK1, 4, T], BF16) for i in range(SLOTS)]
        km = [ph.sb(f"km{i}", [STACK1, 4, MEMW], BF16) for i in range(SLOTS)]
        v = [ph.sb(f"v{i}", [P, BLOCKS, VW]) for i in range(SLOTS)]
        vm = [ph.sb(f"vm{i}", [P, VW + P]) for i in range(SLOTS)]
        prob = ph.sb("prob", [P, PROB_SLOTS, 2, TILE])
        y = ph.sb("y", [P, 2, T])
        piece_max = ph.sb("piece_max", [P, 4, BLOCKS, PIECE_SLOTS])
        neg_max = ph.sb("neg_max", [P, 4 * BLOCKS])
        max_rest = ph.sb("max_rest", [4 * BLOCKS, P])
        max_parts = ph.sb("max_parts", [4 * BLOCKS, 2, PARTS, P], BF16)
        ps_s = ph.ps("ps_s", [P, 2, 2, TILE])
        ps_m = ph.ps("ps_m", [P, MAX_BANKS, BANK])
        ps_y = ph.ps("ps_y", [P, TILE])
        turned = ps_m[0:4 * BLOCKS, TURN_BANK, 0:P]
        consts_in, cleared, chain_sem = ph.sem("consts_in"), ph.sem("cleared"), ph.chain_sem()
        landed, max_in, stored = ph.sems("landed", SLOTS), ph.sems("max_in", SLOTS), ph.sems("stored", 2)
        scored = ph.sem("scored")
        expd = ph.sems("expd", 2)
        masked, summed = ph.sem("masked"), ph.sem("summed")
        turn = ph.sem("turn")
        y_done = ph.sem("y_done")
        piece_ps, piece_done = ph.sem("piece_ps"), ph.sems("piece_done", MAX_BANKS)
        max_done, max_ps, max_split = ph.sem("max_done"), ph.sem("max_ps"), ph.sem("max_split")
        LOADS = 5
        LEAD = 16

        def quad_before(b, g):
            return b * QUADS + g

        def after(b, g, n=1):
            nb, ng = b + (g + n) // QUADS, (g + n) % QUADS
            return None if isinstance(nb, int) and nb >= B else (nb, ng)

        blk = ph.block()

        @blk.sync
        def _(sp):
            ph.start(sp)
            for dst, name in ((ident, "ident"), (later_f, "later")):
                sp.dma_start(dst[:, :], io[name]).then_inc(consts_in, 16)

            def load(b, g):
                heads = bass.ds(b * HEADS + g * 4, 4)
                sp.dma_start(q[g][0:STACK], stack_rows(io["q_stack"], heads)).then_inc(landed[g], 16)
                sp.dma_start(k[g][0:STACK], stack_rows(io["k_stack"], heads)).then_inc(landed[g], 16)
                sp.dma_start(km[g][0:STACK, :, 0:MEM], stack_rows(io["mem_stack"], heads)).then_inc(landed[g], 16)
                sp.dma_start(v[g][:, :, :], io["v"][bass.ds(b * (QUADS * T) + g * T, T)]
                             .rearrange("(n p) w -> p n w", p=P)).then_inc(landed[g], 16)
                sp.dma_start(vm[g][:, :], io["mem"][bass.ds(b * (QUADS * P) + g * P, P)]).then_inc(landed[g], 16)

            def maxima(b, g):
                sp.wait_ge(max_split, quad_before(b, g) + 1 + START)
                for part in range(PARTS):
                    sp.dma_start(q[g][STACK + part:STACK + part + 1].rearrange("a h t -> a (h t)"),
                                 max_parts[:, g % 2, part]).then_inc(max_in[g], 16)

            def batch_row(b, last):
                for g in range(QUADS):
                    if not (last and g == QUADS - 1):
                        maxima(*after(b, g))
                    sp.wait_ge(y_done, (quad_before(b, g) + 1) * HALVES + START)
                    sp.dma_start(io["y"][bass.ds(b * (QUADS * P) + g * P, P)], y[:, g % 2]).then_inc(stored[g % 2], 16)
                    if not last:
                        load(b + 1, g)

            for g in range(QUADS):
                sp.wait_ge(cleared, g + 1 + (g > 0) + START)
                load(0, g)
            maxima(0, 0)
            with sp.Fori(0, B - 1) as b:
                batch_row(b, False)
            batch_row(B - 1, True)
            for pr in range(2):
                sp.wait_ge(stored[pr], NQ // 2 * 16 + START)

        @blk.tensor
        def _(pe):
            pe.wait_ge(consts_in, 32 + START)
            pe.wait_ge(cleared, 2 + START)

            def piece(b, g, m):
                j, t, _, lo, hi = MAX_PIECES[m]
                s, before = PIECE_BANK[m]
                if m == 0:
                    pe.wait_ge(landed[g], b * (16 * LOADS) + 16 * LOADS + START)
                qs = q[g][0:STACK, j, t * P:(t + 1) * P]
                pe.wait_ge(piece_done[s], quad_before(b, g) * BANK_USES[s] + before + START)
                if m == AFTER_TURN:
                    pe.wait_ge(max_split, quad_before(b, g) + START)
                if lo == 0:
                    nc.tensor.matmul(ps_m[:, s, 0:MEM], qs, km[g][0:STACK, j, 0:MEM], start=True, stop=True, skip_group_check=True)
                a = max(lo, MEM)
                last = nc.tensor.matmul(ps_m[:, s, a - lo:hi - lo], qs, k[g][0:STACK, j, a - MEM:hi - MEM],
                                        start=lo > 0, stop=True, skip_group_check=True)
                a, e = max(lo, MEM + t * P), hi
                if a < e:
                    first = MEM + t * P
                    last = nc.tensor.matmul(ps_m[:, s, a - lo:e - lo], eye[:, :], later[:, a - first:e - first],
                                            start=False, stop=True, skip_group_check=True)
                last.then_inc(piece_ps, 1)

            def turn_maxima(b, g):
                pe.wait_ge(max_done, quad_before(b, g) + 1 + START)
                if after(b, g) is not None:
                    pe.wait_ge(piece_done[TURN_BANK], (quad_before(b, g) + 1) * BANK_USES[TURN_BANK]
                               + PIECE_BANK[AFTER_TURN][1] + START)
                nc.tensor.transpose(turned, neg_max[:, :], ident[:, :]).then_inc(max_ps, 1)

            def scores(b, g, group, u):
                half, kind, kb, first, units = group
                s = u % 2
                pe.wait_ge(expd[s], quad_before(b, g) * (UNITS // 2) + u // 2 + START)
                queries = slice(half * TILE + first, (half + 1) * TILE)
                if kind == "rest":
                    for j in range(4):
                        last = nc.tensor.matmul(ps_s[32 * j:32 * j + 32, s, 0], km[g][:, j, P:MEMW], q[g][:, j, queries],
                                                start=True, stop=True)
                else:
                    for jj in range(2):
                        j = 2 * (u - units[0]) + jj
                        keys = km[g][:, j, 0:P] if kind == "memory" else k[g][:, j, kb * P:(kb + 1) * P]
                        last = nc.tensor.matmul(ps_s[:, s, jj, 0:TILE - first], keys, q[g][:, j, queries], start=True, stop=True)
                last.then_inc(scored, 1)

            def sums(b, g, group, n_masked, finish):
                half, kind, kb, first, units = group
                for u in units:
                    pe.wait_ge(expd[u % 2], quad_before(b, g) * (UNITS // 2) + u // 2 + 1 + START)
                if n_masked:
                    pe.wait_ge(masked, quad_before(b, g) * DIAGONALS + n_masked + START)
                if kind == "rest":
                    pe.wait_ge(y_done, quad_before(b, g) * HALVES + half + START)
                    last = nc.tensor.matmul(ps_y[:, :], vm[g][:, VW:VW + P], prob[:, prob_slot(g, units[0]), 0],
                                            start=True, stop=True, skip_group_check=True)
                else:
                    for j in range(4):
                        values = vm[g][:, j * V1:(j + 1) * V1] if kind == "memory" else v[g][:, kb, j * V1:(j + 1) * V1]
                        last = nc.tensor.matmul(ps_y[32 * j:32 * j + V1, first:TILE], values,
                                                prob[:, prob_slot(g, units[j // 2]), j % 2, 0:TILE - first],
                                                start=False, stop=True, skip_group_check=True)
                if finish:
                    last.then_inc(summed, 1)

            def batch_row(b):
                waiting, done = [], LEAD

                def pieces(g, step):
                    nonlocal done
                    until = LEAD + g * PIECES + through[step]
                    while done < until:
                        if done % PIECES == START_PIECES and after(b, 0, done // PIECES) is not None:
                            turn_maxima(*after(b, 0, done // PIECES))
                        if after(b, 0, 1 + done // PIECES) is not None:
                            piece(*after(b, 0, 1 + done // PIECES), done % PIECES)
                        done += 1

                def next_sums(g, step):
                    sums(b, *waiting.pop(0))
                    pieces(g, step)

                for g in range(QUADS):
                    pe.wait_ge(max_in[g], b * (16 * PARTS) + 16 * PARTS + START)
                    step, n_masked = 0, 0
                    for n, group in enumerate(GROUPS_OF_QUAD):
                        for u in group[4]:
                            scores(b, g, group, u)
                            pieces(g, step)
                            step += 1
                        if len(waiting) == LAG:
                            next_sums(g, step)
                        step += 1
                        diagonal = group[1] == "causal" and group[2] >= group[0] * KEY_BLOCKS
                        n_masked += 2 * diagonal
                        end = n + 1 == len(GROUPS_OF_QUAD) or GROUPS_OF_QUAD[n + 1][1] == "rest"
                        waiting.append((g, group, n_masked if diagonal else 0, end))
                while waiting:
                    next_sums(QUADS - 1, step - 1)

            through = pieces_between(LEAD)
            for m in range(PIECES + LEAD):
                if m == PIECES + START_PIECES:
                    turn_maxima(0, 0)
                piece(0, m // PIECES, m % PIECES)
            with pe.Fori(0, B - 1) as b:
                batch_row(b)
            batch_row(B - 1)

        @blk.scalar
        def _(act):
            def copy_half(b, g, half):
                act.wait_ge(summed, quad_before(b, g) * HALVES + half + 1 + START)
                act.wait_ge(stored[g % 2], b * (QUADS // 2 * 16) + g // 2 * 16 + START)
                nc.scalar.activation(y[:, g % 2, half * TILE:(half + 1) * TILE], ps_y[:, :], ACT.Copy).then_inc(y_done, 1)

            with act.Fori(0, B) as b:
                for g in range(QUADS):
                    for half, kind, kb, first, units in GROUPS_OF_QUAD:
                        for u in units:
                            s, slot = u % 2, prob_slot(g, u)
                            act.wait_ge(scored, quad_before(b, g) * UNITS + u + 1 + START)
                            if kind == "rest":
                                src, dst = ps_s[:, s, 0], prob[:, slot, 0]
                            else:
                                src, dst = ps_s[:, s, :, 0:TILE - first], prob[:, slot, :, 0:TILE - first]
                            nc.scalar.activation(dst, src, ACT.Exp, scale=HD ** -0.5).then_inc(expd[s], 1)
                        if kind == "memory" and half == 1:
                            copy_half(b, g, 0)
                        if kind == "memory" and half == 0 and g > 0:
                            copy_half(b, g - 1, 1)
                copy_half(b, QUADS - 1, 1)

        @blk.gpsimd
        def _(pool):
            with pool.Fori(0, B) as b:
                for g in range(QUADS):
                    for half, kind, kb, first, units in GROUPS_OF_QUAD:
                        if kind == "causal" and kb >= half * KEY_BLOCKS:
                            for u in units:
                                pool.wait_ge(expd[u % 2], quad_before(b, g) * (UNITS // 2) + u // 2 + 1 + START)
                                pool.sem_inc(turn, 1)
                                square = prob[:, prob_slot(g, u), :, 0:P]
                                nc.gpsimd.affine_select(out=square, in_=square, compare_op=ALU.is_ge, fill=0.0, base=0,
                                                        pattern=[[0, 2], [1, P]], channel_multiplier=-1).then_inc(masked, 1)

        @blk.vector
        def _(dve):
            chain = Chain(dve, chain_sem)
            chain.link(nc.vector.memset(piece_max[:, :, :, :], -BIG))
            nc.vector.memset(ps_y[:, :], 0.0)
            for i in range(SLOTS):
                chain.link(nc.vector.memset(km[i][:, :, :], 0.0))
                nc.vector.memset(km[i][STACK:STACK1, :, 0:MEM], 1.0)
                nc.vector.memset(k[i][STACK:STACK1, :, :], 1.0).then_inc(cleared, 1)
                if i == 0:
                    dve.wait_ge(consts_in, 32 + START)
                    nc.vector.tensor_copy(eye[:, :], ident[:, :])
                    nc.vector.tensor_copy(later[:, :], later_f[:, :]).then_inc(cleared, 1)

            FIRST_PIECES = START_PIECES + 1

            def reduce_pieces(b, g, first, end):
                for m in range(first, end):
                    j, t, n, lo, hi = MAX_PIECES[m]
                    dve.wait_ge(piece_ps, quad_before(b, g) * PIECES + m + 1 + START)
                    s = PIECE_BANK[m][0]
                    nc.vector.tensor_reduce(piece_max[:, j, t, n:n + 1], ps_m[:, s, 0:hi - lo], AX.X, ALU.max).then_inc(piece_done[s], 1)

            def quad(b, g):
                reduce_pieces(b, g, FIRST_PIECES, PIECES)
                for s in range(MAX_BANKS):
                    dve.wait_ge(piece_done[s], (quad_before(b, g) + 1) * BANK_USES[s] + START)
                nc.vector.tensor_reduce(neg_max[:, :], piece_max[:, :, :, :].rearrange("p h t n -> p (h t) n"),
                                        AX.X, ALU.max, negate=True).then_inc(max_done, 1)
                if after(b, g) is not None:
                    dve.wait_ge(max_done, quad_before(b, g) + 1 + START)
                    reduce_pieces(*after(b, g), 0, FIRST_PIECES)
                dve.wait_ge(max_ps, quad_before(b, g) + 1 + START)
                if g < 2:
                    dve.wait_ge(max_in[g + 2], b * (16 * PARTS) + START)
                else:
                    dve.wait_ge(max_in[g - 2], b * (16 * PARTS) + 16 * PARTS + START)
                to = max_parts[:, g % 2]
                chain.link(nc.vector.tensor_copy(to[:, 0], turned))
                chain.link(nc.vector.tensor_tensor(max_rest[:, :], turned, to[:, 0], ALU.subtract))
                chain.link(nc.vector.tensor_copy(to[:, 1], max_rest[:, :]))
                nc.vector.tensor_tensor(to[:, 2], max_rest[:, :], to[:, 1], ALU.subtract).then_inc(max_split, 1)

            reduce_pieces(0, 0, 0, FIRST_PIECES)
            with dve.Fori(0, B - 1) as b:
                chain.restart()
                for g in range(QUADS):
                    quad(b, g)
            chain.restart()
            for g in range(QUADS):
                quad(B - 1, g)


EXPERT_W = 2 * C + C


def experts(nc, io):
    NT = B * HALVES
    ALLB = NT * TB
    W_SLOTS = 3
    H_SLOTS = 3
    SUMS = EXPERTS + 1
    UP, DOWN = C, 2 * C
    with Phase(nc, "mo") as ph:
        w = ph.sb("w", [P, W_SLOTS, EXPERT_W])
        w_hi, w_lo = ph.sb("w_hi", [P, ALL_EXPERTS, EXPERT_W], F32R), ph.sb("w_lo", [P, ALL_EXPERTS, EXPERT_W], F32R)
        router = ph.sb("router", [P, CT, 32])
        ident = ph.sb("ident", [P, P])
        e_bias = ph.sb("e_bias", [P, ALLB, EXPERTS])
        xT = ph.sb("xT", [P, HALVES, CT, TILE])
        x_hi, x_lo = ph.sb("x_hi", [P, HALVES, CT, TILE], F32R), ph.sb("x_lo", [P, HALVES, CT, TILE], F32R)
        x = ph.sb("x", [P, HALVES, TB, C])
        comb = ph.sb("comb", [P, HALVES, TB, EXPERTS])
        silu = ph.sb("silu", [P, 2, TILE])
        h = ph.sb("h", [P, 2, TILE])
        h_hi, h_lo = ph.sb("h_hi", [P, H_SLOTS, TILE], F32R), ph.sb("h_lo", [P, H_SLOTS, TILE], F32R)
        acc = ph.sb("acc", [P, TB, C])
        stats, moments = ph.sb("stats", [P, TB, 6]), ph.sb("moments", [P, TB, 2])
        var, power, rstd = (ph.sb(n, [P, TB]) for n in ("var", "power", "rstd"))
        score, biased, keep, equal, equal_kept = (ph.sb(n, [P, ALLB, EXPERTS]) for n in ("score", "biased", "keep", "equal", "equal_kept"))
        up_to = [ph.sb(f"up_to{i}", [P, ALLB, EXPERTS]) for i in range(2)]
        largest = ph.sb("largest", [P, ALLB, 8])
        pair_hi, pair_lo = ph.sb("pair_hi", [P, ALLB, GROUPS, 2]), ph.sb("pair_lo", [P, ALLB, GROUPS, 2])
        g1, g2, g3, gsum, grank, gge = (ph.sb(n, [P, ALLB, GROUPS]) for n in ("g1", "g2", "g3", "gsum", "grank", "gge"))
        wsum = ph.sb("wsum", [P, ALLB])
        ps_g, ps_u = ph.ps("ps_g", [P, 2, TILE]), ph.ps("ps_u", [P, 2, TILE])
        ps_o = ph.ps("ps_o", [P, 2, TB, C])
        logit = ps_o[:, 0].rearrange("p t c -> p (t c)").rearrange("p (g t) -> p g t", t=TILE)
        scoreT = silu
        score_ps = ps_o[:, 1].rearrange("p t c -> p (t c)").rearrange("p (g t j e) -> p g j t e", t=TB, j=4, e=32)
        consts_in, chain_sem, power_set = ph.sem("consts_in"), ph.chain_sem(), ph.sem("power_set")
        w_in, w_hi_done, w_split = ph.sems("w_in", W_SLOTS), ph.sem("w_hi_done"), ph.sem("w_split")
        router_in = ph.sems("router_in", NT // 4)
        xT_in, x_hi_done, x_split = ph.sems("xT_in", HALVES), ph.sem("x_hi_done"), ph.sems("x_split", HALVES)
        logits, sigmoid, turned, scored, routed, comb_out = (ph.sem(n) for n in ("logits", "sigmoid", "turned", "scored", "routed", "comb_out"))
        landed = ph.sems("landed", HALVES)
        turn = ph.sem("turn")
        g_ps, u_ps, silu_done, multiplied = (ph.sem(n) for n in ("g_ps", "u_ps", "silu_done", "multiplied"))
        h_hi_done, h_split, o_ps, added = (ph.sem(n) for n in ("h_hi_done", "h_split", "o_ps", "added"))
        var_ready, rooted = ph.sem("var_ready"), ph.sem("rooted")
        normed, stored = ph.sems("normed", HALVES), ph.sems("stored", HALVES)
        blk = ph.block()

        def tile(b, half):
            return b * HALVES + half

        X_SPLIT_AT = (0, ALL_EXPERTS - 4)

        ROUTED_AT = 8

        def router_x(b, half):
            if b == 0:
                return xT[:, half]
            end = ALL_EXPERTS * EXPERT_W - (tile(b, half) - HALVES) * CT * TILE
            return (w_hi[:, :, :].rearrange("p e c -> p (e c)")[:, end - CT * TILE:end].bitcast(F32)
                    .rearrange("p (a t) -> p a t", a=CT))

        @blk.sync
        def _(sp):
            ph.start(sp)
            sp.dma_start(router[:, :, :], io["router"].rearrange("(a p) e -> p a e", p=P)).then_inc(router_in[0], 16)

            def load_xT(b, half, to, sem):
                sp.dma_start(to, io["xT3"][bass.ds(b * C, C), half * TILE:(half + 1) * TILE]
                             .rearrange("(a p) t -> p a t", p=P)).then_inc(sem, 16)

            def load_rows(b, half):
                rows = bass.ds(b * T + half * TILE, TILE)
                sp.dma_start(x[:, half], io["x3"][rows].rearrange("(n p) c -> p n c", p=P)).then_inc(landed[half], 16)
                sp.dma_start(comb[:, half], io["combine"][rows].rearrange("(n p) e -> p n e", p=P)).then_inc(landed[half], 16)

            for b in range(B):
                for half in range(HALVES):
                    load_xT(b, half, router_x(b, half), router_in[b // 2] if b else xT_in[half])
            sp.dma_start(ident[:, :], io["ident"]).then_inc(consts_in, 16)
            for to, name in ((e_bias, "e_bias"), (grank, "grank0")):
                sp.dma_start(to[:, :, :], io[name]).then_inc(consts_in, 16)
            for e in range(ALL_EXPERTS):
                if e == ROUTED_AT:
                    sp.wait_ge(routed, 1 + START)
                    sp.dma_start(io["combine"].rearrange("(n p) e -> p n e", p=P), keep[:, :, :]).then_inc(comb_out, 16)
                    sp.wait_ge(comb_out, 16 + START)
                    for half in range(HALVES):
                        load_rows(0, half)
                if e >= W_SLOTS:
                    sp.wait_ge(w_split, e - W_SLOTS + 1 + START)
                sp.dma_start(w[:, e % W_SLOTS], io["experts"][:, e]).then_inc(w_in[e % W_SLOTS], 16)

            def batch_row(b, more):
                for half in range(HALVES):
                    if more:
                        sp.wait_ge(x_split[half], b + 1 + START)
                        load_xT(b + 1, half, xT[:, half], xT_in[half])
                    sp.wait_ge(normed[half], b + 1 + START)
                    sp.dma_start(io["out"][bass.ds(b * T + half * TILE, TILE)].rearrange("(n p) c -> p n c", p=P),
                                 x[:, half]).then_inc(stored[half], 16)
                    if more:
                        sp.wait_ge(stored[half], b * 16 + 16 + START)
                        load_rows(b + 1, half)

            with sp.Fori(0, B - 1) as b:
                batch_row(b, True)
            batch_row(B - 1, False)
            for half in range(HALVES):
                sp.wait_ge(stored[half], 16 * B + START)

        @blk.tensor
        def _(pe):
            for half in range(HALVES):
                pe.wait_ge(xT_in[half], 16 + START)
            for group in range(NT // 4):
                pe.wait_ge(router_in[group], (48, 64)[group] + START)
                for a in range(CT):
                    for j in range(4):
                        n = 4 * group + j
                        last = nc.tensor.matmul(logit[32 * j:32 * j + 32, group], router[:, a], router_x(n // HALVES, n % HALVES)[:, a],
                                                start=a == 0, stop=a == CT - 1, skip_group_check=True)
                last.then_inc(logits, 1)
            pe.wait_ge(consts_in, 48 + START)
            for group in range(NT // 4):
                pe.wait_ge(sigmoid, group + 1 + START)
                for t in range(TB):
                    last = nc.tensor.transpose(ps_o[:, 1].rearrange("p t c -> p (t c)")[:, (group * TB + t) * P:(group * TB + t + 1) * P],
                                               scoreT[:, group, t * P:(t + 1) * P], ident[:, :])
                last.then_inc(turned, 1)
            pe.wait_ge(scored, 1 + START)

            def three_passes(out, left_hi, left_lo, right_hi, right_lo, start, stop):
                nc.tensor.matmul(out, left_hi, right_lo, start=start, stop=False)
                nc.tensor.matmul(out, left_lo, right_hi, start=False, stop=False)
                return nc.tensor.matmul(out, left_hi, right_hi, start=False, stop=stop)

            with pe.Fori(0, B) as b:
                for half in range(HALVES):
                    n = tile(b, half)

                    def gate_up(e):
                        s = e % 2
                        pe.wait_ge(w_split, e + 1 + START)
                        pe.wait_ge(multiplied, n * ALL_EXPERTS + max(0, e - 1) + START)
                        for first, ps, ready in ((0, ps_g, g_ps), (UP, ps_u, u_ps)):
                            for a in range(CT):
                                cols = slice(first + a * INNER, first + (a + 1) * INNER)
                                last = three_passes(ps[:, s], w_hi[:, e, cols], w_lo[:, e, cols], x_hi[:, half, a], x_lo[:, half, a],
                                                    start=a == 0, stop=a == CT - 1)
                            last.then_inc(ready, 1)

                    def project_down(es, i):
                        s = i % 2
                        pe.wait_ge(h_split, n * ALL_EXPERTS + es[-1] + 1 + START)
                        pe.wait_ge(added, n * SUMS + max(0, i - 1) + START)
                        for t in range(TB):
                            for e in es:
                                tokens = slice(t * P, (t + 1) * P)
                                last = three_passes(ps_o[:, s, t], h_hi[:, e % H_SLOTS, tokens], h_lo[:, e % H_SLOTS, tokens],
                                                    w_hi[:, e, DOWN:EXPERT_W], w_lo[:, e, DOWN:EXPERT_W],
                                                    start=e == es[0], stop=e == es[-1])
                        last.then_inc(o_ps, 1)

                    pe.wait_ge(x_split[half], b + 1 + START)
                    for e in range(SHARED + 1):
                        gate_up(e)
                    project_down(range(SHARED), 0)
                    gate_up(SHARED + 1)
                    for e in range(SHARED, ALL_EXPERTS):
                        if e + 2 < ALL_EXPERTS:
                            gate_up(e + 2)
                        project_down((e,), e - 1)

        @blk.scalar
        def _(act):
            for group in range(NT // 4):
                act.wait_ge(logits, group + 1 + START)
                nc.scalar.activation(scoreT[:, group], logit[:, group], ACT.Sigmoid).then_inc(sigmoid, 1)
            with act.Fori(0, B) as b:
                for half in range(HALVES):
                    for e in range(ALL_EXPERTS):
                        count = tile(b, half) * ALL_EXPERTS + e + 1 + START
                        act.wait_ge(g_ps, count)
                        nc.scalar.activation(silu[:, e % 2], ps_g[:, e % 2], ACT.Silu).then_inc(silu_done, 1)
                        act.wait_ge(multiplied, count)
                        nc.scalar.activation(h_hi[:, e % H_SLOTS], h[:, e % 2], ACT.Copy).then_inc(h_hi_done, 1)

        @blk.gpsimd
        def _(pool):
            nc.gpsimd.memset(power[:, :], -0.5).then_inc(power_set, 1)

            def split_x(n, half):
                nc.gpsimd.tensor_copy(x_hi[:, half], xT[:, half]).then_inc(x_hi_done, 1)
                pool.wait_ge(x_hi_done, n + 1 + START)
                pool.sem_inc(turn, 1)
                nc.gpsimd.tensor_tensor(x_lo[:, half], xT[:, half], x_hi[:, half].bitcast(F32), ALU.subtract).then_inc(x_split[half], 1)

            def root(n):
                pool.wait_ge(var_ready, n + 1 + START)
                pool.sem_inc(turn, 1)
                nc.gpsimd.tensor_tensor(rstd[:, :], var[:, :], power[:, :], ALU.pow).then_inc(rooted, 1)

            for e in range(ALL_EXPERTS):
                if e in X_SPLIT_AT:
                    half = X_SPLIT_AT.index(e)
                    pool.wait_ge(xT_in[half], 16 + START)
                    split_x(tile(0, half), half)
                pool.wait_ge(w_in[e % W_SLOTS], 16 * (e // W_SLOTS + 1) + START)
                if e == ALL_EXPERTS // 2:
                    pool.wait_ge(logits, NT // 4 + START)
                nc.gpsimd.tensor_copy(w_hi[:, e], w[:, e % W_SLOTS]).then_inc(w_hi_done, 1)
                pool.wait_ge(w_hi_done, e + 1 + START)
                nc.gpsimd.tensor_tensor(w_lo[:, e], w[:, e % W_SLOTS], w_hi[:, e].bitcast(F32), ALU.subtract).then_inc(w_split, 1)
            pool.wait_ge(power_set, 1 + START)
            with pool.Fori(0, B - 1) as b:
                for half in range(HALVES):
                    root(tile(b, half))
                    pool.wait_ge(xT_in[half], b * 16 + 32 + START)
                    pool.sem_inc(turn, 1)
                    split_x(tile(b + 1, half), half)
            for half in range(HALVES):
                root(tile(B - 1, half))

        @blk.vector
        def _(dve):
            chain = Chain(dve, chain_sem)
            tt, ts = nc.vector.tensor_tensor, nc.vector.tensor_scalar
            link = chain.link
            dve.wait_ge(consts_in, 48 + START)
            dve.wait_ge(turned, NT // 4 + START)
            for group in range(NT // 4):
                to = score[:, group * 4 * TB:(group + 1) * 4 * TB].rearrange("p (j t) e -> p j t e", t=TB)
                last = nc.vector.tensor_copy(to, score_ps[:, group, :, :, 0:EXPERTS])
            last.then_inc(scored, 1)
            dve.wait_ge(scored, 1 + START)
            link(tt(biased[:, :, :], score[:, :, :], e_bias[:, :, :], ALU.add))
            four = biased[:, :, :].rearrange("p n (g a b) -> p n g a b", g=GROUPS, a=2)
            tt(pair_hi[:, :, :, :], four[:, :, :, :, 0], four[:, :, :, :, 1], ALU.max)
            link(tt(pair_lo[:, :, :, :], four[:, :, :, :, 0], four[:, :, :, :, 1], ALU.min))
            tt(g1[:, :, :], pair_hi[:, :, :, 0], pair_hi[:, :, :, 1], ALU.max)
            tt(g2[:, :, :], pair_hi[:, :, :, 0], pair_hi[:, :, :, 1], ALU.min)
            link(tt(g3[:, :, :], pair_lo[:, :, :, 0], pair_lo[:, :, :, 1], ALU.max))
            link(tt(g2[:, :, :], g2[:, :, :], g3[:, :, :], ALU.max))
            link(tt(gsum[:, :, :], g1[:, :, :], g2[:, :, :], ALU.add))

            def ranks(values, out, ahead, width):
                for d in range(1, width):
                    w = width - d
                    link(tt(ahead[:, :, 0:w], values[:, :, 0:w], values[:, :, d:width], ALU.is_ge))
                    link(tt(out[:, :, d:width], out[:, :, d:width], ahead[:, :, 0:w], ALU.add))
                    link(tt(out[:, :, 0:w], out[:, :, 0:w], ahead[:, :, 0:w], ALU.subtract))

            ranks(gsum, grank, gge, GROUPS)
            link(ts(gge[:, :, :], grank[:, :, :], float(TOP_GROUPS), None, ALU.is_lt))
            per = EXPERTS // GROUPS
            for i in range(per):
                last = tt(biased[:, :, i::per], biased[:, :, i::per], gge[:, :, :], ALU.mult)
            link(last)
            for i in range(ALLB):
                last = nc.vector.max(largest[:, i], biased[:, i])
            link(last)
            least = largest[:, :, TOPK - 1:TOPK].broadcast_to([P, ALLB, EXPERTS])
            link(tt(keep[:, :, :], biased[:, :, :], least, ALU.is_gt))
            link(tt(equal[:, :, :], biased[:, :, :], least, ALU.is_equal))
            link(nc.vector.tensor_reduce(wsum[:, :], keep[:, :, :], AX.X, ALU.add))
            link(ts(wsum[:, :], wsum[:, :], -1.0, float(TOPK), ALU.mult, ALU.add))
            counts = (equal, up_to[0], up_to[1], up_to[0], up_to[1])
            for i, (source, target) in enumerate(zip(counts, counts[1:])):
                d = 2 ** i
                nc.vector.tensor_copy(target[:, :, 0:d], source[:, :, 0:d])
                link(tt(target[:, :, d:], source[:, :, d:], source[:, :, 0:EXPERTS - d], ALU.add))
            link(tt(equal_kept[:, :, :], target[:, :, :], wsum[:, :].unsqueeze(2).broadcast_to([P, ALLB, EXPERTS]), ALU.is_le))
            link(tt(equal[:, :, :], equal[:, :, :], equal_kept[:, :, :], ALU.mult))
            link(tt(keep[:, :, :], keep[:, :, :], equal[:, :, :], ALU.add))
            link(tt(keep[:, :, :], keep[:, :, :], score[:, :, :], ALU.mult))
            link(nc.vector.tensor_reduce(wsum[:, :], keep[:, :, :], AX.X, ALU.add))
            link(ts(wsum[:, :], wsum[:, :], 1e-20, None, ALU.add))
            link(nc.vector.reciprocal(wsum[:, :], wsum[:, :]))
            link(ts(wsum[:, :], wsum[:, :], ROUTE_SCALE, None, ALU.mult))
            tt(keep[:, :, :], keep[:, :, :], wsum[:, :].unsqueeze(2).broadcast_to([P, ALLB, EXPERTS]), ALU.mult).then_inc(routed, 1)

            with dve.Fori(0, B) as b:
                chain.restart()
                for half in range(HALVES):
                    n = tile(b, half)

                    def multiply(e):
                        count = n * ALL_EXPERTS + e + 1 + START
                        dve.wait_ge(silu_done, count)
                        dve.wait_ge(u_ps, count)
                        tt(h[:, e % 2], silu[:, e % 2], ps_u[:, e % 2], ALU.mult).then_inc(multiplied, 1)

                    def rest(e):
                        dve.wait_ge(h_hi_done, n * ALL_EXPERTS + e + 1 + START)
                        tt(h_lo[:, e % H_SLOTS], h[:, e % 2], h_hi[:, e % H_SLOTS].bitcast(F32), ALU.subtract).then_inc(h_split, 1)

                    def add_up(i):
                        dve.wait_ge(o_ps, n * SUMS + i + 1 + START)
                        if i == 0:
                            dve.wait_ge(landed[half], b * 32 + 32 + START)
                            for t in range(0, TB, 2):
                                last = tt(acc[:, t:t + 2], ps_o[:, i % 2, t:t + 2], x[:, half, t:t + 2], ALU.add)
                        else:
                            dve.wait_ge(added, n * SUMS + i + START)
                            for t in range(TB):
                                last = nc.vector.scalar_tensor_tensor(acc[:, t], ps_o[:, i % 2, t], comb[:, half, t, i - 1:i],
                                                                      acc[:, t], ALU.mult, ALU.add)
                        last.then_inc(added, 1)

                    for e in range(ALL_EXPERTS):
                        multiply(e)
                        if e >= 3:
                            add_up(e - 3)
                        rest(e)
                    for i in range(ALL_EXPERTS - 3, SUMS):
                        add_up(i)
                    dve.wait_ge(added, (n + 1) * SUMS + START)
                    layernorm_stats(nc, dve, chain, acc, stats, moments, var).then_inc(var_ready, 1)
                    dve.wait_ge(rooted, n + 1 + START)
                    for t in range(TB):
                        last = ts(x[:, half, t], acc[:, t], moments[:, t, 0:1], rstd[:, t:t + 1], ALU.subtract, ALU.mult)
                    last.then_inc(normed[half], 1)


SCRATCH = {
    "omega_stack": ((HD, SIX, FEAT), BF16), "mem_stack": ((B * C, SIX, MEM), BF16),
    "q_stack": ((B * C, SIX, T), BF16), "k_stack": ((B * C, SIX, T), BF16), "norms": ((PARTS, B * HEADS * 2, T), BF16),
    "v": ((NQ * T, VW), F32), "y": ((NQ * P, T), F32), "inv": ((B * HEADS, T), F32),
    "combine": ((B * T, EXPERTS), F32), "x2": ((B * T, C), F32), "x3": ((B * T, C), F32), "xT2": ((B * C, T), F32), "xT3": ((B * C, T), F32),
}


def decoder_layer(nc, io, phases=("const", "p1", "a1", "c1", "p2", "a2", "c2", "moe")):
    for name, (shape, dt) in SCRATCH.items():
        if name not in io:
            io[name] = nc.dram_tensor(f"s_{name}", shape, dt).ap()
    if "const" in phases:
        split_constants(nc, io)
    if "p1" in phases:
        project(nc, io, 1)
    if "a1" in phases:
        linear_attention(nc, io)
    if "c1" in phases:
        close_attention(nc, io, 1)
    if "p2" in phases:
        project(nc, io, 2)
    if "a2" in phases:
        softmax_attention(nc, io)
    if "c2" in phases:
        close_attention(nc, io, 2)
    if "moe" in phases:
        experts(nc, io)


def lay_out(x, ctx_1024, L0_attn_W_attn, L0_attn_b_attn, L0_attn_W_proj, L0_attn_b_proj, L0_attn_omega,
            L0_xattn_W_attn, L0_xattn_b_attn, L0_xattn_W_proj, L0_xattn_b_proj, L0_ffn_router_weight,
            L0_ffn_e_bias, L0_ffn_gate_w, L0_ffn_up_w, L0_ffn_down_w, L0_ffn_sh_gate_w, L0_ffn_sh_up_w,
            L0_ffn_sh_down_w):
    import numpy as np

    def rows(v, n):
        return np.ascontiguousarray(np.broadcast_to(np.asarray(v)[None], (n, *np.asarray(v).shape)))

    a = {}
    x = np.asarray(x)
    a["x1"] = x.reshape(B * T, C)
    a["xT1"] = x.transpose(0, 2, 1).reshape(B * C, T)
    ctx = np.asarray(ctx_1024)
    a["memT"] = ctx.transpose(0, 2, 1).reshape(B * C, MEM)
    heads = ctx.reshape(B, MEM, QUADS, 4, HD).transpose(0, 2, 1, 3, 4).reshape(NQ, MEM, 4, HD)
    mem = np.zeros((NQ, P, VW + P), np.float32)
    first = mem[:, :, 0:VW].reshape(NQ, P, 4, V1)
    first[..., 0:HD], first[..., HD] = heads[:, 0:P], 1
    mem[:, :, 0:VW] = first.reshape(NQ, P, VW)
    for j in range(4):
        mem[:, 32 * j:32 * j + MEMR, VW + 32 * j:VW + 32 * j + HD] = heads[:, P:, j]
        mem[:, 32 * j:32 * j + MEMR, VW + 32 * j + HD] = 1
    a["mem"] = mem.reshape(NQ * P, VW + P)
    a["omega"] = np.asarray(L0_attn_omega)
    for n, (w, b, wo, bo) in enumerate(((L0_attn_W_attn, L0_attn_b_attn, L0_attn_W_proj, L0_attn_b_proj),
                                        (L0_xattn_W_attn, L0_xattn_b_attn, L0_xattn_W_proj, L0_xattn_b_proj)), 1):
        a[f"w{n}"] = np.asarray(w)
        a[f"bT{n}"] = np.asarray(b).reshape(6, P).T
        a[f"bv{n}"] = rows(np.asarray(b)[2 * C:], P)
        a[f"wo{n}"] = np.asarray(wo)
        a[f"bo{n}"] = rows(rows(bo, TB), P)
    a["router"] = np.zeros((C, 32), np.float32)
    a["router"][:, 0:EXPERTS] = np.asarray(L0_ffn_router_weight).T
    a["e_bias"] = rows(rows(L0_ffn_e_bias, B * BLOCKS), P)
    a["grank0"] = rows(rows(np.arange(GROUPS - 1, -1, -1, dtype=np.float32), B * BLOCKS), P)
    columns = []
    for routed, shared in ((L0_ffn_gate_w, L0_ffn_sh_gate_w), (L0_ffn_up_w, L0_ffn_sh_up_w)):
        both = np.concatenate([np.asarray(shared).reshape(SHARED, INNER, C), np.asarray(routed)])
        columns.append(both.reshape(ALL_EXPERTS, INNER, CT, P).transpose(3, 0, 2, 1).reshape(P, ALL_EXPERTS, CT * INNER))
    down = np.concatenate([np.asarray(L0_ffn_sh_down_w).reshape(C, SHARED, INNER).transpose(1, 0, 2), np.asarray(L0_ffn_down_w)])
    a["experts"] = np.concatenate([*columns, down.transpose(2, 0, 1)], axis=2)
    eye = np.eye(P, dtype=np.float32)
    a["ident"] = eye
    a["cap"] = rows(np.where(np.arange(P)[:, None] <= np.arange(P)[None], np.finfo(np.float32).max, np.float32(0)), 4).transpose(1, 0, 2)
    sel = np.zeros((P, 2 * CT, 32), np.float32)
    for s in range(2 * CT):
        for p in range(P):
            sel[p, s, 2 * ((s % CT) * (P // HD) + p // HD) + s // CT] = -0.5 / HD
    a["select"] = sel
    a["later"] = np.where(np.arange(P)[None] <= np.arange(P)[:, None], np.float32(0), np.float32(-1.0e30))
    return {k: np.ascontiguousarray(v) for k, v in a.items()}


def kernel(**inputs):
    import numpy as np
    import concourse.bacc as bacc
    from concourse.bass_utils import run_bass_kernel_spmd

    arrays = lay_out(**inputs)
    nc = bacc.Bacc("TRN2", target_bir_lowering=False, num_devices=1)
    io = {n: nc.dram_tensor(n, a.shape, mybir.dt.from_np(a.dtype), kind="ExternalInput").ap() for n, a in arrays.items()}
    io["out"] = nc.dram_tensor("out", (B * T, C), F32, kind="ExternalOutput").ap()
    decoder_layer(nc, io)
    r = run_bass_kernel_spmd(nc, [arrays], core_ids=[0])
    return r.results[0]["out"].reshape(B, T, C)
```

```python
from contextlib import ExitStack

import concourse.bass as bass
from concourse import mybir

F32 = mybir.dt.float32
BF16 = mybir.dt.bfloat16
F32R = mybir.dt.float32r
ALU = mybir.AluOpType
ACT = mybir.ActivationFunctionType
AX = mybir.AxisListType

B, T, C = 4, 1024, 256
HEADS, HD = 16, 16
FEAT = 128
MEM = 154
EXPERTS, SHARED, INNER = 16, 2, 128
ALL_EXPERTS = EXPERTS + SHARED
TOPK, GROUPS, TOP_GROUPS, ROUTE_SCALE = 4, 4, 2, 2.5
LN_EPS = 1e-5
DEN_EPS = 1e-6
P = 128
TILE = 512
HALVES = T // TILE
CT = C // P
TB = TILE // P
QUADS = HEADS // 4
NQ = B * QUADS
BLOCKS = T // P
V1 = HD + 1
VW = 4 * V1
PARTS = 3
LEFT = ((0, 3, 0, 1), (3, 2, 1, 1), (5, 1, 2, 1))
RIGHT = ((0, 3, 0, 3), (3, 2, 0, 2), (5, 1, 0, 1))
SIX = 6
STACK = SIX * HD
STACK1 = STACK + PARTS
START = 1
BIG = 3.0e38
MEMR = MEM - P
MEMW = P + 32


class Phase:

    def __init__(self, nc, name):
        self.nc, self.name, self.ctx, self.held = nc, name, ExitStack(), []
        self.chain = None

    def __enter__(self):
        return self

    def __exit__(self, *a):
        self.ctx.__exit__(*a)
        if a[0] is None:
            self.nc.clear_and_free_semaphores(self.held)
            self.nc.all_engine_barrier()

    def sb(self, name, shape, dt=F32):
        return self.ctx.enter_context(self.nc.sbuf_tensor(f"{self.name}_{name}", shape, dt))

    def ps(self, name, shape, dt=F32):
        return self.ctx.enter_context(self.nc.psum_tensor(f"{self.name}_{name}", shape, dt))

    def sem(self, name):
        self.held.append(self.nc.alloc_semaphore(f"{self.name}_{name}"))
        return self.held[-1]

    def chain_sem(self):
        self.held.append(self.nc.alloc_semaphore(f"{self.name}_chain"))
        self.chain = self.held[-1]
        return self.chain

    def start(self, eng):
        for sem in self.held:
            if sem is not self.chain:
                eng.sem_inc(sem, START)

    def sems(self, name, n):
        return [self.sem(f"{name}{i}") for i in range(n)]

    def block(self):
        return self.ctx.enter_context(self.nc.Block())


class Chain:

    def __init__(self, eng, sem):
        self.eng, self.sem, self.n = eng, sem, 0

    def restart(self):
        self.eng.sem_clear(self.sem)
        self.n = 0

    def link(self, ins):
        self.n += 1
        ins.then_inc(self.sem, 1)
        self.eng.wait_ge(self.sem, self.n)


QUAD_ROWS = 4 * HD


def load_stack(eng, dst, parts, quad, order, sem):
    for first, count, part, n in order:
        src = parts[part:part + n, bass.ds(quad * QUAD_ROWS, QUAD_ROWS)].rearrange("r (d h) t -> r d (h t)", d=HD)
        if n < count:
            src = src.broadcast_to([count, *src.shape[1:]])
        eng.dma_start(dst[first * HD:(first + count) * HD].rearrange("p h t -> p (h t)"), src).then_inc(sem, 16)


def three_passes(nc, out, left, right, start, stop):
    nc.tensor.matmul(out, left[0], right[1], start=start, stop=False)
    nc.tensor.matmul(out, left[1], right[0], start=False, stop=False)
    return nc.tensor.matmul(out, left[0], right[0], start=False, stop=stop)


def project(nc, io):
    xT, w_d, bT_d, bv_d, v_out = io["xT1"], io["w1"], io["bT1"], io["bv1"], io["v"]
    out = (io["q_parts"], io["k_parts"])
    NS = 2 * CT
    n_tiles = B * C // P
    with Phase(nc, "pj") as ph:
        om = ph.sb("om", [HD, FEAT])
        om_rest = ph.sb("om_rest", [HD, FEAT])
        om_parts = ph.sb("om_parts", [HD, PARTS, FEAT], BF16)
        mk = ph.sb("mk", [P, n_tiles, MEMW])
        mk_rest = ph.sb("mk_rest", [P, n_tiles, MEMW])
        mk_parts = ph.sb("mk_parts", [P, PARTS, n_tiles, MEMW], BF16)
        keys_in, keys_split, keys_out = ph.sem("keys_in"), ph.sem("keys_split"), ph.sem("keys_out")
        w = ph.sb("w", [P, CT, 3 * C])
        w_hi, w_lo = ph.sb("w_hi", [P, CT, 3 * C], F32R), ph.sb("w_lo", [P, CT, 3 * C], F32R)
        bias = ph.sb("bias", [P, 6])
        bias_v = ph.sb("bias_v", [P, C])
        x = ph.sb("x", [P, HALVES, CT, TILE])
        x_hi, x_lo = ph.sb("x_hi", [P, HALVES, CT, TILE], F32R), ph.sb("x_lo", [P, HALVES, CT, TILE], F32R)
        full = ph.sb("full", [P, NS, TILE])
        rest = ph.sb("rest", [P, 2, TILE])
        parts = ph.sb("parts", [P, HALVES * NS, PARTS, TILE], BF16)
        v = ph.sb("v", [P, 2, TB, HEADS, V1])
        ps_qk = ph.ps("ps_qk", [P, 2, TILE])
        ps_v = ph.ps("ps_v", [P, TB, C])
        consts_in, chain_sem = ph.sem("consts_in"), ph.chain_sem()
        x_in = ph.sems("x_in", HALVES)
        x_hi_done, x_split = ph.sem("x_hi_done"), ph.sem("x_split")
        w_hi_done, w_split = ph.sem("w_hi_done"), ph.sem("w_split")
        turn = ph.sem("turn")
        qk_ps = ph.sem("qk_ps")
        v_ps = ph.sems("v_ps", HALVES)
        qk_full = ph.sems("qk_full", 2)
        qk_split = ph.sems("qk_split", 2)
        v_full = ph.sem("v_full")
        qk_out = ph.sems("qk_out", HALVES * NS)
        v_out_sem = ph.sems("v_out", 2)
        squares = ph.sb("squares", [P, NS, TILE])
        select = ph.sb("select", [P, NS, 32])
        n_rest = ph.sb("n_rest", [32, TILE])
        n_parts = ph.sb("n_parts", [32, 2, PARTS, TILE], BF16)
        ps_n = ph.ps("ps_n", [32, TILE])
        squared, n_ps, n_split = ph.sem("squared"), ph.sem("n_ps"), ph.sem("n_split")
        qk_first = ph.sem("qk_first")
        n_out = ph.sems("n_out", 2)
        n_consts = 4
        blk = ph.block()

        def load_x(eng, b, half):
            eng.dma_start(x[:, half], xT[bass.ds(b * C, C), half * TILE:(half + 1) * TILE]
                          .rearrange("(a p) t -> p a t", p=P)).then_inc(x_in[half], 16)

        @blk.sync
        def _(sp):
            ph.start(sp)
            sp.dma_start(w[:, :, :], w_d.rearrange("(a p) n -> p a n", p=P)).then_inc(consts_in, 16)
            sp.dma_start(bias[:, :], bT_d).then_inc(consts_in, 16)
            sp.dma_start(bias_v[:, :], bv_d).then_inc(consts_in, 16)
            sp.dma_start(select[:, :, :], io["select"]).then_inc(consts_in, 16)

            def batch_row(b):
                for half in range(HALVES):
                    cols = slice(half * TILE, (half + 1) * TILE)
                    for s in range(NS):
                        sp.wait_ge(qk_split[s % 2], b * (HALVES * NS // 2) + half * (NS // 2) + s // 2 + 1 + START)
                        sp.dma_start(out[s // CT][:, bass.ds(b * C + (s % CT) * P, P), cols].rearrange("r c t -> c r t"), parts[:, half * NS + s]).then_inc(qk_out[half * NS + s], 16)
                    sp.wait_ge(v_full, b * HALVES + half + 1 + START)
                    for t in range(TB):
                        rows = v_out.rearrange("(i t) w -> i t w", t=T)[bass.ds(b * QUADS, QUADS),
                                                                        half * TILE + t * P:half * TILE + (t + 1) * P]
                        sp.dma_start(rows.rearrange("g t w -> t g w"),
                                     v[:, half, t].rearrange("p (g h) d -> p g (h d)", g=QUADS)).then_inc(v_out_sem[half], 16)
                    sp.wait_ge(n_split, b * HALVES + half + 1 + START)
                    sp.dma_start(io["norms"][:, bass.ds(b * 2 * HEADS, 2 * HEADS), cols].rearrange("n h t -> h n t"),
                                 n_parts[:, half]).then_inc(n_out[half], 16)

            for half in range(HALVES):
                load_x(sp, 0, half)
            sp.dma_start(om[:, :], io["omega"]).then_inc(keys_in, 16)
            sp.dma_start(mk[:, :, :], io["memT"].rearrange("(a p) s -> p a s", p=P)).then_inc(keys_in, 16)
            with sp.Fori(0, B) as b:
                batch_row(b)
            sp.wait_ge(keys_out, 16 * (1 + PARTS) + START)
            for sem in qk_out:
                sp.wait_ge(sem, 16 * B + START)
            for half in range(HALVES):
                sp.wait_ge(v_out_sem[half], 16 * TB * B + START)
                sp.wait_ge(n_out[half], 16 * B + START)

        @blk.tensor
        def _(pe):
            pe.wait_ge(w_split, 1 + START)
            with pe.Fori(0, B) as b:
                for half in range(HALVES):
                    n = b * HALVES + half
                    pe.wait_ge(x_split, n + 1 + START)
                    for s in range(NS):
                        pe.wait_ge(qk_full[s % 2], b * (HALVES * NS // 2) + half * (NS // 2) + s // 2 + START)
                        cols = slice(s * P, (s + 1) * P)
                        for a in range(CT):
                            last = three_passes(nc, ps_qk[:, s % 2], (w_hi[:, a, cols], w_lo[:, a, cols]),
                                                (x_hi[:, half, a], x_lo[:, half, a]), start=a == 0, stop=a == CT - 1)
                        last.then_inc(qk_ps, 1)
                    pe.wait_ge(v_full, n + START)
                    for t in range(TB):
                        tokens = slice(t * P, (t + 1) * P)
                        for a in range(CT):
                            last = three_passes(nc, ps_v[:, t], (x_hi[:, half, a, tokens], x_lo[:, half, a, tokens]),
                                                (w_hi[:, a, 2 * C:3 * C], w_lo[:, a, 2 * C:3 * C]),
                                                start=a == 0, stop=a == CT - 1)
                    last.then_inc(v_ps[half], 1)
                    pe.wait_ge(squared, (n + 1) * NS + START)
                    pe.wait_ge(n_split, n + START)
                    for s in range(NS):
                        last = nc.tensor.matmul(ps_n[:, :], select[:, s], squares[:, s], start=s == 0, stop=s == NS - 1)
                    last.then_inc(n_ps, 1)

        @blk.scalar
        def _(act):
            act.wait_ge(consts_in, 16 * n_consts + START)
            nc.scalar.activation(w_hi[:, :, :], w[:, :, :], ACT.Copy).then_inc(w_hi_done, 1)

            def x_first(b, half):
                act.wait_ge(x_in[half], b * 16 + 16 + START)
                if not (isinstance(b, int) and b == 0):
                    act.wait_ge(v_ps[half], b + START)
                nc.scalar.activation(x_hi[:, half], x[:, half], ACT.Copy).then_inc(x_hi_done, 1)

            def row(b, more):
                for half in range(HALVES):
                    n = b * HALVES + half
                    if half == 0:
                        x_first(b, 1)
                    elif more:
                        x_first(b + 1, 0)
                    if more:
                        act.wait_ge(x_split, n + 1 + START)
                        load_x(act, b + 1, half)
                    act.wait_ge(n_ps, n + START)
                    for s in range(NS):
                        act.wait_ge(qk_ps, n * NS + s + 1 + START)
                        act.wait_ge(qk_split[s % 2], n * (NS // 2) + START)
                        nc.scalar.activation(full[:, s], ps_qk[:, s % 2], ACT.Identity, bias=bias[:, s:s + 1]).then_inc(qk_full[s % 2], 1)
                        act.wait_ge(qk_full[s % 2], b * (HALVES * NS // 2) + half * (NS // 2) + s // 2 + 1 + START)
                        act.wait_ge(qk_out[half * NS + s], b * 16 + START)
                        nc.scalar.activation(parts[:, half * NS + s, 0], full[:, s], ACT.Copy).then_inc(qk_first, 1)
                        nc.scalar.activation(squares[:, s], full[:, s], ACT.Square).then_inc(squared, 1)

            x_first(0, 0)
            with act.Fori(0, B - 1) as b:
                row(b, True)
            act.wait_ge(keys_split, 2 + START)
            act.dma_start(io["omega_parts"].rearrange("r d m -> d r m"), om_parts[:, :, :]).then_inc(keys_out, 16)
            for part in range(PARTS):
                act.dma_start(io["mem_parts"][part].rearrange("(a p) s -> p a s", p=P), mk_parts[:, part]).then_inc(keys_out, 16)
            row(B - 1, False)

        @blk.gpsimd
        def _(pool):
            def x_rest(b, half):
                pool.wait_ge(x_hi_done, b * HALVES + half + 1 + START)
                pool.sem_inc(turn, 1)
                nc.gpsimd.tensor_tensor(x_lo[:, half], x[:, half], x_hi[:, half].bitcast(F32), ALU.subtract).then_inc(x_split, 1)

            def row(b, more):
                for half in range(HALVES):
                    if half == 0:
                        x_rest(b, 1)
                    elif more:
                        x_rest(b + 1, 0)

            x_rest(0, 0)
            with pool.Fori(0, B - 1) as b:
                row(b, True)
            row(B - 1, False)

        @blk.vector
        def _(dve):
            chain = Chain(dve, chain_sem)
            chain.link(nc.vector.memset(v[:, :, :, :, HD:V1], 1.0))
            dve.wait_ge(consts_in, 16 * n_consts + START)
            dve.wait_ge(w_hi_done, 1 + START)
            nc.vector.tensor_tensor(w_lo[:, :, :], w[:, :, :], w_hi[:, :, :].bitcast(F32), ALU.subtract).then_inc(w_split, 1)
            dve.wait_ge(keys_in, 32 + START)
            chain.link(nc.vector.tensor_scalar(om[:, :], om[:, :], HD ** -0.5, None, ALU.mult))
            for full_keys, keys_rest, keys_parts in ((om[:, :], om_rest[:, :], [om_parts[:, i] for i in range(PARTS)]),
                                                     (mk[:, :, :], mk_rest[:, :, :], [mk_parts[:, i] for i in range(PARTS)])):
                chain.link(nc.vector.tensor_copy(keys_parts[0], full_keys))
                chain.link(nc.vector.tensor_tensor(keys_rest, full_keys, keys_parts[0], ALU.subtract))
                chain.link(nc.vector.tensor_copy(keys_parts[1], keys_rest))
                nc.vector.tensor_tensor(keys_parts[2], keys_rest, keys_parts[1], ALU.subtract).then_inc(keys_split, 1)
            with dve.Fori(0, B) as b:
                chain.restart()
                for half in range(HALVES):
                    for s in range(NS):
                        use = b * (HALVES * NS // 2) + half * (NS // 2) + s // 2
                        dve.wait_ge(qk_full[s % 2], use + 1 + START)
                        dve.wait_ge(qk_first, b * (HALVES * NS) + half * NS + s + 1 + START)
                        chain.link(nc.vector.tensor_tensor(rest[:, s % 2], full[:, s], parts[:, half * NS + s, 0], ALU.subtract))
                        chain.link(nc.vector.tensor_copy(parts[:, half * NS + s, 1], rest[:, s % 2]))
                        nc.vector.tensor_tensor(parts[:, half * NS + s, 2], rest[:, s % 2], parts[:, half * NS + s, 1],
                                                ALU.subtract).then_inc(qk_split[s % 2], 1)
                    dve.wait_ge(v_ps[half], b + 1 + START)
                    dve.wait_ge(v_out_sem[half], b * (16 * TB) + START)
                    for t in range(TB):
                        last = nc.vector.tensor_tensor(v[:, half, t, :, 0:HD],
                                                       ps_v[:, t].rearrange("p (h d) -> p h d", d=HD),
                                                       bias_v[:, :].rearrange("p (h d) -> p h d", d=HD), ALU.add)
                    last.then_inc(v_full, 1)
                    dve.wait_ge(n_ps, b * HALVES + half + 1 + START)
                    dve.wait_ge(n_out[half], b * 16 + START)
                    chain.link(nc.vector.tensor_copy(n_parts[:, half, 0], ps_n[:, :]))
                    chain.link(nc.vector.tensor_tensor(n_rest[:, :], ps_n[:, :], n_parts[:, half, 0], ALU.subtract))
                    chain.link(nc.vector.tensor_copy(n_parts[:, half, 1], n_rest[:, :]))
                    nc.vector.tensor_tensor(n_parts[:, half, 2], n_rest[:, :], n_parts[:, half, 1],
                                            ALU.subtract).then_inc(n_split, 1)


def linear_attention(nc, io):
    PAIRS = NQ // 2
    with Phase(nc, "la") as ph:
        omega = ph.sb("omega", [STACK1, FEAT], BF16)
        cap = ph.sb("cap", [P, 4, P])
        ident = ph.sb("ident", [P, P])
        q = [ph.sb(f"q{i}", [STACK1, 4, T], BF16) for i in range(2)]
        k = [ph.sb(f"k{i}", [STACK1, 4, T], BF16) for i in range(2)]
        v = [ph.sb(f"v{i}", [P, BLOCKS, VW]) for i in range(2)]
        phi_kT = ph.sb("phi_kT", [P, 2, 4, P])
        phi_qT = ph.sb("phi_qT", [P, 2, 4, P])
        phi_k = ph.sb("phi_k", [P, 2, 4, FEAT])
        att = ph.sb("att", [P, 2, 4, P])
        stateT = ph.sb("stateT", [P, FEAT])
        state = ph.sb("state", [P, P])
        y = ph.sb("y", [P, 2, T])
        ps_kT, ps_qT, ps_k, ps_att = (ph.ps(n, [P, 4, P]) for n in ("ps_kT", "ps_qT", "ps_k", "ps_att"))
        ps_y = ph.ps("ps_y", [P, TILE])
        ps_stateT = ph.ps("ps_stateT", [P, TILE])
        ps_state = ph.ps("ps_state", [P, TILE])
        consts_in, cleared = ph.sem("consts_in"), ph.sem("cleared")
        landed = ph.sems("landed", 2)
        kT_ps, qT_ps, k_ps, att_ps, y_ps, stateT_ps, state_ps = (
            ph.sem(n) for n in ("kT_ps", "qT_ps", "k_ps", "att_ps", "y_ps", "stateT_ps", "state_ps"))
        kT_done, qT_done, k_done, att_done, stateT_done, state_done = (
            ph.sem(n) for n in ("kT_done", "qT_done", "k_done", "att_done", "stateT_done", "state_done"))
        y_done = ph.sems("y_done", 2)
        stored = ph.sems("stored", 2)
        LOADS = 9
        N_CONST = 5

        def step(kk, pr, c):
            return kk * (2 * BLOCKS) + pr * BLOCKS + c

        def state_step(kk, pr, c):
            return kk * (2 * (BLOCKS - 1)) + pr * (BLOCKS - 1) + c

        blk = ph.block()

        @blk.sync
        def _(sp):
            ph.start(sp)
            for first, count, part, n in RIGHT:
                src = io["omega_parts"][part:part + n]
                sp.dma_start(omega[first * HD:(first + count) * HD, :], src).then_inc(consts_in, 16)
            sp.dma_start(cap[:, :, :], io["cap"]).then_inc(consts_in, 16)
            sp.dma_start(ident[:, :], io["ident"]).then_inc(consts_in, 16)

            def load(kk, pr):
                heads = bass.ds(kk * 8 + pr * 4, 4)
                for side, (dst, stored_parts) in enumerate(((q[pr], io["q_parts"]), (k[pr], io["k_parts"]))):
                    load_stack(sp, dst, stored_parts, kk * 2 + pr, LEFT, landed[pr])
                    sp.dma_start(dst[STACK:STACK1], io["norms"].rearrange("n (h s) t -> n h s t", s=2)[:, heads, side]).then_inc(landed[pr], 16)
                sp.dma_start(v[pr][:, :, :], io["v"][bass.ds(kk * (2 * T) + pr * T, T)]
                             .rearrange("(n p) w -> p n w", p=P)).then_inc(landed[pr], 16)

            def pair(kk, more):
                for pr in range(2):
                    sp.wait_ge(y_done[pr], kk * BLOCKS + BLOCKS + START)
                    sp.dma_start(io["y"][bass.ds(kk * (2 * P) + pr * P, P)], y[:, pr]).then_inc(stored[pr], 16)
                    if more:
                        load(kk + 1, pr)

            for pr in range(2):
                load(0, pr)
            with sp.Fori(0, PAIRS - 1) as kk:
                pair(kk, True)
            pair(PAIRS - 1, False)
            for pr in range(2):
                sp.wait_ge(stored[pr], PAIRS * 16 + START)

        @blk.tensor
        def _(pe):
            pe.wait_ge(consts_in, 16 * N_CONST + START)
            pe.wait_ge(cleared, 3 + START)

            def features(kk, pr, c):
                if c == 0:
                    pe.wait_ge(landed[pr], kk * (16 * LOADS) + 16 * LOADS + START)
                cols = slice(c * P, (c + 1) * P)
                pe.wait_ge(kT_done, step(kk, pr, c) + START)
                nc.tensor.matmul(ps_kT[:, :, :], omega[:, :], k[pr][:, :, cols],
                                 start=True, stop=True).then_inc(kT_ps, 1)
                pe.wait_ge(qT_done, step(kk, pr, c) + START)
                nc.tensor.matmul(ps_qT[:, :, :], omega[:, :], q[pr][:, :, cols],
                                 start=True, stop=True).then_inc(qT_ps, 1)
                if c < BLOCKS - 1:
                    pe.wait_ge(k_done, state_step(kk, pr, c) + START)
                    for j in range(4):
                        last = nc.tensor.matmul(ps_k[:, j], k[pr][:, j, cols], omega[:, :], start=True, stop=True)
                    last.then_inc(k_ps, 1)

            def quad(kk, pr, following):
                for c in range(BLOCKS):
                    d = c % 2
                    pe.wait_ge(kT_done, step(kk, pr, c) + 1 + START)
                    pe.wait_ge(qT_done, step(kk, pr, c) + 1 + START)
                    pe.wait_ge(att_done, step(kk, pr, c) + START)
                    for j in range(4):
                        last = nc.tensor.matmul(ps_att[:, j], phi_kT[:, d, j], phi_qT[:, d, j], start=True, stop=True)
                    last.then_inc(att_ps, 1)
                    if c < BLOCKS - 1:
                        features(kk, pr, c + 1)
                        pe.wait_ge(k_done, state_step(kk, pr, c) + 1 + START)
                        pe.wait_ge(stateT_done, state_step(kk, pr, c) + START)
                        for j in range(4):
                            last = nc.tensor.matmul(ps_stateT[32 * j:32 * j + V1, 0:FEAT],
                                                    v[pr][:, c, j * V1:(j + 1) * V1], phi_k[:, d, j],
                                                    start=c == 0, stop=True, skip_group_check=True)
                        last.then_inc(stateT_ps, 1)
                    elif following is not None:
                        features(*following, 0)
                    if c > 0:
                        pe.wait_ge(y_done[pr], kk * BLOCKS + c + START)
                        pe.wait_ge(state_done, state_step(kk, pr, c - 1) + 1 + START)
                        for j in range(4):
                            nc.tensor.matmul(ps_y[32 * j:32 * j + V1, 0:P], state[:, 32 * j:32 * j + V1],
                                             phi_qT[:, d, j], start=True, stop=False)
                    else:
                        pe.wait_ge(y_done[1 - pr], kk * BLOCKS + pr * BLOCKS + START)
                    pe.wait_ge(att_done, step(kk, pr, c) + 1 + START)
                    for j in range(4):
                        last = nc.tensor.matmul(ps_y[32 * j:32 * j + V1, 0:P], v[pr][:, c, j * V1:(j + 1) * V1],
                                                att[:, d, j], start=c == 0, stop=True)
                    last.then_inc(y_ps, 1)
                    if c < BLOCKS - 1:
                        pe.wait_ge(stateT_done, state_step(kk, pr, c) + 1 + START)
                        pe.wait_ge(state_done, state_step(kk, pr, c) + START)
                        nc.tensor.transpose(ps_state[:, 0:P], stateT[:, :], ident[:, :]).then_inc(state_ps, 1)

            features(0, 0, 0)
            with pe.Fori(0, PAIRS - 1) as kk:
                quad(kk, 0, (kk, 1))
                quad(kk, 1, (kk + 1, 0))
            quad(PAIRS - 1, 0, (PAIRS - 1, 1))
            quad(PAIRS - 1, 1, None)

        @blk.scalar
        def _(act):
            def exps(kk, pr, c):
                d = c % 2
                act.wait_ge(kT_ps, step(kk, pr, c) + 1 + START)
                nc.scalar.activation(phi_kT[:, d], ps_kT[:, :, :], ACT.Exp).then_inc(kT_done, 1)
                act.wait_ge(qT_ps, step(kk, pr, c) + 1 + START)
                nc.scalar.activation(phi_qT[:, d], ps_qT[:, :, :], ACT.Exp).then_inc(qT_done, 1)

            def exp_k(kk, pr, c):
                act.wait_ge(k_ps, state_step(kk, pr, c) + 1 + START)
                nc.scalar.activation(phi_k[:, c % 2], ps_k[:, :, :], ACT.Exp).then_inc(k_done, 1)

            def quad(kk, pr, following):
                for c in range(BLOCKS - 1):
                    exps(kk, pr, c + 1)
                    if c < BLOCKS - 2:
                        exp_k(kk, pr, c + 1)
                if following is not None:
                    exps(*following, 0)
                    exp_k(*following, 0)

            exps(0, 0, 0)
            exp_k(0, 0, 0)
            with act.Fori(0, PAIRS - 1) as kk:
                quad(kk, 0, (kk, 1))
                quad(kk, 1, (kk + 1, 0))
            quad(PAIRS - 1, 0, (PAIRS - 1, 1))
            quad(PAIRS - 1, 1, None)

        @blk.vector
        def _(dve):
            nc.vector.memset(omega[STACK:STACK1, :], 1.0).then_inc(cleared, 1)
            nc.vector.memset(ps_y[:, :], 0.0).then_inc(cleared, 1)
            nc.vector.memset(ps_stateT[:, :], 0.0).then_inc(cleared, 1)
            dve.wait_ge(consts_in, 16 * N_CONST + START)
            with dve.Fori(0, PAIRS) as kk:
                for pr in range(2):
                    dve.wait_ge(stored[pr], kk * 16 + START)
                    for c in range(BLOCKS):
                        dve.wait_ge(att_ps, step(kk, pr, c) + 1 + START)
                        nc.vector.tensor_tensor(att[:, c % 2], ps_att[:, :, :], cap[:, :, :], ALU.min).then_inc(att_done, 1)
                        if c < BLOCKS - 1:
                            dve.wait_ge(stateT_ps, state_step(kk, pr, c) + 1 + START)
                            nc.vector.tensor_copy(stateT[:, :], ps_stateT[:, 0:FEAT]).then_inc(stateT_done, 1)
                        dve.wait_ge(y_ps, step(kk, pr, c) + 1 + START)
                        nc.vector.tensor_copy(y[:, pr, c * P:(c + 1) * P], ps_y[:, 0:P]).then_inc(y_done[pr], 1)
                        if c < BLOCKS - 1:
                            dve.wait_ge(state_ps, state_step(kk, pr, c) + 1 + START)
                            nc.vector.tensor_copy(state[:, :], ps_state[:, 0:P]).then_inc(state_done, 1)


def layernorm_stats(nc, dve, chain, z, stats, moments, var):
    for t in range(TB):
        ins = nc.vector.bn_stats(stats[:, t], z[:, t])
    chain.link(ins)
    for t in range(TB):
        ins = nc.vector.bn_aggr(moments[:, t], stats[:, t])
    chain.link(ins)
    return nc.vector.tensor_scalar(var[:, :], moments[:, :, 1], LN_EPS, None, ALU.add)


def close_attention(nc, io, stage):
    x_d, xo_d = io[f"x{stage}"], io[f"x{stage + 1}"]
    eps = DEN_EPS * FEAT if stage == 1 else 0.0
    on = stage == 1
    AHEAD = 1 if on else 2
    out = (io["q_parts"], io["k_parts"])
    NS = 2 * CT
    with Phase(nc, f"cl{stage}") as ph:
        w = ph.sb("w", [P, CT, C])
        bias = ph.sb("bias", [P, TB, C])
        ident = ph.sb("ident", [P, P])
        den = ph.sb("den", [P, T * B * HEADS // P])
        y = ph.sb("y", [P, HALVES, CT, TILE])
        inv = ph.sb("inv", [P, HALVES, CT, TILE])
        yn = ph.sb("yn", [P, HALVES, CT, TILE])
        x = ph.sb("x", [P, HALVES, TB, C])
        xb = ph.sb("xb", [P, HALVES, TB, C])
        z = ph.sb("z", [P, TB, C])
        xn = ph.sb("xn", [P, HALVES, TB, C])
        xT = ph.sb("xT", [P, HALVES, CT, TILE])
        stats, moments = ph.sb("stats", [P, TB, 6]), ph.sb("moments", [P, TB, 2])
        var, power, rstd = (ph.sb(n, [P, TB]) for n in ("var", "power", "rstd"))
        ps_o = ph.ps("ps_o", [P, AHEAD, TB, C])
        ps_t = ph.ps("ps_t", [P, CT, TILE])
        consts_in, chain_sem, power_set = ph.sem("consts_in"), ph.chain_sem(), ph.sem("power_set")
        den_in, den_inv, inv_out, first_in, first_inv = (ph.sem(n) for n in ("den_in", "den_inv", "inv_out", "first_in", "first_inv"))
        landed = ph.sems("landed", HALVES)
        scaled, biased, o_ps, summed, var_ready, rooted = (
            ph.sem(n) for n in ("scaled", "biased", "o_ps", "summed", "var_ready", "rooted"))
        turn = ph.sem("turn")
        normed, stored, stored_T = (ph.sems(n, HALVES) for n in ("normed", "stored", "stored_T"))
        t_ps, t_done = ph.sem("t_ps"), ph.sem("t_done")
        if on:
            w_qkv = ph.sb("w_qkv", [P, CT, 3 * C])
            bias_qk = ph.sb("bias_qk", [P, 6])
            bias_v = ph.sb("bias_v", [P, C])
            full = ph.sb("full", [P, NS, TILE])
            rest = ph.sb("rest", [P, NS, TILE])
            parts = ph.sb("parts", [P, NS, PARTS, TILE], BF16)
            v = ph.sb("v", [P, 2, TB, HEADS, V1])
            ps_qk = ph.ps("ps_qk", [P, 2, TILE])
            ps_v = ph.ps("ps_v", [P, TB, C])
            qk_ps, v_ps, qk_first = ph.sem("qk_ps"), ph.sem("v_ps"), ph.sem("qk_first")
            qk_full = ph.sems("qk_full", 2)
            qk_split = ph.sems("qk_split", 2)
            v_full = ph.sem("v_full")
            qk_out, v_out = ph.sems("qk_out", NS), ph.sems("v_out", 2)
        else:
            router = ph.sb("router", [P, CT, 32])
            scoreT = ph.sb("scoreT", [P, TILE])
            score = ph.sb("score", [P, HALVES, TB, EXPERTS])
            ps_r = ph.ps("ps_r", [32, TILE])
            ps_s = ph.ps("ps_s", [P, TB, P])
            cleared = ph.sem("cleared")
            r_ps, r_done, s_ps, s_done = (ph.sem(n) for n in ("r_ps", "r_done", "s_ps", "s_done"))
            scores_out = ph.sems("scores_out", HALVES)
        N_CONST = 6 if on else 4
        LOADS = 5
        blk = ph.block()

        def tile(b, half):
            return b * HALVES + half

        def wait_summed(eng, n, behind):
            if not (isinstance(n, int) and n < behind):
                eng.wait_ge(summed, n - behind + 1 + START)

        def use(b, half, s):
            return b * (HALVES * NS // 2) + half * (NS // 2) + s // 2

        def load_y(eng, b, half):
            for a in range(CT):
                rows = io["y"].rearrange("(h r) t -> h r t", r=32)[bass.ds(b * HEADS + a * (HEADS // CT), HEADS // CT), 0:HD,
                                                                 half * TILE:(half + 1) * TILE]
                eng.dma_start(y[:, half, a], rows).then_inc(landed[half], 16)

        def load_inv(eng, b, half):
            for a in range(CT):
                heads = io["inv"][bass.ds(b * HEADS + a * (HEADS // CT), HEADS // CT), half * TILE:(half + 1) * TILE]
                eng.dma_start(inv[:, half, a], heads.unsqueeze(1).broadcast_to([HEADS // CT, HD, TILE])).then_inc(landed[half], 16)

        def load_x(eng, b, half):
            eng.dma_start(x[:, half], x_d[bass.ds(b * T + half * TILE, TILE)]
                          .rearrange("(n p) c -> p n c", p=P)).then_inc(landed[half], 16)

        def load_inputs(eng, b, half):
            eng.wait_ge(biased, tile(b, half) + 1 + START)
            load_y(eng, b + 1, half)
            load_inv(eng, b + 1, half)
            load_x(eng, b + 1, half)

        @blk.sync
        def _(sp):
            ph.start(sp)
            rows = io["y"].rearrange("(h r) t -> h r t", r=32)
            for a in range(CT):
                heads = rows[a * (HEADS // CT):(a + 1) * (HEADS // CT), HD, 0:TILE]
                sp.dma_start(inv[:, 0, a], heads.unsqueeze(1).broadcast_to([HEADS // CT, HD, TILE])).then_inc(first_in, 16)
            sp.dma_start(den[:, :], io["y"].rearrange("(h r) (s t) -> h r s t", r=32, s=2)[:, HD]).then_inc(den_in, 16)
            load_y(sp, 0, 0)
            load_x(sp, 0, 0)
            sp.dma_start(w[:, :, :], io[f"wo{stage}"].rearrange("(a p) n -> p a n", p=P)).then_inc(consts_in, 16)
            sp.dma_start(bias[:, :, :], io[f"bo{stage}"]).then_inc(consts_in, 16)
            sp.dma_start(ident[:, :], io["ident"]).then_inc(consts_in, 16)
            if on:
                sp.dma_start(w_qkv[:, :, :], io["w2"].rearrange("(a p) n -> p a n", p=P)).then_inc(consts_in, 16)
                sp.dma_start(bias_qk[:, :], io["bT2"]).then_inc(consts_in, 16)
                sp.dma_start(bias_v[:, :], io["bv2"]).then_inc(consts_in, 16)
            else:
                sp.dma_start(router[:, :, :], io["router"].rearrange("(a p) e -> p a e", p=P)).then_inc(consts_in, 16)

            load_y(sp, 0, 1)
            load_x(sp, 0, 1)
            sp.wait_ge(den_inv, 1 + START)
            sp.dma_start(io["inv"].rearrange("h (s t) -> (h s) t", s=2), den[:, :]).then_inc(inv_out, 16)
            sp.wait_ge(inv_out, 16 + START)
            load_inv(sp, 0, 1)

            def batch_row(b, more):
                for half in range(HALVES):
                    if not on and more:
                        load_inputs(sp, b, half)
                    sp.wait_ge(normed[half], b + 1 + START)
                    sp.dma_start(xo_d[bass.ds(b * T + half * TILE, TILE)].rearrange("(n p) c -> p n c", p=P),
                                 xn[:, half]).then_inc(stored[half], 16)
                    cols = slice(half * TILE, (half + 1) * TILE)
                    if not on:
                        sp.wait_ge(t_done, tile(b, half) + 1 + START)
                        sp.dma_start(io["xT3"][bass.ds(b * C, C), cols].rearrange("(a p) t -> p a t", p=P),
                                     xT[:, half]).then_inc(stored_T[half], 16)
                        continue
                    for s in range(NS):
                        sp.wait_ge(qk_split[s % 2], use(b, half, s) + 1 + START)
                        sp.dma_start(out[s // CT][:, bass.ds(b * C + (s % CT) * P, P), cols].rearrange("r c t -> c r t"), parts[:, s]).then_inc(qk_out[s], 16)
                    sp.wait_ge(v_full, tile(b, half) + 1 + START)
                    for t in range(TB):
                        rows = io["v"].rearrange("(i t) w -> i t w", t=T)[bass.ds(b * QUADS, QUADS),
                                                                          half * TILE + t * P:half * TILE + (t + 1) * P]
                        sp.dma_start(rows.rearrange("g t w -> t g w"),
                                     v[:, half, t].rearrange("p (g h) d -> p g (h d)", g=QUADS)).then_inc(v_out[half], 16)

            with sp.Fori(0, B - 1) as b:
                batch_row(b, True)
            batch_row(B - 1, False)
            for half in range(HALVES):
                sp.wait_ge(stored[half], 16 * B + START)
                if on:
                    sp.wait_ge(v_out[half], 16 * TB * B + START)
                else:
                    sp.wait_ge(stored_T[half], 16 * B + START)
                    sp.wait_ge(scores_out[half], 16 * B + START)
            if on:
                for s in range(NS):
                    sp.wait_ge(qk_out[s], 16 * B * HALVES + START)

        @blk.gpsimd
        def _(pool):
            nc.gpsimd.memset(power[:, :], -0.5).then_inc(power_set, 1)
            pool.wait_ge(power_set, 1 + START)
            pool.wait_ge(consts_in, 16 * N_CONST + START)

            def inputs(b, half):
                if half == 0:
                    pool.wait_ge(landed[0], b * (16 * LOADS) + 16 * (LOADS - CT) + START)
                    pool.wait_ge(first_inv, 1 + START)
                else:
                    pool.wait_ge(landed[1], b * (16 * LOADS) + 16 * LOADS + START)
                wait_summed(pool, tile(b, half), 2)
                nc.gpsimd.tensor_tensor(yn[:, half], y[:, half], inv[:, half], ALU.mult).then_inc(scaled, 1)
                nc.gpsimd.tensor_tensor(xb[:, half], x[:, half], bias[:, :, :], ALU.add).then_inc(biased, 1)

            def root(b, half):
                pool.wait_ge(var_ready, tile(b, half) + 1 + START)
                pool.sem_inc(turn, 1)
                nc.gpsimd.tensor_tensor(rstd[:, :], var[:, :], power[:, :], ALU.pow).then_inc(rooted, 1)

            inputs(0, 0)
            inputs(0, 1)
            if on:
                root(0, 0)
            with pool.Fori(0, B - 1) as b:
                root(b, AHEAD % 2)
                inputs(b + 1, 0)
                root(*((b + 1, 0) if on else (b, 1)))
                inputs(b + 1, 1)
            for half in range(AHEAD % 2, HALVES):
                root(B - 1, half)

        @blk.tensor
        def _(pe):
            pe.wait_ge(consts_in, 16 * N_CONST + START)

            def out_project(b, half):
                pe.wait_ge(scaled, tile(b, half) + 1 + START)
                wait_summed(pe, tile(b, half), AHEAD)
                for t in range(TB):
                    for a in range(CT):
                        last = nc.tensor.matmul(ps_o[:, half % AHEAD, t], yn[:, half, a, t * P:(t + 1) * P], w[:, a],
                                                start=a == 0, stop=a == CT - 1)
                last.then_inc(o_ps, 1)

            def qkv(b, half):
                n = tile(b, half)
                pe.wait_ge(t_done, n + 1 + START)
                for s in range(NS):
                    pe.wait_ge(qk_full[s % 2], use(b, half, s) + START)
                    for a in range(CT):
                        last = nc.tensor.matmul(ps_qk[:, s % 2], w_qkv[:, a, s * P:(s + 1) * P], xT[:, half, a],
                                                start=a == 0, stop=a == CT - 1)
                    last.then_inc(qk_ps, 1)
                pe.wait_ge(v_full, n + START)
                for t in range(TB):
                    for a in range(CT):
                        last = nc.tensor.matmul(ps_v[:, t], xT[:, half, a, t * P:(t + 1) * P], w_qkv[:, a, 2 * C:3 * C],
                                                start=a == 0, stop=a == CT - 1)
                last.then_inc(v_ps, 1)

            def route(b, half):
                n = tile(b, half)
                pe.wait_ge(t_done, n + 1 + START)
                pe.wait_ge(r_done, n + START)
                for a in range(CT):
                    last = nc.tensor.matmul(ps_r[:, :], router[:, a], xT[:, half, a], start=a == 0, stop=a == CT - 1)
                last.then_inc(r_ps, 1)

            def turn_scores(b, half):
                n = tile(b, half)
                pe.wait_ge(r_done, n + 1 + START)
                pe.wait_ge(s_done, n + START)
                for t in range(TB):
                    last = nc.tensor.transpose(ps_s[:, t], scoreT[:, t * P:(t + 1) * P], ident[:, :])
                last.then_inc(s_ps, 1)

            def row(b, first, more):
                for half in range(HALVES):
                    pe.wait_ge(normed[half], b + 1 + START)
                    pe.wait_ge(t_done, tile(b, half) + START)
                    for a in range(CT):
                        for t in range(TB):
                            last = nc.tensor.transpose(ps_t[:, a, t * P:(t + 1) * P], xn[:, half, t, a * P:(a + 1) * P], ident[:, :])
                    last.then_inc(t_ps, 1)
                    if not on and not (first and half == 0):
                        turn_scores(*((b, 0) if half else (b - 1, 1)))
                    row_ahead, half_ahead = (half + AHEAD) // HALVES, (half + AHEAD) % HALVES
                    if more or not row_ahead:
                        out_project(b + row_ahead, half_ahead)
                    if on:
                        qkv(b, half)
                    else:
                        route(b, half)

            for half in range(AHEAD):
                out_project(0, half)
            row(0, True, True)
            with pe.Fori(1, B - 1) as b:
                row(b, False, True)
            row(B - 1, False, False)
            if not on:
                turn_scores(B - 1, 1)

        @blk.scalar
        def _(act):
            act.wait_ge(consts_in, 16 * N_CONST + START)
            act.wait_ge(inv_out, 16 + START)
            if not on:
                act.wait_ge(cleared, 1 + START)

            def store_scores(b, half):
                n = tile(b, half)
                act.wait_ge(s_ps, n + 1 + START)
                act.wait_ge(scores_out[half], b * 16 + START)
                nc.scalar.activation(score[:, half], ps_s[:, :, 0:EXPERTS], ACT.Copy).then_inc(s_done, 1)
                act.wait_ge(s_done, n + 1 + START)
                act.dma_start(io["score"][bass.ds(b * T + half * TILE, TILE)].rearrange("(n p) e -> p n e", p=P),
                              score[:, half]).then_inc(scores_out[half], 16)

            def row(b, first, more):
                for half in range(HALVES):
                    n = tile(b, half)
                    if on and more:
                        load_inputs(act, b, half)
                    act.wait_ge(t_ps, n + 1 + START)
                    if not on:
                        act.wait_ge(stored_T[half], b * 16 + START)
                    nc.scalar.activation(xT[:, half], ps_t[:, :, :], ACT.Copy).then_inc(t_done, 1)
                    if not on:
                        if not (first and half == 0):
                            store_scores(*((b, 0) if half else (b - 1, 1)))
                        act.wait_ge(r_ps, n + 1 + START)
                        nc.scalar.activation(scoreT[0:32, :], ps_r[:, :], ACT.Sigmoid).then_inc(r_done, 1)
                    if on:
                        for s in range(NS):
                            act.wait_ge(qk_ps, n * NS + s + 1 + START)
                            act.wait_ge(qk_out[s], n * 16 + START)
                            nc.scalar.activation(parts[:, s, 0], ps_qk[:, s % 2], ACT.Identity,
                                                 bias=bias_qk[:, s:s + 1]).then_inc(qk_first, 1)
                            act.wait_ge(qk_split[s % 2], n * (NS // 2) + START)
                            nc.scalar.activation(full[:, s], ps_qk[:, s % 2], ACT.Identity,
                                                 bias=bias_qk[:, s:s + 1]).then_inc(qk_full[s % 2], 1)

            row(0, True, True)
            with act.Fori(1, B - 1) as b:
                row(b, False, True)
            row(B - 1, False, False)
            if not on:
                store_scores(B - 1, 1)

        @blk.vector
        def _(dve):
            chain = Chain(dve, chain_sem)
            if on:
                chain.link(nc.vector.memset(v[:, :, :, :, HD:V1], 1.0))
            else:
                nc.vector.memset(scoreT[:, :], 0.0).then_inc(cleared, 1)
            dve.wait_ge(first_in, 16 * CT + START)
            if eps:
                chain.link(nc.vector.tensor_scalar(inv[:, 0], inv[:, 0], eps, None, ALU.add))
            nc.vector.reciprocal(inv[:, 0], inv[:, 0]).then_inc(first_inv, 1)
            dve.wait_ge(den_in, 16 + START)
            if eps:
                chain.link(nc.vector.tensor_scalar(den[:, :], den[:, :], eps, None, ALU.add))
            nc.vector.reciprocal(den[:, :], den[:, :]).then_inc(den_inv, 1)
            dve.wait_ge(consts_in, 16 * N_CONST + START)

            def sum_up(b, half):
                n = tile(b, half)
                dve.wait_ge(o_ps, n + 1 + START)
                dve.wait_ge(biased, n + 1 + START)
                dve.wait_ge(normed[1 - half], b + half + START)
                for t in range(0, TB, 2):
                    ins = nc.vector.tensor_tensor(z[:, t:t + 2], ps_o[:, half % AHEAD, t:t + 2], xb[:, half, t:t + 2], ALU.add)
                ins.then_inc(summed, 1)
                dve.wait_ge(summed, n + 1 + START)
                layernorm_stats(nc, dve, chain, z, stats, moments, var).then_inc(var_ready, 1)

            def normalise(b, half):
                dve.wait_ge(rooted, tile(b, half) + 1 + START)
                dve.wait_ge(stored[half], b * 16 + START)
                for t in range(TB):
                    ins = nc.vector.tensor_scalar(xn[:, half, t], z[:, t], moments[:, t, 0:1], rstd[:, t:t + 1],
                                                  ALU.subtract, ALU.mult)
                ins.then_inc(normed[half], 1)

            def split(b, half, pair):
                for s in pair:
                    dve.wait_ge(qk_full[s % 2], use(b, half, s) + 1 + START)
                    dve.wait_ge(qk_first, tile(b, half) * NS + s + 1 + START)
                    ins = nc.vector.tensor_tensor(rest[:, s], full[:, s], parts[:, s, 0], ALU.subtract)
                chain.link(ins)
                for s in pair:
                    ins = nc.vector.tensor_copy(parts[:, s, 1], rest[:, s])
                chain.link(ins)
                for s in pair:
                    nc.vector.tensor_tensor(parts[:, s, 2], rest[:, s], parts[:, s, 1],
                                            ALU.subtract).then_inc(qk_split[s % 2], 1)

            def copy_v(b, half):
                dve.wait_ge(v_ps, tile(b, half) + 1 + START)
                dve.wait_ge(v_out[half], b * (16 * TB) + START)
                for t in range(TB):
                    last = nc.vector.tensor_tensor(v[:, half, t, :, 0:HD],
                                                   ps_v[:, t].rearrange("p (h d) -> p h d", d=HD),
                                                   bias_v[:, :].rearrange("p (h d) -> p h d", d=HD), ALU.add)
                last.then_inc(v_full, 1)

            def row(b, more):
                chain.restart()
                for half in range(HALVES):
                    following = (b, 1) if half == 0 else (b + 1, 0) if more else None
                    if following:
                        sum_up(*following)
                    if on:
                        split(b, half, (0, 1))
                    if following:
                        normalise(*following)
                    if on:
                        split(b, half, (2, 3))
                        copy_v(b, half)

            sum_up(0, 0)
            normalise(0, 0)
            with dve.Fori(0, B - 1) as b:
                row(b, True)
            row(B - 1, False)


KEY_BLOCKS = TILE // P


def score_groups():
    groups, unit = [], 0
    for half in range(HALVES):
        groups.append((half, "rest", None, 0, [unit]))
        unit += 1
        groups.append((half, "memory", None, 0, [unit, unit + 1]))
        unit += 2
        for blk in range((half + 1) * KEY_BLOCKS):
            groups.append((half, "causal", blk, max(0, blk - half * KEY_BLOCKS) * P, [unit, unit + 1]))
            unit += 2
    return groups, unit


GROUPS_OF_QUAD, UNITS = score_groups()
DIAGONALS = 2 * BLOCKS
BANK = 512
MAX_PIECES = [(j, t, n, n * BANK, min(MEM + (t + 1) * P, (n + 1) * BANK))
              for t in range(BLOCKS) for j in range(4) for n in range(-(-(MEM + (t + 1) * P) // BANK))]
PIECES = len(MAX_PIECES)
PIECE_SLOTS = 3

MAX_BANKS = 3
START_PIECES = 4
TURN_BANK = START_PIECES % MAX_BANKS


def piece_banks():
    places, used = [], [0] * MAX_BANKS
    for m in range(PIECES):
        bank = (m + (m >= START_PIECES)) % MAX_BANKS
        places.append((bank, used[bank]))
        used[bank] += 1
    return places, used


PIECE_BANK, BANK_USES = piece_banks()
AFTER_TURN = [m for m in range(START_PIECES, PIECES) if PIECE_BANK[m][0] == TURN_BANK][0]


def pieces_between(lead):
    steps = []
    for half, kind, kb, first, units in GROUPS_OF_QUAD:
        steps += [2 * (TILE - first)] * len(units) + [4 * (TILE - first) if kind != "rest" else 2 * TILE]
    reduction = [64 + hi - lo for _, _, _, lo, hi in MAX_PIECES]
    order = [reduction[(lead + i) % PIECES] for i in range(PIECES)]
    through, at, done, total = [], 0, 0, sum(order)
    for n, cost in enumerate(steps):
        at += cost
        while done < PIECES and sum(order[:done + 1]) <= total * at / sum(steps):
            done += 1
        through.append(done)
    through[-1] = PIECES
    return through


LAG = 2
PROB_SLOTS = 2 * (LAG + 1)


def prob_slot(g, u):
    return (g * UNITS + u) % PROB_SLOTS


def softmax_attention(nc, io):
    SLOTS = QUADS
    with Phase(nc, "sa") as ph:
        ident = ph.sb("ident", [P, P])
        eye = ph.sb("eye", [P, P], BF16)
        later_f = ph.sb("later_f", [P, P])
        later = ph.sb("later", [P, P], BF16)
        q = [ph.sb(f"q{i}", [STACK1, 4, T], BF16) for i in range(SLOTS)]
        k = [ph.sb(f"k{i}", [STACK1, 4, T], BF16) for i in range(SLOTS)]
        km = [ph.sb(f"km{i}", [STACK1, 4, MEMW], BF16) for i in range(SLOTS)]
        v = [ph.sb(f"v{i}", [P, BLOCKS, VW]) for i in range(SLOTS)]
        vm = [ph.sb(f"vm{i}", [P, VW + P]) for i in range(SLOTS)]
        prob = ph.sb("prob", [P, PROB_SLOTS, 2, TILE])
        y = ph.sb("y", [P, 2, T])
        piece_max = ph.sb("piece_max", [P, 4, BLOCKS, PIECE_SLOTS])
        neg_max = ph.sb("neg_max", [P, 4 * BLOCKS])
        max_rest = ph.sb("max_rest", [4 * BLOCKS, P])
        max_parts = ph.sb("max_parts", [4 * BLOCKS, 2, PARTS, P], BF16)
        ps_s = ph.ps("ps_s", [P, 2, 2, TILE])
        ps_m = ph.ps("ps_m", [P, MAX_BANKS, BANK])
        ps_y = ph.ps("ps_y", [P, TILE])
        turned = ps_m[0:4 * BLOCKS, TURN_BANK, 0:P]
        consts_in, cleared, chain_sem = ph.sem("consts_in"), ph.sem("cleared"), ph.chain_sem()
        landed, max_in, stored = ph.sems("landed", SLOTS), ph.sems("max_in", SLOTS), ph.sems("stored", 2)
        scored = ph.sem("scored")
        expd = ph.sems("expd", 2)
        masked, summed = ph.sem("masked"), ph.sem("summed")
        turn = ph.sem("turn")
        y_done = ph.sem("y_done")
        piece_ps, piece_done = ph.sem("piece_ps"), ph.sems("piece_done", MAX_BANKS)
        max_done, max_ps, max_split = ph.sem("max_done"), ph.sem("max_ps"), ph.sem("max_split")
        LOADS = 11
        LEAD = 14

        def quad_before(b, g):
            return b * QUADS + g

        def after(b, g, n=1):
            nb, ng = b + (g + n) // QUADS, (g + n) % QUADS
            return None if isinstance(nb, int) and nb >= B else (nb, ng)

        blk = ph.block()

        @blk.sync
        def _(sp):
            ph.start(sp)
            for dst, name in ((ident, "ident"), (later_f, "later")):
                sp.dma_start(dst[:, :], io[name]).then_inc(consts_in, 16)

            def load(b, g):
                load_stack(sp, q[g], io["q_parts"], quad_before(b, g), LEFT, landed[g])
                load_stack(sp, k[g], io["k_parts"], quad_before(b, g), RIGHT, landed[g])
                load_stack(sp, km[g], io["mem_parts"], quad_before(b, g), RIGHT, landed[g])
                sp.dma_start(v[g][:, :, :], io["v"][bass.ds(b * (QUADS * T) + g * T, T)]
                             .rearrange("(n p) w -> p n w", p=P)).then_inc(landed[g], 16)
                sp.dma_start(vm[g][:, :], io["mem"][bass.ds(b * (QUADS * P) + g * P, P)]).then_inc(landed[g], 16)

            def maxima(b, g):
                sp.wait_ge(max_split, quad_before(b, g) + 1 + START)
                for part in range(PARTS):
                    sp.dma_start(q[g][STACK + part:STACK + part + 1].rearrange("a h t -> a (h t)"),
                                 max_parts[:, g % 2, part]).then_inc(max_in[g], 16)

            def batch_row(b, last):
                for g in range(QUADS):
                    if not (last and g == QUADS - 1):
                        maxima(*after(b, g))
                    sp.wait_ge(y_done, (quad_before(b, g) + 1) * HALVES + START)
                    sp.dma_start(io["y"][bass.ds(b * (QUADS * P) + g * P, P)], y[:, g % 2]).then_inc(stored[g % 2], 16)
                    if not last:
                        load(b + 1, g)

            for g in range(QUADS):
                sp.wait_ge(cleared, g + 1 + (g > 0) + START)
                load(0, g)
            maxima(0, 0)
            with sp.Fori(0, B - 1) as b:
                batch_row(b, False)
            batch_row(B - 1, True)
            for pr in range(2):
                sp.wait_ge(stored[pr], NQ // 2 * 16 + START)

        @blk.tensor
        def _(pe):
            pe.wait_ge(consts_in, 32 + START)
            pe.wait_ge(cleared, 2 + START)

            def piece(b, g, m):
                j, t, _, lo, hi = MAX_PIECES[m]
                s, before = PIECE_BANK[m]
                if m == 0:
                    pe.wait_ge(landed[g], b * (16 * LOADS) + 16 * LOADS + START)
                qs = q[g][0:STACK, j, t * P:(t + 1) * P]
                pe.wait_ge(piece_done[s], quad_before(b, g) * BANK_USES[s] + before + START)
                if m == AFTER_TURN:
                    pe.wait_ge(max_split, quad_before(b, g) + START)
                if lo == 0:
                    nc.tensor.matmul(ps_m[:, s, 0:MEM], qs, km[g][0:STACK, j, 0:MEM], start=True, stop=True, skip_group_check=True)
                a = max(lo, MEM)
                last = nc.tensor.matmul(ps_m[:, s, a - lo:hi - lo], qs, k[g][0:STACK, j, a - MEM:hi - MEM],
                                        start=lo > 0, stop=True, skip_group_check=True)
                a, e = max(lo, MEM + t * P), hi
                if a < e:
                    first = MEM + t * P
                    last = nc.tensor.matmul(ps_m[:, s, a - lo:e - lo], eye[:, :], later[:, a - first:e - first],
                                            start=False, stop=True, skip_group_check=True)
                last.then_inc(piece_ps, 1)

            def turn_maxima(b, g):
                pe.wait_ge(max_done, quad_before(b, g) + 1 + START)
                if after(b, g) is not None:
                    pe.wait_ge(piece_done[TURN_BANK], (quad_before(b, g) + 1) * BANK_USES[TURN_BANK]
                               + PIECE_BANK[AFTER_TURN][1] + START)
                nc.tensor.transpose(turned, neg_max[:, :], ident[:, :]).then_inc(max_ps, 1)

            def scores(b, g, group, u):
                half, kind, kb, first, units = group
                s = u % 2
                pe.wait_ge(expd[s], quad_before(b, g) * (UNITS // 2) + u // 2 + START)
                queries = slice(half * TILE + first, (half + 1) * TILE)
                if kind == "rest":
                    for j in range(4):
                        last = nc.tensor.matmul(ps_s[32 * j:32 * j + 32, s, 0], km[g][:, j, P:MEMW], q[g][:, j, queries],
                                                start=True, stop=True)
                else:
                    for jj in range(2):
                        j = 2 * (u - units[0]) + jj
                        keys = km[g][:, j, 0:P] if kind == "memory" else k[g][:, j, kb * P:(kb + 1) * P]
                        last = nc.tensor.matmul(ps_s[:, s, jj, 0:TILE - first], keys, q[g][:, j, queries], start=True, stop=True)
                last.then_inc(scored, 1)

            def sums(b, g, group, n_masked, finish):
                half, kind, kb, first, units = group
                for u in units:
                    pe.wait_ge(expd[u % 2], quad_before(b, g) * (UNITS // 2) + u // 2 + 1 + START)
                if n_masked:
                    pe.wait_ge(masked, quad_before(b, g) * DIAGONALS + n_masked + START)
                if kind == "rest":
                    pe.wait_ge(y_done, quad_before(b, g) * HALVES + half + START)
                    last = nc.tensor.matmul(ps_y[:, :], vm[g][:, VW:VW + P], prob[:, prob_slot(g, units[0]), 0],
                                            start=True, stop=True, skip_group_check=True)
                else:
                    for j in range(4):
                        values = vm[g][:, j * V1:(j + 1) * V1] if kind == "memory" else v[g][:, kb, j * V1:(j + 1) * V1]
                        last = nc.tensor.matmul(ps_y[32 * j:32 * j + V1, first:TILE], values,
                                                prob[:, prob_slot(g, units[j // 2]), j % 2, 0:TILE - first],
                                                start=False, stop=True, skip_group_check=True)
                if finish:
                    last.then_inc(summed, 1)

            def batch_row(b):
                waiting, done = [], LEAD

                def pieces(g, step):
                    nonlocal done
                    until = LEAD + g * PIECES + through[step]
                    while done < until:
                        if done % PIECES == START_PIECES and after(b, 0, done // PIECES) is not None:
                            turn_maxima(*after(b, 0, done // PIECES))
                        if after(b, 0, 1 + done // PIECES) is not None:
                            piece(*after(b, 0, 1 + done // PIECES), done % PIECES)
                        done += 1

                def next_sums(g, step):
                    sums(b, *waiting.pop(0))
                    pieces(g, step)

                for g in range(QUADS):
                    pe.wait_ge(max_in[g], b * (16 * PARTS) + 16 * PARTS + START)
                    step, n_masked = 0, 0
                    for n, group in enumerate(GROUPS_OF_QUAD):
                        for u in group[4]:
                            scores(b, g, group, u)
                            pieces(g, step)
                            step += 1
                        if len(waiting) == LAG:
                            next_sums(g, step)
                        step += 1
                        diagonal = group[1] == "causal" and group[2] >= group[0] * KEY_BLOCKS
                        n_masked += 2 * diagonal
                        end = n + 1 == len(GROUPS_OF_QUAD) or GROUPS_OF_QUAD[n + 1][1] == "rest"
                        waiting.append((g, group, n_masked if diagonal else 0, end))
                while waiting:
                    next_sums(QUADS - 1, step - 1)

            through = pieces_between(LEAD)
            for m in range(PIECES + LEAD):
                if m == PIECES + START_PIECES:
                    turn_maxima(0, 0)
                piece(0, m // PIECES, m % PIECES)
            with pe.Fori(0, B - 1) as b:
                batch_row(b)
            batch_row(B - 1)

        @blk.scalar
        def _(act):
            def copy_half(b, g, half):
                act.wait_ge(summed, quad_before(b, g) * HALVES + half + 1 + START)
                act.wait_ge(stored[g % 2], b * (QUADS // 2 * 16) + g // 2 * 16 + START)
                nc.scalar.activation(y[:, g % 2, half * TILE:(half + 1) * TILE], ps_y[:, :], ACT.Copy).then_inc(y_done, 1)

            with act.Fori(0, B) as b:
                for g in range(QUADS):
                    for half, kind, kb, first, units in GROUPS_OF_QUAD:
                        for u in units:
                            s, slot = u % 2, prob_slot(g, u)
                            act.wait_ge(scored, quad_before(b, g) * UNITS + u + 1 + START)
                            if kind == "rest":
                                src, dst = ps_s[:, s, 0], prob[:, slot, 0]
                            else:
                                src, dst = ps_s[:, s, :, 0:TILE - first], prob[:, slot, :, 0:TILE - first]
                            nc.scalar.activation(dst, src, ACT.Exp, scale=HD ** -0.5).then_inc(expd[s], 1)
                        if kind == "memory" and half == 1:
                            copy_half(b, g, 0)
                        if kind == "memory" and half == 0 and g > 0:
                            copy_half(b, g - 1, 1)
                copy_half(b, QUADS - 1, 1)

        @blk.gpsimd
        def _(pool):
            with pool.Fori(0, B) as b:
                for g in range(QUADS):
                    for half, kind, kb, first, units in GROUPS_OF_QUAD:
                        if kind == "causal" and kb >= half * KEY_BLOCKS:
                            for u in units:
                                pool.wait_ge(expd[u % 2], quad_before(b, g) * (UNITS // 2) + u // 2 + 1 + START)
                                pool.sem_inc(turn, 1)
                                square = prob[:, prob_slot(g, u), :, 0:P]
                                nc.gpsimd.affine_select(out=square, in_=square, compare_op=ALU.is_ge, fill=0.0, base=0,
                                                        pattern=[[0, 2], [1, P]], channel_multiplier=-1).then_inc(masked, 1)

        @blk.vector
        def _(dve):
            chain = Chain(dve, chain_sem)
            chain.link(nc.vector.memset(piece_max[:, :, :, :], -BIG))
            nc.vector.memset(ps_y[:, :], 0.0)
            for i in range(SLOTS):
                chain.link(nc.vector.memset(km[i][STACK:STACK1, :, :], 0.0))
                nc.vector.memset(km[i][STACK:STACK1, :, 0:MEM], 1.0)
                nc.vector.memset(k[i][STACK:STACK1, :, :], 1.0).then_inc(cleared, 1)
                if i == 0:
                    dve.wait_ge(consts_in, 32 + START)
                    nc.vector.tensor_copy(eye[:, :], ident[:, :])
                    nc.vector.tensor_copy(later[:, :], later_f[:, :]).then_inc(cleared, 1)

            FIRST_PIECES = START_PIECES + 1

            def reduce_pieces(b, g, first, end):
                for m in range(first, end):
                    j, t, n, lo, hi = MAX_PIECES[m]
                    dve.wait_ge(piece_ps, quad_before(b, g) * PIECES + m + 1 + START)
                    s = PIECE_BANK[m][0]
                    nc.vector.tensor_reduce(piece_max[:, j, t, n:n + 1], ps_m[:, s, 0:hi - lo], AX.X, ALU.max).then_inc(piece_done[s], 1)

            def quad(b, g):
                reduce_pieces(b, g, FIRST_PIECES, PIECES)
                for s in range(MAX_BANKS):
                    dve.wait_ge(piece_done[s], (quad_before(b, g) + 1) * BANK_USES[s] + START)
                nc.vector.tensor_reduce(neg_max[:, :], piece_max[:, :, :, :].rearrange("p h t n -> p (h t) n"),
                                        AX.X, ALU.max, negate=True).then_inc(max_done, 1)
                if after(b, g) is not None:
                    dve.wait_ge(max_done, quad_before(b, g) + 1 + START)
                    reduce_pieces(*after(b, g), 0, FIRST_PIECES)
                dve.wait_ge(max_ps, quad_before(b, g) + 1 + START)
                if g < 2:
                    dve.wait_ge(max_in[g + 2], b * (16 * PARTS) + START)
                else:
                    dve.wait_ge(max_in[g - 2], b * (16 * PARTS) + 16 * PARTS + START)
                to = max_parts[:, g % 2]
                chain.link(nc.vector.tensor_copy(to[:, 0], turned))
                chain.link(nc.vector.tensor_tensor(max_rest[:, :], turned, to[:, 0], ALU.subtract))
                chain.link(nc.vector.tensor_copy(to[:, 1], max_rest[:, :]))
                nc.vector.tensor_tensor(to[:, 2], max_rest[:, :], to[:, 1], ALU.subtract).then_inc(max_split, 1)

            reduce_pieces(0, 0, 0, FIRST_PIECES)
            with dve.Fori(0, B - 1) as b:
                chain.restart()
                for g in range(QUADS):
                    quad(b, g)
            chain.restart()
            for g in range(QUADS):
                quad(B - 1, g)


EXPERT_W = 2 * C + C


def experts(nc, io):
    NT = B * HALVES
    ALLB = NT * TB
    W_SLOTS = 3
    H_SLOTS = 3
    SUMS = EXPERTS + 1
    UP, DOWN = C, 2 * C
    with Phase(nc, "mo") as ph:
        w = ph.sb("w", [P, W_SLOTS, EXPERT_W])
        w_hi, w_lo = ph.sb("w_hi", [P, ALL_EXPERTS, EXPERT_W], F32R), ph.sb("w_lo", [P, ALL_EXPERTS, EXPERT_W], F32R)
        e_bias = ph.sb("e_bias", [P, ALLB, EXPERTS])
        xT = ph.sb("xT", [P, HALVES, CT, TILE])
        x_hi, x_lo = ph.sb("x_hi", [P, HALVES, CT, TILE], F32R), ph.sb("x_lo", [P, HALVES, CT, TILE], F32R)
        x = ph.sb("x", [P, HALVES, TB, C])
        comb = ph.sb("comb", [P, HALVES, TB, EXPERTS])
        silu = ph.sb("silu", [P, 2, TILE])
        h = ph.sb("h", [P, 2, TILE])
        h_hi, h_lo = ph.sb("h_hi", [P, H_SLOTS, TILE], F32R), ph.sb("h_lo", [P, H_SLOTS, TILE], F32R)
        acc = ph.sb("acc", [P, TB, C])
        stats, moments = ph.sb("stats", [P, TB, 6]), ph.sb("moments", [P, TB, 2])
        var, power, rstd = (ph.sb(n, [P, TB]) for n in ("var", "power", "rstd"))
        score, biased, keep, equal, equal_kept = (ph.sb(n, [P, ALLB, EXPERTS]) for n in ("score", "biased", "keep", "equal", "equal_kept"))
        up_to = [ph.sb(f"up_to{i}", [P, ALLB, EXPERTS]) for i in range(2)]
        largest = ph.sb("largest", [P, ALLB, 8])
        pair_hi, pair_lo = ph.sb("pair_hi", [P, ALLB, GROUPS, 2]), ph.sb("pair_lo", [P, ALLB, GROUPS, 2])
        g1, g2, g3, gsum, grank, gge = (ph.sb(n, [P, ALLB, GROUPS]) for n in ("g1", "g2", "g3", "gsum", "grank", "gge"))
        wsum = ph.sb("wsum", [P, ALLB])
        ps_g, ps_u = ph.ps("ps_g", [P, 2, TILE]), ph.ps("ps_u", [P, 2, TILE])
        ps_o = ph.ps("ps_o", [P, 2, TB, C])
        consts_in, chain_sem, power_set = ph.sem("consts_in"), ph.chain_sem(), ph.sem("power_set")
        w_in, w_hi_done, w_split = ph.sems("w_in", W_SLOTS), ph.sem("w_hi_done"), ph.sem("w_split")
        xT_in, x_hi_done, x_split = ph.sems("xT_in", HALVES), ph.sem("x_hi_done"), ph.sems("x_split", HALVES)
        routed, comb_out = ph.sem("routed"), ph.sem("comb_out")
        landed = ph.sems("landed", HALVES)
        turn = ph.sem("turn")
        g_ps, u_ps, silu_done, multiplied = (ph.sem(n) for n in ("g_ps", "u_ps", "silu_done", "multiplied"))
        h_hi_done, h_split, o_ps, added = (ph.sem(n) for n in ("h_hi_done", "h_split", "o_ps", "added"))
        var_ready, rooted = ph.sem("var_ready"), ph.sem("rooted")
        normed, stored = ph.sems("normed", HALVES), ph.sems("stored", HALVES)
        blk = ph.block()

        def tile(b, half):
            return b * HALVES + half

        HI_ON_ACT = 6
        X1_AT = 6
        X_SPLIT_AT = (0, ALL_EXPERTS - 4)

        ROUTED_AT = 10

        @blk.sync
        def _(sp):
            ph.start(sp)
            def load_xT(b, half):
                sp.dma_start(xT[:, half], io["xT3"][bass.ds(b * C, C), half * TILE:(half + 1) * TILE]
                             .rearrange("(a p) t -> p a t", p=P)).then_inc(xT_in[half], 16)

            def load_rows(b, half):
                rows = bass.ds(b * T + half * TILE, TILE)
                sp.dma_start(x[:, half], io["x3"][rows].rearrange("(n p) c -> p n c", p=P)).then_inc(landed[half], 16)
                sp.dma_start(comb[:, half], io["combine"][rows].rearrange("(n p) e -> p n e", p=P)).then_inc(landed[half], 16)

            sp.dma_start(score[:, :, :], io["score"].rearrange("(n p) e -> p n e", p=P)).then_inc(consts_in, 16)
            load_xT(0, 0)
            for to, name in ((e_bias, "e_bias"), (grank, "grank0")):
                sp.dma_start(to[:, :, :], io[name]).then_inc(consts_in, 16)
            for e in range(ALL_EXPERTS):
                if e == X1_AT:
                    load_xT(0, 1)
                if e == ROUTED_AT:
                    sp.wait_ge(routed, 1 + START)
                    sp.dma_start(io["combine"].rearrange("(n p) e -> p n e", p=P), keep[:, :, :]).then_inc(comb_out, 16)
                    sp.wait_ge(comb_out, 16 + START)
                    for half in range(HALVES):
                        load_rows(0, half)
                if e >= W_SLOTS:
                    sp.wait_ge(w_split, e - W_SLOTS + 1 + START)
                sp.dma_start(w[:, e % W_SLOTS], io["experts"][:, e]).then_inc(w_in[e % W_SLOTS], 16)

            def batch_row(b, more):
                for half in range(HALVES):
                    if more:
                        sp.wait_ge(x_split[half], b + 1 + START)
                        load_xT(b + 1, half)
                    sp.wait_ge(normed[half], b + 1 + START)
                    sp.dma_start(io["out"][bass.ds(b * T + half * TILE, TILE)].rearrange("(n p) c -> p n c", p=P),
                                 x[:, half]).then_inc(stored[half], 16)
                    if more:
                        sp.wait_ge(stored[half], b * 16 + 16 + START)
                        load_rows(b + 1, half)

            with sp.Fori(0, B - 1) as b:
                batch_row(b, True)
            batch_row(B - 1, False)
            for half in range(HALVES):
                sp.wait_ge(stored[half], 16 * B + START)

        @blk.tensor
        def _(pe):
            def gate_up(b, half, e):
                n, s = tile(b, half), e % 2
                if e == 0:
                    pe.wait_ge(x_split[half], b + 1 + START)
                pe.wait_ge(w_split, e + 1 + START)
                if not (isinstance(n, int) and n * ALL_EXPERTS + e < 2):
                    pe.wait_ge(multiplied, n * ALL_EXPERTS + e - 1 + START)
                for first, ps, ready in ((0, ps_g, g_ps), (UP, ps_u, u_ps)):
                    for a in range(CT):
                        cols = slice(first + a * INNER, first + (a + 1) * INNER)
                        last = three_passes(nc, ps[:, s], (w_hi[:, e, cols], w_lo[:, e, cols]), (x_hi[:, half, a], x_lo[:, half, a]),
                                            start=a == 0, stop=a == CT - 1)
                    last.then_inc(ready, 1)

            def project_down(b, half, es, i):
                n, s = tile(b, half), i % 2
                pe.wait_ge(h_split, n * ALL_EXPERTS + es[-1] + 1 + START)
                pe.wait_ge(added, n * SUMS + max(0, i - 1) + START)
                for t in range(TB):
                    for e in es:
                        tokens = slice(t * P, (t + 1) * P)
                        last = three_passes(nc, ps_o[:, s, t], (h_hi[:, e % H_SLOTS, tokens], h_lo[:, e % H_SLOTS, tokens]),
                                            (w_hi[:, e, DOWN:EXPERT_W], w_lo[:, e, DOWN:EXPERT_W]),
                                            start=e == es[0], stop=e == es[-1])
                last.then_inc(o_ps, 1)

            def experts_of(b, half, following):
                gate_up(b, half, SHARED)
                project_down(b, half, range(SHARED), 0)
                gate_up(b, half, SHARED + 1)
                for e in range(SHARED, ALL_EXPERTS):
                    if e + 2 < ALL_EXPERTS:
                        gate_up(b, half, e + 2)
                    elif following:
                        gate_up(*following, e + 2 - ALL_EXPERTS)
                    project_down(b, half, (e,), e - 1)

            gate_up(0, 0, 0)
            gate_up(0, 0, 1)
            with pe.Fori(0, B - 1) as b:
                experts_of(b, 0, (b, 1))
                experts_of(b, 1, (b + 1, 0))
            experts_of(B - 1, 0, (B - 1, 1))
            experts_of(B - 1, 1, None)

        @blk.scalar
        def _(act):
            act.wait_ge(xT_in[0], 16 + START)
            nc.scalar.activation(x_hi[:, 0], xT[:, 0], ACT.Copy).then_inc(x_hi_done, 1)
            for e in range(HI_ON_ACT):
                act.wait_ge(w_in[e % W_SLOTS], 16 * (e // W_SLOTS + 1) + START)
                nc.scalar.activation(w_hi[:, e], w[:, e % W_SLOTS], ACT.Copy).then_inc(w_hi_done, 1)
            with act.Fori(0, B) as b:
                for half in range(HALVES):
                    for e in range(ALL_EXPERTS):
                        count = tile(b, half) * ALL_EXPERTS + e + 1 + START
                        act.wait_ge(g_ps, count)
                        nc.scalar.activation(silu[:, e % 2], ps_g[:, e % 2], ACT.Silu).then_inc(silu_done, 1)
                        act.wait_ge(multiplied, count)
                        nc.scalar.activation(h_hi[:, e % H_SLOTS], h[:, e % 2], ACT.Copy).then_inc(h_hi_done, 1)

        @blk.gpsimd
        def _(pool):
            nc.gpsimd.memset(power[:, :], -0.5).then_inc(power_set, 1)

            def split_x(n, half):
                if not (isinstance(n, int) and n == 0):
                    nc.gpsimd.tensor_copy(x_hi[:, half], xT[:, half]).then_inc(x_hi_done, 1)
                pool.wait_ge(x_hi_done, n + 1 + START)
                pool.sem_inc(turn, 1)
                nc.gpsimd.tensor_tensor(x_lo[:, half], xT[:, half], x_hi[:, half].bitcast(F32), ALU.subtract).then_inc(x_split[half], 1)

            def root(n):
                pool.wait_ge(var_ready, n + 1 + START)
                pool.sem_inc(turn, 1)
                nc.gpsimd.tensor_tensor(rstd[:, :], var[:, :], power[:, :], ALU.pow).then_inc(rooted, 1)

            for e in range(ALL_EXPERTS):
                if e in X_SPLIT_AT:
                    half = X_SPLIT_AT.index(e)
                    pool.wait_ge(xT_in[half], 16 + START)
                    split_x(tile(0, half), half)
                pool.wait_ge(w_in[e % W_SLOTS], 16 * (e // W_SLOTS + 1) + START)
                if e >= HI_ON_ACT:
                    nc.gpsimd.tensor_copy(w_hi[:, e], w[:, e % W_SLOTS]).then_inc(w_hi_done, 1)
                pool.wait_ge(w_hi_done, e + 1 + START)
                nc.gpsimd.tensor_tensor(w_lo[:, e], w[:, e % W_SLOTS], w_hi[:, e].bitcast(F32), ALU.subtract).then_inc(w_split, 1)
            pool.wait_ge(power_set, 1 + START)
            with pool.Fori(0, B - 1) as b:
                for half in range(HALVES):
                    root(tile(b, half))
                    pool.wait_ge(xT_in[half], b * 16 + 32 + START)
                    pool.sem_inc(turn, 1)
                    split_x(tile(b + 1, half), half)
            for half in range(HALVES):
                root(tile(B - 1, half))

        @blk.vector
        def _(dve):
            chain = Chain(dve, chain_sem)
            tt, ts = nc.vector.tensor_tensor, nc.vector.tensor_scalar
            link = chain.link
            dve.wait_ge(consts_in, 48 + START)
            link(tt(biased[:, :, :], score[:, :, :], e_bias[:, :, :], ALU.add))
            four = biased[:, :, :].rearrange("p n (g a b) -> p n g a b", g=GROUPS, a=2)
            tt(pair_hi[:, :, :, :], four[:, :, :, :, 0], four[:, :, :, :, 1], ALU.max)
            link(tt(pair_lo[:, :, :, :], four[:, :, :, :, 0], four[:, :, :, :, 1], ALU.min))
            tt(g1[:, :, :], pair_hi[:, :, :, 0], pair_hi[:, :, :, 1], ALU.max)
            tt(g2[:, :, :], pair_hi[:, :, :, 0], pair_hi[:, :, :, 1], ALU.min)
            link(tt(g3[:, :, :], pair_lo[:, :, :, 0], pair_lo[:, :, :, 1], ALU.max))
            link(tt(g2[:, :, :], g2[:, :, :], g3[:, :, :], ALU.max))
            link(tt(gsum[:, :, :], g1[:, :, :], g2[:, :, :], ALU.add))

            def ranks(values, out, ahead, width):
                for d in range(1, width):
                    w = width - d
                    link(tt(ahead[:, :, 0:w], values[:, :, 0:w], values[:, :, d:width], ALU.is_ge))
                    link(tt(out[:, :, d:width], out[:, :, d:width], ahead[:, :, 0:w], ALU.add))
                    link(tt(out[:, :, 0:w], out[:, :, 0:w], ahead[:, :, 0:w], ALU.subtract))

            ranks(gsum, grank, gge, GROUPS)
            link(ts(gge[:, :, :], grank[:, :, :], float(TOP_GROUPS), None, ALU.is_lt))
            per = EXPERTS // GROUPS
            for i in range(per):
                last = tt(biased[:, :, i::per], biased[:, :, i::per], gge[:, :, :], ALU.mult)
            link(last)
            for i in range(ALLB):
                last = nc.vector.max(largest[:, i], biased[:, i])
            link(last)
            least = largest[:, :, TOPK - 1:TOPK].broadcast_to([P, ALLB, EXPERTS])
            link(tt(keep[:, :, :], biased[:, :, :], least, ALU.is_gt))
            link(tt(equal[:, :, :], biased[:, :, :], least, ALU.is_equal))
            link(nc.vector.tensor_reduce(wsum[:, :], keep[:, :, :], AX.X, ALU.add))
            link(ts(wsum[:, :], wsum[:, :], -1.0, float(TOPK), ALU.mult, ALU.add))
            counts = (equal, up_to[0], up_to[1], up_to[0], up_to[1])
            for i, (source, target) in enumerate(zip(counts, counts[1:])):
                d = 2 ** i
                nc.vector.tensor_copy(target[:, :, 0:d], source[:, :, 0:d])
                link(tt(target[:, :, d:], source[:, :, d:], source[:, :, 0:EXPERTS - d], ALU.add))
            link(tt(equal_kept[:, :, :], target[:, :, :], wsum[:, :].unsqueeze(2).broadcast_to([P, ALLB, EXPERTS]), ALU.is_le))
            link(tt(equal[:, :, :], equal[:, :, :], equal_kept[:, :, :], ALU.mult))
            link(tt(keep[:, :, :], keep[:, :, :], equal[:, :, :], ALU.add))
            link(tt(keep[:, :, :], keep[:, :, :], score[:, :, :], ALU.mult))
            link(nc.vector.tensor_reduce(wsum[:, :], keep[:, :, :], AX.X, ALU.add))
            link(ts(wsum[:, :], wsum[:, :], 1e-20, None, ALU.add))
            link(nc.vector.reciprocal(wsum[:, :], wsum[:, :]))
            link(ts(wsum[:, :], wsum[:, :], ROUTE_SCALE, None, ALU.mult))
            tt(keep[:, :, :], keep[:, :, :], wsum[:, :].unsqueeze(2).broadcast_to([P, ALLB, EXPERTS]), ALU.mult).then_inc(routed, 1)

            def multiply(b, half, e):
                count = tile(b, half) * ALL_EXPERTS + e + 1 + START
                dve.wait_ge(silu_done, count)
                dve.wait_ge(u_ps, count)
                tt(h[:, e % 2], silu[:, e % 2], ps_u[:, e % 2], ALU.mult).then_inc(multiplied, 1)

            def rest(b, half, e):
                dve.wait_ge(h_hi_done, tile(b, half) * ALL_EXPERTS + e + 1 + START)
                tt(h_lo[:, e % H_SLOTS], h[:, e % 2], h_hi[:, e % H_SLOTS].bitcast(F32), ALU.subtract).then_inc(h_split, 1)

            def add_up(b, half, i):
                n = tile(b, half)
                dve.wait_ge(o_ps, n * SUMS + i + 1 + START)
                if i == 0:
                    dve.wait_ge(landed[half], b * 32 + 32 + START)
                    dve.wait_ge(normed[1 - half], b + half + START)
                    for t in range(0, TB, 2):
                        last = tt(acc[:, t:t + 2], ps_o[:, i % 2, t:t + 2], x[:, half, t:t + 2], ALU.add)
                else:
                    dve.wait_ge(added, n * SUMS + i + START)
                    for t in range(TB):
                        last = nc.vector.scalar_tensor_tensor(acc[:, t], ps_o[:, i % 2, t], comb[:, half, t, i - 1:i],
                                                              acc[:, t], ALU.mult, ALU.add)
                last.then_inc(added, 1)

            def experts_of(b, half, following):
                n = tile(b, half)
                for e in range(3, ALL_EXPERTS + 2):
                    here = (b, half, e) if e < ALL_EXPERTS else following and (*following, e - ALL_EXPERTS)
                    if here:
                        multiply(*here)
                    add_up(b, half, e - 3)
                    if here:
                        rest(*here)
                dve.wait_ge(added, (n + 1) * SUMS + START)
                layernorm_stats(nc, dve, chain, acc, stats, moments, var).then_inc(var_ready, 1)
                if following:
                    multiply(*following, 2)
                dve.wait_ge(rooted, n + 1 + START)
                for t in range(TB):
                    last = ts(x[:, half, t], acc[:, t], moments[:, t, 0:1], rstd[:, t:t + 1], ALU.subtract, ALU.mult)
                last.then_inc(normed[half], 1)
                if following:
                    rest(*following, 2)

            for e in range(3):
                multiply(0, 0, e)
                rest(0, 0, e)
            with dve.Fori(0, B - 1) as b:
                chain.restart()
                experts_of(b, 0, (b, 1))
                experts_of(b, 1, (b + 1, 0))
            chain.restart()
            experts_of(B - 1, 0, (B - 1, 1))
            experts_of(B - 1, 1, None)


SCRATCH = {
    "omega_parts": ((PARTS, HD, FEAT), BF16), "mem_parts": ((PARTS, B * C, MEMW), BF16),
    "q_parts": ((PARTS, B * C, T), BF16), "k_parts": ((PARTS, B * C, T), BF16), "norms": ((PARTS, B * HEADS * 2, T), BF16),
    "v": ((NQ * T, VW), F32), "y": ((NQ * P, T), F32), "inv": ((B * HEADS, T), F32),
    "score": ((B * T, EXPERTS), F32), "combine": ((B * T, EXPERTS), F32), "x2": ((B * T, C), F32), "x3": ((B * T, C), F32), "xT2": ((B * C, T), F32), "xT3": ((B * C, T), F32),
}


def decoder_layer(nc, io, phases=("p1", "a1", "c1", "a2", "c2", "moe")):
    for name, (shape, dt) in SCRATCH.items():
        if name not in io:
            io[name] = nc.dram_tensor(f"s_{name}", shape, dt).ap()
    if "p1" in phases:
        project(nc, io)
    if "a1" in phases:
        linear_attention(nc, io)
    if "c1" in phases:
        close_attention(nc, io, 1)
    if "a2" in phases:
        softmax_attention(nc, io)
    if "c2" in phases:
        close_attention(nc, io, 2)
    if "moe" in phases:
        experts(nc, io)


def lay_out(x, ctx_1024, L0_attn_W_attn, L0_attn_b_attn, L0_attn_W_proj, L0_attn_b_proj, L0_attn_omega,
            L0_xattn_W_attn, L0_xattn_b_attn, L0_xattn_W_proj, L0_xattn_b_proj, L0_ffn_router_weight,
            L0_ffn_e_bias, L0_ffn_gate_w, L0_ffn_up_w, L0_ffn_down_w, L0_ffn_sh_gate_w, L0_ffn_sh_up_w,
            L0_ffn_sh_down_w):
    import numpy as np

    def rows(v, n):
        return np.ascontiguousarray(np.broadcast_to(np.asarray(v)[None], (n, *np.asarray(v).shape)))

    a = {}
    x = np.asarray(x)
    a["x1"] = x.reshape(B * T, C)
    a["xT1"] = x.transpose(0, 2, 1).reshape(B * C, T)
    ctx = np.asarray(ctx_1024)
    order = np.arange(C).reshape(QUADS, 4, HD).transpose(0, 2, 1).reshape(C)
    memT = np.zeros((B, C, MEMW), np.float32)
    memT[:, :, 0:MEM] = ctx.transpose(0, 2, 1)[:, order]
    a["memT"] = memT.reshape(B * C, MEMW)
    heads = ctx.reshape(B, MEM, QUADS, 4, HD).transpose(0, 2, 1, 3, 4).reshape(NQ, MEM, 4, HD)
    mem = np.zeros((NQ, P, VW + P), np.float32)
    first = mem[:, :, 0:VW].reshape(NQ, P, 4, V1)
    first[..., 0:HD], first[..., HD] = heads[:, 0:P], 1
    mem[:, :, 0:VW] = first.reshape(NQ, P, VW)
    for j in range(4):
        mem[:, 32 * j:32 * j + MEMR, VW + 32 * j:VW + 32 * j + HD] = heads[:, P:, j]
        mem[:, 32 * j:32 * j + MEMR, VW + 32 * j + HD] = 1
    a["mem"] = mem.reshape(NQ * P, VW + P)
    a["omega"] = np.asarray(L0_attn_omega)
    for n, (w, b, wo, bo) in enumerate(((L0_attn_W_attn, L0_attn_b_attn, L0_attn_W_proj, L0_attn_b_proj),
                                        (L0_xattn_W_attn, L0_xattn_b_attn, L0_xattn_W_proj, L0_xattn_b_proj)), 1):
        columns = np.concatenate([order, C + order, 2 * C + np.arange(C)])
        a[f"w{n}"] = np.asarray(w)[:, columns]
        a[f"bT{n}"] = np.asarray(b)[columns].reshape(6, P).T
        a[f"bv{n}"] = rows(np.asarray(b)[2 * C:], P)
        a[f"wo{n}"] = np.asarray(wo)
        a[f"bo{n}"] = rows(rows(bo, TB), P)
    a["router"] = np.zeros((C, 32), np.float32)
    a["router"][:, 0:EXPERTS] = np.asarray(L0_ffn_router_weight).T
    a["e_bias"] = rows(rows(L0_ffn_e_bias, B * BLOCKS), P)
    a["grank0"] = rows(rows(np.arange(GROUPS - 1, -1, -1, dtype=np.float32), B * BLOCKS), P)
    columns = []
    for routed, shared in ((L0_ffn_gate_w, L0_ffn_sh_gate_w), (L0_ffn_up_w, L0_ffn_sh_up_w)):
        both = np.concatenate([np.asarray(shared).reshape(SHARED, INNER, C), np.asarray(routed)])
        columns.append(both.reshape(ALL_EXPERTS, INNER, CT, P).transpose(3, 0, 2, 1).reshape(P, ALL_EXPERTS, CT * INNER))
    down = np.concatenate([np.asarray(L0_ffn_sh_down_w).reshape(C, SHARED, INNER).transpose(1, 0, 2), np.asarray(L0_ffn_down_w)])
    a["experts"] = np.concatenate([*columns, down.transpose(2, 0, 1)], axis=2)
    eye = np.eye(P, dtype=np.float32)
    a["ident"] = eye
    a["cap"] = rows(np.where(np.arange(P)[:, None] <= np.arange(P)[None], np.finfo(np.float32).max, np.float32(0)), 4).transpose(1, 0, 2)
    sel = np.zeros((P, 2 * CT, 32), np.float32)
    for s in range(2 * CT):
        for p in range(P):
            head = (s % CT) * (P // HD) + p // QUAD_ROWS * 4 + p % 4
            sel[p, s, 2 * head + s // CT] = -0.5 / HD
    a["select"] = sel
    a["later"] = np.where(np.arange(P)[None] <= np.arange(P)[:, None], np.float32(0), np.float32(-1.0e30))
    return {k: np.ascontiguousarray(v) for k, v in a.items()}


def kernel(**inputs):
    import numpy as np
    import concourse.bacc as bacc
    from concourse.bass_utils import run_bass_kernel_spmd

    arrays = lay_out(**inputs)
    nc = bacc.Bacc("TRN2", target_bir_lowering=False, num_devices=1)
    io = {n: nc.dram_tensor(n, a.shape, mybir.dt.from_np(a.dtype), kind="ExternalInput").ap() for n, a in arrays.items()}
    io["out"] = nc.dram_tensor("out", (B * T, C), F32, kind="ExternalOutput").ap()
    decoder_layer(nc, io)
    r = run_bass_kernel_spmd(nc, [arrays], core_ids=[0])
    return r.results[0]["out"].reshape(B, T, C)
```
